# Optimizing a Trainium2 kernel written in Bass

```python
import numpy as np
import jax
import jax.numpy as jnp

def _softmax(x, axis=-1):
    return jax.nn.softmax(x, axis=axis)

def _gelu(x):
    return jax.nn.gelu(x, approximate=True)

def _silu(x):
    return jax.nn.silu(x)

def _sigmoid(x):
    return jax.nn.sigmoid(x)

def _layernorm(x, axis=-1, eps=1e-05):
    m = jnp.mean(x, axis=axis, keepdims=True)
    v = jnp.var(x, axis=axis, keepdims=True)
    return (x - m) / jnp.sqrt(v + eps)

def _scatter_add(tgt, idx, src, axis=0):
    return tgt.at[idx].add(src)

def _segment_sum(src, seg, n):
    return jax.ops.segment_sum(src, seg, n)
kernel_name = 'mk_metaformer_d4_conv_nhwc256_r2_53a775'

def setup_inputs(seed: int=0):
    np.random.seed(seed)
    _w = jnp.asarray

    def _rec_inputs():
        import jax
        import jax.numpy as jnp
        _gk = jax.random.key(seed)
        x = 7.22e-05 + 1 * jax.random.normal(jax.random.fold_in(_gk, 1), (8, 32, 32, 128), jnp.float32)
        return x
    x = _rec_inputs()

    def _L0_conv_setup():
        import jax, jax.numpy as jnp
        import numpy as np
        B, H, W, C = (8, 32, 32, 128)
        G, K = (8, 3)
        GC = C // G
        K2 = K * K
        KD = 3
        OFFSET_SCALE = 1.0
        PAD = (K - 1) // 2
        EPS = 1e-06

        def _bilinear_gather(xg, px, py, Hp, Wp):
            x0 = jnp.floor(px)
            y0 = jnp.floor(py)
            wx1 = px - x0
            wy1 = py - y0
            x0i = x0.astype(jnp.int32)
            y0i = y0.astype(jnp.int32)

            def corner(xi, yi, wgt):
                valid = (xi >= 0) & (xi < Wp) & (yi >= 0) & (yi < Hp)
                idx = jnp.clip(yi, 0, Hp - 1) * Wp + jnp.clip(xi, 0, Wp - 1)
                v = jnp.take_along_axis(xg, idx[..., None], axis=2)
                return v * (wgt * valid)[..., None]
            return corner(x0i, y0i, (1 - wx1) * (1 - wy1)) + corner(x0i + 1, y0i, wx1 * (1 - wy1)) + corner(x0i, y0i + 1, (1 - wx1) * wy1) + corner(x0i + 1, y0i + 1, wx1 * wy1)
        key = jax.random.key(seed)
        ks = jax.random.split(key, 8)

        def r(k, shp, s):
            return jax.random.normal(k, shp, jnp.float32) * s
        return {'inputs': jax.random.normal(ks[0], (B, H, W, C), jnp.float32), 'w_in': r(ks[1], (C, C), 0.02), 'b_in': jnp.zeros((C,), jnp.float32), 'dw_kernel': r(ks[2], (KD, KD, 1, C), 0.1), 'dw_bias': jnp.zeros((C,), jnp.float32), 'ln_gamma': jnp.ones((C,), jnp.float32), 'ln_beta': jnp.zeros((C,), jnp.float32), 'w_off': r(ks[3], (C, 2 * G * K2), 0.01), 'b_off': jnp.zeros((2 * G * K2,), jnp.float32), 'w_mask': r(ks[4], (C, G * K2), 0.01), 'b_mask': jnp.zeros((G * K2,), jnp.float32), 'w_out': r(ks[5], (C, C), 0.02), 'b_out': jnp.zeros((C,), jnp.float32)}
    _L0_conv_all = _L0_conv_setup()
    _L0_conv_in = {k: v for k, v in _L0_conv_all.items() if k in ('w_in', 'b_in', 'dw_kernel', 'dw_bias', 'ln_gamma', 'ln_beta', 'w_off', 'b_off', 'w_mask', 'b_mask', 'w_out', 'b_out')}
    del _L0_conv_all

    def _L0_ffn_setup():
        import jax, jax.numpy as jnp
        import numpy as np
        from jax import lax
        key = jax.random.key(seed)
        B, T, I, H = (32, 1024, 128, 128)
        ks = jax.random.split(key, 13)
        s = 1.0 / np.sqrt(H)

        def w(k, shape):
            return jax.random.uniform(k, shape, jnp.float32, -s, s)
        return {'x': jax.random.normal(ks[0], (B, T, I), jnp.float32), 'U_i': w(ks[1], (I, H)), 'V_i': w(ks[2], (H, H)), 'b_i': w(ks[3], (H,)), 'U_f': w(ks[4], (I, H)), 'V_f': w(ks[5], (H, H)), 'b_f': w(ks[6], (H,)), 'U_c': w(ks[7], (I, H)), 'V_c': w(ks[8], (H, H)), 'b_c': w(ks[9], (H,)), 'U_o': w(ks[10], (I, H)), 'V_o': w(ks[11], (H, H)), 'b_o': w(ks[12], (H,))}
    _L0_ffn_all = _L0_ffn_setup()
    _L0_ffn_in = {k: v for k, v in _L0_ffn_all.items() if k in ('U_i', 'V_i', 'b_i', 'U_f', 'V_f', 'b_f', 'U_c', 'V_c', 'b_c', 'U_o', 'V_o', 'b_o')}
    del _L0_ffn_all

    def _L1_conv_setup():
        import jax, jax.numpy as jnp
        import numpy as np
        BETA_MIN = 1e-06
        key = jax.random.key(seed)
        ks = jax.random.split(key, 4)
        B, H, W, C = (32, 56, 56, 128)
        x = jax.random.normal(ks[0], (B, H, W, C), dtype=jnp.float32)
        gamma_k = jax.random.uniform(ks[1], (1, 1, 8, C), dtype=jnp.float32) * (1.0 / 16.0)
        gamma_s = jax.random.uniform(ks[2], (3, 3, C, 1), dtype=jnp.float32) * (1.0 / 16.0)
        beta = jax.random.uniform(ks[3], (C,), dtype=jnp.float32) * 1e-06
        beta_outside = jnp.zeros((C,), dtype=jnp.float32)
        gamma_outside = jnp.ones((C,), dtype=jnp.float32)
        return {'x': x, 'gamma_k': gamma_k, 'gamma_s': gamma_s, 'beta': beta, 'beta_outside': beta_outside, 'gamma_outside': gamma_outside, 'surround_dist': 1}
    _L1_conv_all = _L1_conv_setup()
    _L1_conv_in = {k: v for k, v in _L1_conv_all.items() if k in ('gamma_k', 'gamma_s', 'beta', 'beta_outside', 'gamma_outside')}
    del _L1_conv_all

    def _L1_ffn_setup():
        import jax, jax.numpy as jnp
        import numpy as np
        B, S, D = (8, 2048, 128)
        H = 4 * D
        CAPACITY = 0.5
        key = jax.random.key(seed)
        ks = jax.random.split(key, 6)
        x = jax.random.normal(ks[0], (B, S, D), dtype=jnp.float32)
        attention_mask = jnp.zeros((B, 1, 1, S), dtype=jnp.float32)
        wr = jax.random.normal(ks[1], (D, 1), dtype=jnp.float32) * 0.02
        br = jnp.zeros((1,), dtype=jnp.float32)
        w1 = jax.random.normal(ks[2], (D, H), dtype=jnp.float32) * 0.02
        b1 = jnp.zeros((H,), dtype=jnp.float32)
        w2 = jax.random.normal(ks[3], (H, D), dtype=jnp.float32) * 0.02
        b2 = jnp.zeros((D,), dtype=jnp.float32)
        return {'x': x, 'attention_mask': attention_mask, 'wr': wr, 'br': br, 'w1': w1, 'b1': b1, 'w2': w2, 'b2': b2}
    _L1_ffn_all = _L1_ffn_setup()
    _L1_ffn_in = {k: v for k, v in _L1_ffn_all.items() if k in ('attention_mask', 'wr', 'br', 'w1', 'b1', 'w2', 'b2')}
    del _L1_ffn_all

    def _L2_conv_setup():
        import jax, jax.numpy as jnp
        import numpy as np
        E = 2
        EPS = 1e-05

        def _linear_scan(inp, lam):

            def comb(l, r):
                al, bl = l
                ar, br = r
                return (ar * al, ar * bl + br)
            _, h = jax.lax.associative_scan(comb, (lam, inp), axis=0)
            return h

        def _bidir_scan(inp, lam):
            fwd = _linear_scan(inp, lam)
            rev = jnp.flip(_linear_scan(jnp.flip(inp, 0), jnp.flip(lam, 0)), 0)
            return fwd + rev
        key = jax.random.key(seed)
        ks = jax.random.split(key, 7)
        H, W, B, D = (32, 32, 8, 128)
        s = 0.02
        return {'x': jax.random.normal(ks[0], (H, W, B, D), dtype=jnp.float32), 'in_w': jax.random.normal(ks[1], (D, 3 * D), dtype=jnp.float32) * s, 'in_b': jnp.zeros((3 * D,), dtype=jnp.float32), 'out_w': jax.random.normal(ks[2], (D, D), dtype=jnp.float32) * s, 'out_b': jnp.zeros((D,), dtype=jnp.float32), 'gamma': jnp.ones((D,), dtype=jnp.float32), 'beta': jnp.zeros((D,), dtype=jnp.float32)}
    _L2_conv_all = _L2_conv_setup()
    _L2_conv_in = {k: v for k, v in _L2_conv_all.items() if k in ('in_w', 'in_b', 'out_w', 'out_b', 'gamma', 'beta')}
    del _L2_conv_all

    def _L2_ffn_setup():
        import jax, jax.numpy as jnp
        import numpy as np
        D_MODEL = 128
        N_EXPERTS = 16
        HIDDEN = 256
        SCALE = 0.02
        key = jax.random.key(seed)
        ks = jax.random.split(key, 5)
        x = jax.random.normal(ks[0], (4, 4096, D_MODEL), dtype=jnp.float32)
        gate_w = jax.random.normal(ks[1], (D_MODEL, N_EXPERTS), dtype=jnp.float32) * SCALE
        gate_b = jnp.zeros((N_EXPERTS,), dtype=jnp.float32)
        w1 = jax.random.normal(ks[2], (N_EXPERTS, D_MODEL, HIDDEN), dtype=jnp.float32) * SCALE
        w2 = jax.random.normal(ks[3], (N_EXPERTS, D_MODEL, HIDDEN), dtype=jnp.float32) * SCALE
        w3 = jax.random.normal(ks[4], (N_EXPERTS, HIDDEN, D_MODEL), dtype=jnp.float32) * SCALE
        return {'x': x, 'gate_w': gate_w, 'gate_b': gate_b, 'w1': w1, 'w2': w2, 'w3': w3}
    _L2_ffn_all = _L2_ffn_setup()
    _L2_ffn_in = {k: v for k, v in _L2_ffn_all.items() if k in ('gate_w', 'gate_b', 'w1', 'w2', 'w3')}
    del _L2_ffn_all

    def _L3_conv_setup():
        import jax, jax.numpy as jnp
        import numpy as np
        K_SIZE = 3
        CH_IN = 128
        NFILT = 128

        def _magnitude_aware_weight(w):
            scale = jax.lax.stop_gradient(jnp.mean(jnp.abs(w), axis=(0, 1, 2), keepdims=True))
            bw_no_grad = scale * jnp.sign(w)
            clipped = jnp.clip(w, -1.0, 1.0)
            return jax.lax.stop_gradient(bw_no_grad) - jax.lax.stop_gradient(clipped) + clipped
        key = jax.random.key(seed)
        k1, k2 = jax.random.split(key)
        x = jax.random.normal(k1, (32, 56, 56, CH_IN), dtype=jnp.float32)
        stdv = 1.0 / np.sqrt(K_SIZE * K_SIZE * CH_IN)
        w = jax.random.normal(k2, (K_SIZE, K_SIZE, CH_IN, NFILT), dtype=jnp.float32) * stdv
        pruning_mask = jnp.ones((K_SIZE * K_SIZE * CH_IN, NFILT), dtype=jnp.float32)
        return {'x': x, 'w': w, 'pruning_mask': pruning_mask}
    _L3_conv_all = _L3_conv_setup()
    _L3_conv_in = {k: v for k, v in _L3_conv_all.items() if k in ('w', 'pruning_mask')}
    del _L3_conv_all

    def _L3_ffn_setup():
        import jax, jax.numpy as jnp
        import numpy as np
        TOP_K = 2
        LN_EPS = 1e-05
        key = jax.random.key(seed)
        ks = jax.random.split(key, 8)
        B, S, D, E, H = (16, 512, 128, 8, 512)
        x = jax.random.normal(ks[0], (B, S, D), dtype=jnp.float32)
        Wr = jax.random.normal(ks[1], (D, E), dtype=jnp.float32) * 0.1
        br = jnp.zeros((E,), dtype=jnp.float32)
        ln_g = jnp.ones((E, D), dtype=jnp.float32)
        ln_b = jnp.zeros((E, D), dtype=jnp.float32)
        W1 = jax.random.normal(ks[2], (E, D, H), dtype=jnp.float32) * (1.0 / np.sqrt(D))
        b1 = jnp.zeros((E, H), dtype=jnp.float32)
        W2 = jax.random.normal(ks[3], (E, H, D), dtype=jnp.float32) * (1.0 / np.sqrt(H))
        b2 = jnp.zeros((E, D), dtype=jnp.float32)
        return {'x': x, 'Wr': Wr, 'br': br, 'ln_g': ln_g, 'ln_b': ln_b, 'W1': W1, 'b1': b1, 'W2': W2, 'b2': b2}
    _L3_ffn_all = _L3_ffn_setup()
    _L3_ffn_in = {k: v for k, v in _L3_ffn_all.items() if k in ('Wr', 'br', 'ln_g', 'ln_b', 'W1', 'b1', 'W2', 'b2')}
    del _L3_ffn_all
    return {'x': x, 'L0_conv_w_in': _L0_conv_in['w_in'], 'L0_conv_b_in': _L0_conv_in['b_in'], 'L0_conv_dw_kernel': _L0_conv_in['dw_kernel'], 'L0_conv_dw_bias': _L0_conv_in['dw_bias'], 'L0_conv_ln_gamma': _L0_conv_in['ln_gamma'], 'L0_conv_ln_beta': _L0_conv_in['ln_beta'], 'L0_conv_w_off': _L0_conv_in['w_off'], 'L0_conv_b_off': _L0_conv_in['b_off'], 'L0_conv_w_mask': _L0_conv_in['w_mask'], 'L0_conv_b_mask': _L0_conv_in['b_mask'], 'L0_conv_w_out': _L0_conv_in['w_out'], 'L0_conv_b_out': _L0_conv_in['b_out'], 'L0_ffn_U_i': _L0_ffn_in['U_i'], 'L0_ffn_V_i': _L0_ffn_in['V_i'], 'L0_ffn_b_i': _L0_ffn_in['b_i'], 'L0_ffn_U_f': _L0_ffn_in['U_f'], 'L0_ffn_V_f': _L0_ffn_in['V_f'], 'L0_ffn_b_f': _L0_ffn_in['b_f'], 'L0_ffn_U_c': _L0_ffn_in['U_c'], 'L0_ffn_V_c': _L0_ffn_in['V_c'], 'L0_ffn_b_c': _L0_ffn_in['b_c'], 'L0_ffn_U_o': _L0_ffn_in['U_o'], 'L0_ffn_V_o': _L0_ffn_in['V_o'], 'L0_ffn_b_o': _L0_ffn_in['b_o'], 'L1_conv_gamma_k': _L1_conv_in['gamma_k'], 'L1_conv_gamma_s': _L1_conv_in['gamma_s'], 'L1_conv_beta': _L1_conv_in['beta'], 'L1_conv_beta_outside': _L1_conv_in['beta_outside'], 'L1_conv_gamma_outside': _L1_conv_in['gamma_outside'], 'L1_ffn_attention_mask': _L1_ffn_in['attention_mask'], 'L1_ffn_wr': _L1_ffn_in['wr'], 'L1_ffn_br': _L1_ffn_in['br'], 'L1_ffn_w1': _L1_ffn_in['w1'], 'L1_ffn_b1': _L1_ffn_in['b1'], 'L1_ffn_w2': _L1_ffn_in['w2'], 'L1_ffn_b2': _L1_ffn_in['b2'], 'L2_conv_in_w': _L2_conv_in['in_w'], 'L2_conv_in_b': _L2_conv_in['in_b'], 'L2_conv_out_w': _L2_conv_in['out_w'], 'L2_conv_out_b': _L2_conv_in['out_b'], 'L2_conv_gamma': _L2_conv_in['gamma'], 'L2_conv_beta': _L2_conv_in['beta'], 'L2_ffn_gate_w': _L2_ffn_in['gate_w'], 'L2_ffn_gate_b': _L2_ffn_in['gate_b'], 'L2_ffn_w1': _L2_ffn_in['w1'], 'L2_ffn_w2': _L2_ffn_in['w2'], 'L2_ffn_w3': _L2_ffn_in['w3'], 'L3_conv_w': _L3_conv_in['w'], 'L3_conv_pruning_mask': _L3_conv_in['pruning_mask'], 'L3_ffn_Wr': _L3_ffn_in['Wr'], 'L3_ffn_br': _L3_ffn_in['br'], 'L3_ffn_ln_g': _L3_ffn_in['ln_g'], 'L3_ffn_ln_b': _L3_ffn_in['ln_b'], 'L3_ffn_W1': _L3_ffn_in['W1'], 'L3_ffn_b1': _L3_ffn_in['b1'], 'L3_ffn_W2': _L3_ffn_in['W2'], 'L3_ffn_b2': _L3_ffn_in['b2']}

def reference(x, L0_conv_w_in, L0_conv_b_in, L0_conv_dw_kernel, L0_conv_dw_bias, L0_conv_ln_gamma, L0_conv_ln_beta, L0_conv_w_off, L0_conv_b_off, L0_conv_w_mask, L0_conv_b_mask, L0_conv_w_out, L0_conv_b_out, L0_ffn_U_i, L0_ffn_V_i, L0_ffn_b_i, L0_ffn_U_f, L0_ffn_V_f, L0_ffn_b_f, L0_ffn_U_c, L0_ffn_V_c, L0_ffn_b_c, L0_ffn_U_o, L0_ffn_V_o, L0_ffn_b_o, L1_conv_gamma_k, L1_conv_gamma_s, L1_conv_beta, L1_conv_beta_outside, L1_conv_gamma_outside, L1_ffn_attention_mask, L1_ffn_wr, L1_ffn_br, L1_ffn_w1, L1_ffn_b1, L1_ffn_w2, L1_ffn_b2, L2_conv_in_w, L2_conv_in_b, L2_conv_out_w, L2_conv_out_b, L2_conv_gamma, L2_conv_beta, L2_ffn_gate_w, L2_ffn_gate_b, L2_ffn_w1, L2_ffn_w2, L2_ffn_w3, L3_conv_w, L3_conv_pruning_mask, L3_ffn_Wr, L3_ffn_br, L3_ffn_ln_g, L3_ffn_ln_b, L3_ffn_W1, L3_ffn_b1, L3_ffn_W2, L3_ffn_b2):
    import jax
    import jax.numpy as jnp

    def _L0_conv_ref(inputs, w_in, b_in, dw_kernel, dw_bias, ln_gamma, ln_beta, w_off, b_off, w_mask, b_mask, w_out, b_out):
        import jax, jax.numpy as jnp
        import numpy as np
        B, H, W, C = (8, 32, 32, 128)
        G, K = (8, 3)
        GC = C // G
        K2 = K * K
        KD = 3
        OFFSET_SCALE = 1.0
        PAD = (K - 1) // 2
        EPS = 1e-06

        def _bilinear_gather(xg, px, py, Hp, Wp):
            x0 = jnp.floor(px)
            y0 = jnp.floor(py)
            wx1 = px - x0
            wy1 = py - y0
            x0i = x0.astype(jnp.int32)
            y0i = y0.astype(jnp.int32)

            def corner(xi, yi, wgt):
                valid = (xi >= 0) & (xi < Wp) & (yi >= 0) & (yi < Hp)
                idx = jnp.clip(yi, 0, Hp - 1) * Wp + jnp.clip(xi, 0, Wp - 1)
                v = jnp.take_along_axis(xg, idx[..., None], axis=2)
                return v * (wgt * valid)[..., None]
            return corner(x0i, y0i, (1 - wx1) * (1 - wy1)) + corner(x0i + 1, y0i, wx1 * (1 - wy1)) + corner(x0i, y0i + 1, (1 - wx1) * wy1) + corner(x0i + 1, y0i + 1, wx1 * wy1)
        x_proj = inputs @ w_in + b_in
        x1 = jax.lax.conv_general_dilated(inputs, dw_kernel, (1, 1), 'SAME', dimension_numbers=('NHWC', 'HWIO', 'NHWC'), feature_group_count=C) + dw_bias
        mu = jnp.mean(x1, -1, keepdims=True)
        var = jnp.mean(jnp.square(x1 - mu), -1, keepdims=True)
        x1 = (x1 - mu) * jax.lax.rsqrt(var + EPS) * ln_gamma + ln_beta
        x1 = jax.nn.gelu(x1, approximate=False)
        offset = (x1 @ w_off + b_off).reshape(B, H, W, G, K2, 2)
        mask = jax.nn.softmax((x1 @ w_mask + b_mask).reshape(B, H, W, G, K2), axis=-1)
        ky, kx = jnp.meshgrid(jnp.arange(K) - PAD, jnp.arange(K) - PAD, indexing='ij')
        kx = kx.reshape(-1).astype(jnp.float32)
        ky = ky.reshape(-1).astype(jnp.float32)
        px = (PAD + jnp.arange(W, dtype=jnp.float32))[None, None, :, None, None] + (kx + offset[..., 0]) * OFFSET_SCALE
        py = (PAD + jnp.arange(H, dtype=jnp.float32))[None, :, None, None, None] + (ky + offset[..., 1]) * OFFSET_SCALE
        Hp, Wp = (H + 2 * PAD, W + 2 * PAD)
        x_pad = jnp.pad(x_proj, ((0, 0), (PAD, PAD), (PAD, PAD), (0, 0)))
        xg = x_pad.reshape(B, Hp * Wp, G, GC).transpose(0, 2, 1, 3)
        N = H * W * K2
        pxf = px.transpose(0, 3, 1, 2, 4).reshape(B, G, N)
        pyf = py.transpose(0, 3, 1, 2, 4).reshape(B, G, N)
        samp = _bilinear_gather(xg, pxf, pyf, Hp, Wp).reshape(B, G, H, W, K2, GC)
        maskg = mask.transpose(0, 3, 1, 2, 4)
        out = jnp.sum(samp * maskg[..., None], axis=4)
        out = out.transpose(0, 2, 3, 1, 4).reshape(B, H, W, C)
        return out @ w_out + b_out

    def _L0_ffn_ref(x, U_i, V_i, b_i, U_f, V_f, b_f, U_c, V_c, b_c, U_o, V_o, b_o):
        import jax, jax.numpy as jnp
        import numpy as np
        from jax import lax
        B, T, _ = x.shape
        H = U_i.shape[1]
        xt = jnp.swapaxes(x, 0, 1)
        xi = xt @ U_i + b_i
        xf = xt @ U_f + b_f
        xg = xt @ U_c + b_c
        xo = xt @ U_o + b_o
        h0 = jnp.zeros((B, H), x.dtype)
        c0 = jnp.zeros((B, H), x.dtype)

        def step(carry, xs):
            h, c = carry
            xi_t, xf_t, xg_t, xo_t = xs
            i_t = jax.nn.sigmoid(xi_t + h @ V_i)
            f_t = jax.nn.sigmoid(xf_t + h @ V_f)
            g_t = jnp.tanh(xg_t + h @ V_c)
            o_t = jax.nn.sigmoid(xo_t + h @ V_o)
            c_new = h * c + i_t * g_t
            h_new = o_t * jnp.tanh(c_new)
            return ((h_new, c_new), h_new)
        (_, _), hs = lax.scan(step, (h0, c0), (xi, xf, xg, xo))
        return jnp.swapaxes(hs, 0, 1)

    def _L1_conv_ref(x, gamma_k, gamma_s, beta, beta_outside, gamma_outside, surround_dist):
        import jax, jax.numpy as jnp
        import numpy as np
        BETA_MIN = 1e-06
        B, H, W, C = x.shape
        G = C // 8
        x2 = x * x
        w = gamma_k[0, 0].reshape(8, G, 8)
        Pk = jnp.einsum('bhwgi,igo->bhwgo', x2.reshape(B, H, W, G, 8), w)
        Pk = Pk.reshape(B, H, W, C)
        mask = jnp.array([[1.0, 1.0, 1.0], [1.0, 0.0, 1.0], [1.0, 1.0, 1.0]], dtype=x.dtype)
        k = gamma_s[..., 0] * mask[:, :, None]
        kern = k[:, :, None, :]
        Ps = jax.lax.conv_general_dilated(x2, kern, window_strides=(1, 1), padding='SAME', rhs_dilation=(surround_dist, surround_dist), dimension_numbers=('NHWC', 'HWIO', 'NHWC'), feature_group_count=C)
        norm_pool = jnp.reciprocal(jnp.sqrt(Pk + Ps + (beta + BETA_MIN)))
        return x * norm_pool * gamma_outside + beta_outside

    def _L1_ffn_ref(x, attention_mask, wr, br, w1, b1, w2, b2):
        import jax, jax.numpy as jnp
        import numpy as np
        B, S, D = (8, 2048, 128)
        H = 4 * D
        CAPACITY = 0.5
        b, s, d = x.shape
        weights = (jnp.einsum('bsd,do->bso', x, wr) + br)[..., 0]
        k = max(1, int(CAPACITY * s))
        kk = k - 1 if k > 1 else 1
        _, idx = jax.lax.top_k(weights, k)
        sel_idx = idx[:, :kk]
        sel = jnp.take_along_axis(x, sel_idx[:, :, None], axis=1)
        h = jax.nn.gelu(jnp.einsum('bkd,dh->bkh', sel, w1) + b1)
        y = jnp.einsum('bkh,hd->bkd', h, w2) + b2
        w_sel = jnp.take_along_axis(weights, sel_idx, axis=1)
        y = y * w_sel[..., None]
        batch_idx = jnp.arange(b)[:, None]
        processed = jnp.zeros_like(x).at[batch_idx, sel_idx].set(y)
        return processed + x

    def _L2_conv_ref(x, in_w, in_b, out_w, out_b, gamma, beta):
        import jax, jax.numpy as jnp
        import numpy as np
        E = 2
        EPS = 1e-05

        def _linear_scan(inp, lam):

            def comb(l, r):
                al, bl = l
                ar, br = r
                return (ar * al, ar * bl + br)
            _, h = jax.lax.associative_scan(comb, (lam, inp), axis=0)
            return h

        def _bidir_scan(inp, lam):
            fwd = _linear_scan(inp, lam)
            rev = jnp.flip(_linear_scan(jnp.flip(inp, 0), jnp.flip(lam, 0)), 0)
            return fwd + rev
        H, W, B, D = x.shape
        nh = D // E
        feat = x @ in_w + in_b
        inp, og, fg = jnp.split(feat, 3, axis=-1)
        inp = jax.nn.silu(inp)
        og = jax.nn.sigmoid(og)
        lam = jax.nn.sigmoid(fg)
        lam = lam.reshape(H, W, B, nh, E)
        inp = inp.reshape(H, W, B, nh, E)
        og = og.reshape(H, W, B, nh, E)
        inp_o = jnp.einsum('...hd,...he->...hde', 1.0 - lam, inp)
        lam_o = jnp.broadcast_to(lam[..., None], inp_o.shape)
        C = nh * E * E
        inp_f = inp_o.reshape(H, W, B, C)
        lam_f = lam_o.reshape(H, W, B, C)
        s_h = _bidir_scan(inp_f, lam_f)
        inp_w = jnp.swapaxes(inp_f, 0, 1)
        lam_w = jnp.swapaxes(lam_f, 0, 1)
        s_w = jnp.swapaxes(_bidir_scan(inp_w, lam_w), 0, 1)
        state = (s_h + s_w).reshape(H, W, B, nh, E, E)
        out = jnp.einsum('...hde,...hd->...he', state, og)
        out = out.reshape(H, W, B, D)
        mu = out.mean(-1, keepdims=True)
        var = out.var(-1, keepdims=True)
        out = (out - mu) * jax.lax.rsqrt(var + EPS) * gamma + beta
        return out @ out_w + out_b

    def _L2_ffn_ref(x, gate_w, gate_b, w1, w2, w3):
        import jax, jax.numpy as jnp
        import numpy as np
        D_MODEL = 128
        N_EXPERTS = 16
        HIDDEN = 256
        SCALE = 0.02
        n_experts = w1.shape[0]
        logits = jnp.einsum('bsd,de->bse', x, gate_w) + gate_b
        probs = jax.nn.softmax(logits, axis=-1)
        top_probs, top_idx = jax.lax.top_k(probs, 2)
        top_probs = top_probs / jnp.sum(top_probs, axis=-1, keepdims=True)
        dispatch = jnp.sum(jax.nn.one_hot(top_idx, n_experts, dtype=x.dtype) * top_probs[..., None], axis=-2)
        h1 = jnp.einsum('bsd,edh->bseh', x, w1)
        h2 = jnp.einsum('bsd,edh->bseh', x, w2)
        hidden = jax.nn.silu(h1) * h2
        expert_out = jnp.einsum('bseh,eho->bseo', hidden, w3)
        return jnp.einsum('bseo,bse->bso', expert_out, dispatch)

    def _L3_conv_ref(x, w, pruning_mask):
        import jax, jax.numpy as jnp
        import numpy as np
        K_SIZE = 3
        CH_IN = 128
        NFILT = 128

        def _magnitude_aware_weight(w):
            scale = jax.lax.stop_gradient(jnp.mean(jnp.abs(w), axis=(0, 1, 2), keepdims=True))
            bw_no_grad = scale * jnp.sign(w)
            clipped = jnp.clip(w, -1.0, 1.0)
            return jax.lax.stop_gradient(bw_no_grad) - jax.lax.stop_gradient(clipped) + clipped
        kernel = _magnitude_aware_weight(w) * pruning_mask.reshape(K_SIZE, K_SIZE, CH_IN, NFILT)
        out = jax.lax.conv_general_dilated(x, kernel, window_strides=(1, 1), padding='SAME', dimension_numbers=('NHWC', 'HWIO', 'NHWC'))
        return out

    def _L3_ffn_ref(x, Wr, br, ln_g, ln_b, W1, b1, W2, b2):
        import jax, jax.numpy as jnp
        import numpy as np
        TOP_K = 2
        LN_EPS = 1e-05
        B, S, D = x.shape
        N = B * S
        xt = x.reshape(N, D)
        logits = xt @ Wr + br
        probs = jax.nn.softmax(logits, axis=-1)
        top_p, top_idx = jax.lax.top_k(probs, TOP_K)
        weights = top_p / top_p.sum(axis=-1, keepdims=True)
        mu = xt.mean(axis=-1, keepdims=True)
        var = ((xt - mu) ** 2).mean(axis=-1, keepdims=True)
        xn = (xt - mu) * jax.lax.rsqrt(var + LN_EPS)
        xe = xn[None, :, :] * ln_g[:, None, :] + ln_b[:, None, :]
        h = jax.nn.gelu(jnp.einsum('end,edh->enh', xe, W1) + b1[:, None, :], approximate=False)
        y = jnp.einsum('enh,ehd->end', h, W2) + b2[:, None, :]
        y_tok = jnp.transpose(y, (1, 0, 2))
        sel = jnp.take_along_axis(y_tok, top_idx[:, :, None], axis=1)
        out = (weights[:, :, None] * sel).sum(axis=1)
        return out.reshape(B, S, D)

    def _gn(v, G=32, eps=1e-05):
        B_, H_, W_, C_ = v.shape
        g = v.reshape(B_, H_, W_, G, C_ // G)
        m = jnp.mean(g, axis=(1, 2, 4), keepdims=True)
        s = jnp.var(g, axis=(1, 2, 4), keepdims=True)
        return ((g - m) / jnp.sqrt(s + eps)).reshape(v.shape)

    def _ln_c(v, eps=1e-06):
        m = jnp.mean(v, axis=-1, keepdims=True)
        s = jnp.var(v, axis=-1, keepdims=True)
        return (v - m) / jnp.sqrt(s + eps)

    def _ln_t(v, eps=1e-05):
        m = jnp.mean(v, axis=-1, keepdims=True)
        s = jnp.var(v, axis=-1, keepdims=True)
        return (v - m) / jnp.sqrt(s + eps)

    def _to_tokens(v):
        B_, H_, W_, C_ = v.shape
        return v.reshape(B_, H_ * W_, C_)

    def _from_tokens(t, like):
        return t.reshape(like.shape)
    x = x + _L0_conv_ref(_ln_c(x), L0_conv_w_in, L0_conv_b_in, L0_conv_dw_kernel, L0_conv_dw_bias, L0_conv_ln_gamma, L0_conv_ln_beta, L0_conv_w_off, L0_conv_b_off, L0_conv_w_mask, L0_conv_b_mask, L0_conv_w_out, L0_conv_b_out)
    t = _to_tokens(x)
    t = t + _L0_ffn_ref(_ln_t(t), L0_ffn_U_i, L0_ffn_V_i, L0_ffn_b_i, L0_ffn_U_f, L0_ffn_V_f, L0_ffn_b_f, L0_ffn_U_c, L0_ffn_V_c, L0_ffn_b_c, L0_ffn_U_o, L0_ffn_V_o, L0_ffn_b_o)
    x = _from_tokens(t, x)
    x = x + _L1_conv_ref(_ln_c(x), L1_conv_gamma_k, L1_conv_gamma_s, L1_conv_beta, L1_conv_beta_outside, L1_conv_gamma_outside, 1)
    t = _to_tokens(x)
    t = t + _L1_ffn_ref(_ln_t(t), L1_ffn_attention_mask, L1_ffn_wr, L1_ffn_br, L1_ffn_w1, L1_ffn_b1, L1_ffn_w2, L1_ffn_b2)
    x = _from_tokens(t, x)
    x = x + _L2_conv_ref(_ln_c(x), L2_conv_in_w, L2_conv_in_b, L2_conv_out_w, L2_conv_out_b, L2_conv_gamma, L2_conv_beta)
    t = _to_tokens(x)
    t = t + _L2_ffn_ref(_ln_t(t), L2_ffn_gate_w, L2_ffn_gate_b, L2_ffn_w1, L2_ffn_w2, L2_ffn_w3)
    x = _from_tokens(t, x)
    x = x + _L3_conv_ref(_ln_c(x), L3_conv_w, L3_conv_pruning_mask)
    t = _to_tokens(x)
    t = t + _L3_ffn_ref(_ln_t(t), L3_ffn_Wr, L3_ffn_br, L3_ffn_ln_g, L3_ffn_ln_b, L3_ffn_W1, L3_ffn_b1, L3_ffn_W2, L3_ffn_b2)
    x = _from_tokens(t, x)
    return x

_drawn_inputs = setup_inputs


def setup_inputs(seed=0):
    import zlib

    import numpy as np

    out = dict(_drawn_inputs(seed))
    spreads = {'L0_conv_b_in': (0.0, 0.356),
     'L0_conv_dw_bias': (0.0, 0.8),
     'L0_conv_ln_gamma': (1.0, 0.6),
     'L0_conv_ln_beta': (0.0, 0.8),
     'L0_conv_b_off': (0.0, 0.8),
     'L0_conv_b_out': (0.0, 0.1),
     'L1_conv_beta_outside': (0.0, 0.1),
     'L1_conv_gamma_outside': (1.0, 0.2),
     'L1_ffn_b1': (0.0, 0.8),
     'L1_ffn_b2': (0.0, 0.8),
     'L2_conv_in_b': (0.0, 0.1),
     'L2_conv_out_b': (0.0, 0.281),
     'L2_conv_gamma': (1.0, 0.6),
     'L2_conv_beta': (0.0, 0.724),
     'L2_ffn_gate_b': (0.0, 0.8),
     'L3_ffn_br': (0.0, 0.36),
     'L3_ffn_ln_g': (1.0, 0.548),
     'L3_ffn_ln_b': (0.0, 0.562),
     'L3_ffn_b1': (0.0, 0.554),
     'L3_ffn_b2': (0.0, 0.388)}
    factors = {'L0_conv_w_in': 2.909,
     'L0_conv_dw_kernel': 8.0,
     'L0_conv_w_off': 8.0,
     'L0_ffn_V_i': 8.0,
     'L0_ffn_b_i': 8.0,
     'L0_ffn_V_c': 3.068,
     'L0_ffn_b_c': 3.318,
     'L0_ffn_V_o': 7.782,
     'L0_ffn_b_o': 8.0,
     'L1_conv_beta': 64.0,
     'L1_ffn_wr': 8.0,
     'L1_ffn_w1': 8.0,
     'L1_ffn_w2': 8.0,
     'L2_ffn_gate_w': 8.0,
     'L2_ffn_w1': 8.0,
     'L2_ffn_w2': 8.0,
     'L2_ffn_w3': 8.0}
    for name, (base, spread) in spreads.items():
        noise = np.random.default_rng([zlib.crc32(name.encode()), seed]).standard_normal(out[name].shape)
        drawn = base * np.exp(spread * noise) if base else spread * noise
        out[name] = jnp.asarray(drawn.astype(out[name].dtype))
    for name, factor in factors.items():
        out[name] = (out[name] * factor).astype(out[name].dtype)
    return out
```

```python
from contextlib import ExitStack

import concourse.bass as bass
from concourse import mybir

F32 = mybir.dt.float32
BF16 = mybir.dt.bfloat16
I32 = mybir.dt.int32
ALU = mybir.AluOpType
ACT = mybir.ActivationFunctionType
AX = mybir.AxisListType

C = 128
IMG, ROWS, COLS = 8, 32, 32
PIX = ROWS * COLS
TOK = IMG * PIX
HALF = PIX // 2
HROWS = ROWS // 2
PAD = ROWS + 2
TILE = 128
TPI = PIX // TILE

START = 1
LOG_EXP = "natural_log_exp_and_others"


def halves(b):
    return [b * PIX + h * HALF for h in range(2)]


class Core:

    def __init__(self, nc, ctx):
        self.nc, self.ctx, self.new_sems = nc, ctx, []
        self.x = self.sb(ctx, "x_t", [C, TOK])
        self.ident = self.sb(ctx, "ident", [C, C])
        self.mean_w = self.sb(ctx, "mean_w", [C, C])
        self.bank = [ctx.enter_context(nc.psum_tensor(f"bank{n}", [C, HALF], F32)) for n in range(8)]
        self.norm = Norm(self)

    def sb(self, mem, name, shape, dtype=F32):
        return mem.enter_context(self.nc.sbuf_tensor(name, shape, dtype))

    def sem(self, name, raised=True):
        s = self.ctx.enter_context(self.nc.semaphore(name))
        if raised:
            self.new_sems.append(s)
        return s

    def start_counts(self):
        raised, self.new_sems = self.new_sems, []
        with self.nc.Block() as block:
            @block.sync
            def _(sp):
                for s in raised:
                    sp.sem_inc(s, START)


class Norm:

    def __init__(self, core):
        ctx = core.ctx
        self.core, self.base = core, 0
        self.mean, self.var = core.bank[0:2], core.bank[2:4]
        self.cent = [core.sb(ctx, f"norm_cent{h}", [C, HALF]) for h in range(2)]
        self.sq = [core.sb(ctx, f"norm_sq{h}", [C, HALF]) for h in range(2)]
        self.rstd = [core.sb(ctx, f"norm_rstd{h}", [C, HALF]) for h in range(2)]
        self.eps = {e: core.sb(ctx, f"norm_eps{n}", [C, 1]) for n, e in enumerate((1e-6, 1e-5))}
        self.s_mean = core.sem("norm_mean")
        self.s_cent = core.sem("norm_centred")
        self.s_sq = core.sem("norm_squared")
        self.s_var = core.sem("norm_variance")
        self.s_log = core.sem("norm_log")
        self.s_rstd = core.sem("norm_rstd_ready")
        self.s_out = core.sem("norm_out")

    def tensor(self, pe, i, src):
        n = self.base + 2 * i
        pe.wait_ge(self.s_cent, START + n)
        for h in range(2):
            out = self.mean[h][:, :] if len(src[h].shape) == 2 else self.mean[h][:, :].rearrange("c (b t) -> c b t", b=src[h].shape[1])
            pe.matmul(out, self.core.mean_w[:, :], src[h], start=True, stop=True).then_inc(self.s_mean, 1)
        pe.wait_ge(self.s_log, START + n)
        for h in range(2):
            pe.wait_ge(self.s_sq, START + n + h + 1)
            pe.matmul(self.var[h][:, :], self.core.mean_w[:, :], self.sq[h][:, :], start=True, stop=True).then_inc(self.s_var, 1)

    def scalar(self, act, i, eps):
        n = self.base + 2 * i
        act.wait_ge(self.s_var, START + n)
        for h in range(2):
            act.wait_ge(self.s_cent, START + n + h + 1)
            act.activation(self.sq[h][:, :], self.cent[h][:, :], ACT.Square).then_inc(self.s_sq, 1)
        act.wait_ge(self.s_out, START + n)
        for h in range(2):
            act.wait_ge(self.s_var, START + n + h + 1)
            act.activation(self.rstd[h][:, :], self.var[h][:, :], ACT.Ln, bias=self.eps[eps][:, 0:1]).then_inc(self.s_log, 1)
        for h in range(2):
            act.wait_ge(self.s_log, START + n + h + 1)
            act.activation(self.rstd[h][:, :], self.rstd[h][:, :], ACT.Exp, scale=-0.5).then_inc(self.s_rstd, 1)

    def vector(self, dve, i, src, dst, cols=COLS):
        n = self.base + 2 * i
        dve.wait_ge(self.s_out, START + n)
        for h in range(2):
            dve.wait_ge(self.s_mean, START + n + h + 1)
            as_src = (lambda t: t) if len(src[h].shape) == 2 else (lambda t: t.rearrange("c (r w) -> c r w", w=cols))
            dve.tensor_tensor(as_src(self.cent[h][:, :]), src[h], as_src(self.mean[h][:, :]), ALU.subtract).then_inc(self.s_cent, 1)
        for h in range(2):
            dve.wait_ge(self.s_rstd, START + n + h + 1)
            dve.tensor_tensor(dst[h], image(self.cent[h], cols), image(self.rstd[h], cols), ALU.mult).then_inc(self.s_out, 1)

    def ready(self, i, h):
        return self.base + 2 * i + h + 1

    def done(self, times=1):
        self.base += 2 * IMG * times


def image(half, cols=COLS):
    return half[:, :].rearrange("c (r w) -> c r w", w=cols)


def inner(padded, h):
    return padded[:, 1 + HROWS * h:1 + HROWS * (h + 1), 1:1 + COLS]


def window(padded, h, tap):
    dy, dx = divmod(tap, 3)
    return padded[:, HROWS * h + dy:HROWS * (h + 1) + dy, dx:dx + COLS]


def column(vec):
    return vec.rearrange("(c o) -> c o", o=1)


def load_x(core, x):
    nc = core.nc
    rows = x.rearrange("i r w c -> (i r w) c").rearrange("(i j p) c -> i p j c", p=TILE, j=TPI)
    with ExitStack() as mem:
        raw = [core.sb(mem, f"raw{k}", [TILE, TPI, C]) for k in range(2)]
        s_const, s_raw, s_turn, s_copied = (core.sem(f"load_{n}") for n in ("const", "raw", "turned", "copied"))
        s_raws = [s_raw, core.sem("load_raw1")]
        core.start_counts()
        with nc.Block() as block:
            @block.gpsimd
            def _(pool):
                pool.memset(core.ident[:, :], 0.0).then_inc(s_const, 1)
                pool.memset(core.mean_w[:, :], 1.0 / C).then_inc(s_const, 1)
                for e, t in core.norm.eps.items():
                    pool.memset(t[:, :], e).then_inc(s_const, 1)
                pool.wait_ge(s_const, START + 4)
                pool.affine_select(out=core.ident[:, :], in_=core.ident[:, :], compare_op=ALU.not_equal, fill=1.0,
                                   base=0, pattern=[[-1, C]], channel_multiplier=1).then_inc(s_const, 1)

            @block.sync
            def _(sp):
                with sp.Fori(0, IMG // 2) as p:
                    for k in range(2):
                        sp.wait_ge(s_turn, START + 4 * p + 2 * k)
                        sp.dma_start(raw[k][:, :, :], rows[2 * p + k]).then_inc(s_raws[k], 16)

            @block.tensor
            def _(pe):
                pe.wait_ge(s_const, START + 5)
                with pe.Fori(0, IMG // 2) as p:
                    for k in range(2):
                        pe.wait_ge(s_raws[k], START + 16 * p + 16)
                        for h in range(2):
                            if k:
                                pe.wait_ge(s_copied, START + 4 * p + h + 1)
                            else:
                                pe.wait_ge(s_copied, START + 4 * p)
                            for j in range(4):
                                mm = pe.transpose(core.bank[h][:, j * TILE:(j + 1) * TILE], raw[k][:, 4 * h + j, :], core.ident[:, :])
                            mm.then_inc(s_turn, 1)

            @block.vector
            def _(dve):
                with dve.Fori(0, IMG // 2) as p:
                    for k in range(2):
                        for h in range(2):
                            dve.wait_ge(s_turn, START + 4 * p + 2 * k + h + 1)
                            dve.tensor_copy(core.x[:, bass.ds(p * (2 * PIX) + (k * PIX + h * HALF), HALF)], core.bank[h][:, :]).then_inc(s_copied, 1)


def store_x(core, out):
    nc = core.nc
    rows = out.rearrange("i r w c -> (i r w) c").rearrange("(i h j p) c -> i h p j c", p=TILE, j=4, h=2)
    with ExitStack() as mem:
        flat = [core.sb(mem, f"flat{h}", [TILE, 4, C]) for h in range(2)]
        s_turn, s_copied = core.sem("store_turned"), core.sem("store_copied")
        s_stored = [core.sem(f"store_done{h}") for h in range(2)]
        stage = [core.sb(mem, f"store_in{h}", [C, HALF]) for h in range(2)]
        s_stage = core.sem("store_staged")
        core.start_counts()
        with nc.Block() as block:
            @block.vector
            def _(dve):
                with dve.Fori(0, IMG) as b:
                    dve.wait_ge(s_turn, START + 2 * b)
                    for h in range(2):
                        dve.tensor_copy(stage[h][:, :], core.x[:, bass.ds(b * PIX + h * HALF, HALF)]).then_inc(s_stage, 1)

            @block.tensor
            def _(pe):
                with pe.Fori(0, IMG) as b:
                    pe.wait_ge(s_copied, START + 2 * b)
                    for h in range(2):
                        pe.wait_ge(s_stage, START + 2 * b + h + 1)
                        for j in range(4):
                            mm = pe.transpose(core.bank[h][:, j * TILE:(j + 1) * TILE], stage[h][:, j * TILE:(j + 1) * TILE], core.ident[:, :])
                        mm.then_inc(s_turn, 1)

            @block.scalar
            def _(act):
                with act.Fori(0, IMG) as b:
                    for h in range(2):
                        act.wait_ge(s_stored[h], START + 16 * b)
                        act.wait_ge(s_turn, START + 2 * b + h + 1)
                        act.activation(flat[h][:, :, :], core.bank[h][:, :].rearrange("p (j c) -> p j c", c=C), ACT.Copy).then_inc(s_copied, 1)

            @block.sync
            def _(sp):
                with sp.Fori(0, IMG) as b:
                    for h in range(2):
                        sp.wait_ge(s_copied, START + 2 * b + h + 1)
                        sp.dma_start(rows[b, h], flat[h][:, :, :]).then_inc(s_stored[h], 16)
                for h in range(2):
                    sp.wait_ge(s_stored[h], START + 16 * IMG)


class Sampling:
    G, TAPS, XY = 8, 9, 2
    GC = C // G
    GT = G * TAPS
    CORNERS = 4
    CELL = CORNERS * GC
    CROWS = 3
    CW = COLS + 3
    CH = -(-(ROWS + 2) // CROWS) * CROWS
    BW, BH = CW, CH + 2
    CELLS = CH * CW * G
    TILES = TOK // TILE
    NOFF = GT * XY
    NLOG = NOFF + GT


def deformable_mixer_and_recurrence(core, args):
    S = Sampling
    table = core.nc.dram_tensor("corner_table", (IMG * S.CELLS, S.CELL), F32).ap()
    with ExitStack() as keep:
        index = core.sb(keep, "df_index", [TILE, TPI, IMG, S.GT], I32)
        weight = core.sb(keep, "df_weight", [TILE, TPI, IMG, S.GT, S.CORNERS])
        with ExitStack() as mem:
            sample_positions(core, args, mem, table, index, weight)
        with ExitStack() as mem:
            gather_samples(core, args, mem, table, index, weight)


def sample_positions(core, args, mem, table, index, weight):
    nc, norm, X, S = core.nc, core.norm, core.x, Sampling
    G, TAPS, XY, GC, GT, CORNERS, CROWS, CW, CH, BW, BH = S.G, S.TAPS, S.XY, S.GC, S.GT, S.CORNERS, S.CROWS, S.CW, S.CH, S.BW, S.BH
    CELLS, NOFF, NLOG = S.CELLS, S.NOFF, S.NLOG
    table_rows = table.rearrange("(i t p g) d -> i t p (g d)", g=G, p=CROWS * CW, i=IMG)
    sb = lambda name, dims, dt=F32: core.sb(mem, f"df_{name}", dims, dt)
    xpad = sb("padded", [C, BH, BW])
    inside = sb("inside", [1, BH, BW])
    ones = sb("ones", [1, TILE])
    w_in, b_in = sb("w_in", [C, C]), sb("b_in", [1, C])
    taps, dw_bias = sb("taps", [C, TAPS]), sb("dw_bias", [C, 1])
    gamma, beta = sb("gamma", [C, 1]), sb("beta", [C, 1])
    w_log, b_log = sb("w_log", [C, NLOG]), sb("b_log", [1, NLOG])
    cells = [sb(f"cells{k}", [CROWS * CW, G * CORNERS * GC]) for k in range(2)]
    x1 = sb("x1", [C, PIX])
    y = sb("y", [C, PIX])
    logit = sb("logits", [TILE, TPI, NLOG])
    pos = sb("pos", [TILE, TPI, GT, XY])
    whole = sb("whole", [TILE, TPI, GT, XY], I32)
    low = sb("low", [TILE, TPI, GT, XY])
    above = sb("above", [TILE, TPI, GT, XY])
    base = sb("base", [TILE, TPI, GT, XY])
    steps = sb("steps", [TILE, TPI * GT], I32)
    part = sb("part", [TILE, 3], I32)
    partf = sb("partf", [TILE, 2])
    row0 = sb("row0", [TILE, TPI * GT])
    mask = sb("mask", [TILE, TPI * G, TAPS])
    top = sb("top", [TILE, TPI * G])
    wy = [sb(f"wy{k}", [TILE, TPI, GT]) for k in range(2)]
    (s_par, s_zero, s_iota, s_pixel, s_base, s_cell, s_copy, s_conv, s_gelu, s_log, s_logit, s_step, s_exp, s_done) = (
        core.sem(f"df_{n}") for n in ("params", "zero", "iota", "pixel", "base", "cells", "cells_copied", "convolved", "gelu", "logit_products",
                                      "logits", "steps", "exp", "positions"))
    s_table = [core.sem(f"df_table{k}") for k in range(2)]
    NT = CH // CROWS
    NSTEP = 16
    xpad_in = [xpad[:, 1 + HROWS * h:1 + HROWS * (h + 1), 1:1 + COLS] for h in range(2)]
    x13 = x1[:, :].rearrange("c (r w) -> c r w", w=COLS)
    y3 = y[:, :].rearrange("c (r w) -> c r w", w=COLS)
    all_ = lambda t: t[:, :, :, :].rearrange("p t s d -> p (t s d)")
    along = lambda t, d: t[:, :, :, d:d + 1].rearrange("p t s d -> p t (s d)")
    NPAR = 10
    core.start_counts()
    with nc.Block() as block:
        @block.sync
        def _(sp):
            p = lambda n: args[f"L0_conv_{n}"]
            row = lambda a: a.rearrange("(o n) -> o n", o=1)
            for dst, src in ((w_in[:, :], p("w_in")), (b_in[:, :], row(p("b_in"))), (dw_bias[:, :], column(p("dw_bias"))),
                             (gamma[:, :], column(p("ln_gamma"))), (beta[:, :], column(p("ln_beta"))),
                             (w_log[:, 0:NOFF], p("w_off")), (w_log[:, NOFF:NLOG], p("w_mask")),
                             (b_log[:, 0:NOFF], row(p("b_off"))), (b_log[:, NOFF:NLOG], row(p("b_mask")))):
                sp.dma_start(dst, src).then_inc(s_par, 16)
            sp.dma_start(taps[:, :], p("dw_kernel").rearrange("a b o c -> c (a b o)"), allow_slow_non_contiguous=True).then_inc(s_par, 16)
            with sp.Fori(0, IMG) as b:
                for t in range(NT):
                    sp.wait_ge(s_copy, START + NT * b + t + 1)
                    sp.dma_start(table_rows[bass.ds(b, 1), t].rearrange("o p d -> p (o d)"), cells[t % 2][:, :]).then_inc(s_table[t % 2], 16)
            for k in range(2):
                sp.wait_ge(s_table[k], START + 16 * NT // 2 * IMG)

        @block.gpsimd
        def _(pool):
            pool.memset(xpad[:, :, :], 0.0).then_inc(s_zero, 1)
            pool.memset(inside[:, :, :], 0.0).then_inc(s_zero, 1)
            pool.memset(ones[:, :], 1.0).then_inc(s_zero, 1)
            pool.wait_ge(s_zero, START + 3)
            pool.memset(inside[:, 1:1 + ROWS, 1:1 + COLS], 1.0).then_inc(s_zero, 1)
            pool.iota(part[:, 0:1], pattern=[[0, 1]], base=0, channel_multiplier=1).then_inc(s_iota, 1)
            for n, pattern in enumerate(([[0, TPI], [0, G], [0, 3], [1, 3]], [[TILE // COLS, TPI], [0, G], [1, 3], [0, 3]], [[0, TPI], [1, G], [0, 3], [0, 3]])):
                if n:
                    pool.wait_ge(s_base, START + n)
                pool.iota(steps[:, :], pattern=pattern, base=0, channel_multiplier=0).then_inc(s_iota, 1)

        @block.tensor
        def _(pe):
            pe.wait_ge(s_par, START + 16 * NPAR)
            pe.wait_ge(s_zero, START + 4)
            with pe.Fori(0, IMG) as b:
                norm.tensor(pe, 2 * b, [X[:, bass.ds(o, HALF)] for o in halves(b)])
                for h in range(2):
                    pe.wait_ge(norm.s_out, START + norm.ready(2 * b, h))
                for t in range(NT):
                    bank = core.bank[4 + t % 2]
                    pe.wait_ge(s_copy, START + NT * b + max(0, t - 1))
                    for k in range(CORNERS):
                        dy, dx = divmod(k, 2)
                        at = slice((CROWS * t + dy) * BW + dx, (CROWS * (t + 1) + dy) * BW + dx)
                        out = bank[0:CROWS * CW, k * C:(k + 1) * C]
                        pe.matmul(out, xpad[:, :, :].rearrange("c h w -> c (h w)")[:, at], w_in[:, :], start=True, stop=False)
                        mm = pe.matmul(out, inside[:, :, :].rearrange("c h w -> c (h w)")[:, at], b_in[:, :], start=False, stop=True)
                    mm.then_inc(s_cell, 1)
                pe.wait_ge(s_conv, START + TAPS * (b + 1))
                norm.tensor(pe, 2 * b + 1, [x1[:, h * HALF:(h + 1) * HALF] for h in range(2)])
                for j in range(TPI):
                    if j % 4 == 0:
                        pe.wait_ge(s_gelu, START + 2 * b + j // 4 + 1)
                    if j % 2 == 0:
                        pe.wait_ge(s_logit, START + 4 * b + max(0, j // 2 - 1))
                    out = core.bank[6 + j // 2 % 2][:, j % 2 * NLOG:(j % 2 + 1) * NLOG]
                    pe.matmul(out, y[:, j * TILE:(j + 1) * TILE], w_log[:, :], start=True, stop=False)
                    mm = pe.matmul(out, ones[:, :], b_log[:, :], start=False, stop=True)
                    if j % 2:
                        mm.then_inc(s_log, 1)

        @block.scalar
        def _(act):
            act.wait_ge(s_par, START + 16 * NPAR)
            with act.Fori(0, IMG) as b:
                norm.scalar(act, 2 * b, 1e-6)
                for t in range(NT):
                    act.wait_ge(s_cell, START + NT * b + t + 1)
                    act.wait_ge(s_table[t % 2], START + 16 * (NT // 2 * b + t // 2))
                    act.activation(cells[t % 2][:, :].rearrange("p (g k c) -> p k g c", g=G, k=CORNERS),
                                   core.bank[4 + t % 2][0:CROWS * CW, :].rearrange("p (k g c) -> p k g c", g=G, k=CORNERS), ACT.Copy).then_inc(s_copy, 1)
                norm.scalar(act, 2 * b + 1, 1e-6)
                for h in range(2):
                    half = y[:, h * HALF:(h + 1) * HALF]
                    act.wait_ge(norm.s_out, START + norm.ready(2 * b + 1, h))
                    act.activation(half, half, ACT.Gelu, scale=gamma[:, 0:1], bias=beta[:, 0:1]).then_inc(s_gelu, 1)
                act.wait_ge(s_done, START + b)
                for j in range(4):
                    act.wait_ge(s_log, START + 4 * b + j + 1)
                    act.activation(logit[:, 2 * j:2 * j + 2, :], core.bank[6 + j % 2][:, 0:2 * NLOG].rearrange("p (t n) -> p t n", n=NLOG), ACT.Copy).then_inc(s_logit, 1)
                act.wait_ge(s_step, START + NSTEP * b + 3)
                act.activation(mask[:, :, :], mask[:, :, :], ACT.Exp).then_inc(s_exp, 1)

        def positions(dve, b):
            count = 0

            def step(ins):
                nonlocal count
                count += 1
                return ins.then_inc(s_step, 1)

            def after(n):
                dve.wait_ge(s_step, START + NSTEP * b + n)

            ml = logit[:, :, NOFF:NLOG].rearrange("p t (g k) -> p t g k", k=TAPS)
            mg = mask[:, :, :].rearrange("p (t g) k -> p t g k", g=G)
            m3 = mask[:, :, :].rearrange("p (t g) k -> p t (g k)", g=G)
            top_t = top[:, :].rearrange("p (t g) -> p t g", g=G)
            top_wide = top[:, :].rearrange("p (n k) -> p n k", k=1).broadcast_to([TILE, TPI * G, TAPS])
            by_tile = lambda t: t[:, :, :, :].rearrange("p t s d -> p t (s d)")
            step(dve.tensor_reduce(top_t, ml, AX.X, ALU.max))
            step(dve.tensor_tensor(by_tile(pos), logit[:, :, 0:NOFF], by_tile(base), ALU.add))
            after(1)
            step(dve.tensor_tensor(mg, ml, top_t.rearrange("p t (g k) -> p t g k", k=1).broadcast_to([TILE, TPI, G, TAPS]), ALU.subtract))
            after(2)
            step(dve.tensor_scalar(all_(pos), all_(pos), 0.0, float(COLS + 1), ALU.max, ALU.min))
            after(4)
            step(dve.tensor_copy(all_(whole), all_(pos)))
            after(5)
            step(dve.tensor_copy(all_(low), all_(whole)))
            after(6)
            step(dve.tensor_tensor(all_(above), all_(low), all_(pos), ALU.is_gt))
            after(7)
            step(dve.tensor_tensor(all_(low), all_(low), all_(above), ALU.subtract))
            after(8)
            step(dve.tensor_tensor(all_(pos), all_(pos), all_(low), ALU.subtract))
            after(9)
            step(dve.tensor_scalar(all_(above), all_(pos), -1.0, 1.0, ALU.mult, ALU.add))
            flat = lambda t: t[:, :, :].rearrange("p t s -> p (t s)")
            step(dve.scalar_tensor_tensor(out=flat(wy[0]), in0=along(low, 1), scalar=float(CW), in1=along(low, 0), op0=ALU.mult, op1=ALU.add))
            after(11)
            step(dve.scalar_tensor_tensor(out=index[:, :, bass.ds(b, 1), :].rearrange("p t b s -> p t (b s)"), in0=wy[0][:, :, :], scalar=float(G),
                                          in1=row0[:, :].rearrange("p (t s) -> p t s", s=GT), op0=ALU.mult, op1=ALU.add))
            dve.wait_ge(s_exp, START + b + 1)
            step(dve.tensor_reduce(top[:, :], mask[:, :, :], AX.X, ALU.add))
            after(13)
            step(dve.reciprocal(top[:, :], top[:, :]))
            after(12)
            dve.tensor_scalar(row0[:, :], row0[:, :], float(CELLS), None, ALU.add)
            after(14)
            step(dve.tensor_tensor(mask[:, :, :], mask[:, :, :], top_wide, ALU.mult))
            after(15)
            dve.tensor_tensor(flat(wy[0]), along(above, 1), m3.rearrange("p t s -> p (t s)"), ALU.mult)
            step(dve.tensor_tensor(flat(wy[1]), along(pos, 1), m3.rearrange("p t s -> p (t s)"), ALU.mult))
            after(16)
            for k in range(CORNERS):
                dy, dx = divmod(k, 2)
                out = weight[:, :, bass.ds(b, 1), :, k:k + 1].rearrange("p t b s k -> p t (b s k)")
                ins = dve.tensor_tensor(out, wy[dy][:, :, :], (pos if dx else above)[:, :, :, 0:1].rearrange("p t s d -> p t (s d)"), ALU.mult)
            ins.then_inc(s_done, 1)
            assert count == NSTEP

        @block.vector
        def _(dve):
            dve.wait_ge(s_iota, START + 1)
            dve.tensor_scalar(part[:, 1:2], part[:, 0:1], COLS - 1, None, ALU.bitwise_and).then_inc(s_pixel, 1)
            dve.tensor_scalar(part[:, 2:3], part[:, 0:1], COLS.bit_length() - 1, None, ALU.logical_shift_right).then_inc(s_pixel, 1)
            dve.wait_ge(s_pixel, START + 2)
            dve.tensor_copy(partf[:, :], part[:, 1:3]).then_inc(s_pixel, 1)
            dve.wait_ge(s_pixel, START + 3)
            flat_steps = steps[:, :].rearrange("p (t s) -> p t s", s=GT)
            for d in range(XY):
                dve.wait_ge(s_iota, START + 2 + d)
                dve.tensor_scalar(along(base, d), flat_steps, partf[:, d:d + 1], None, ALU.add).then_inc(s_base, 1)
            dve.wait_ge(s_iota, START + 4)
            dve.tensor_copy(row0[:, :], steps[:, :]).then_inc(s_base, 1)
            dve.wait_ge(s_base, START + 3)
            dve.wait_ge(s_par, START + 16 * NPAR)
            dve.wait_ge(s_zero, START + 4)
            with dve.Fori(0, IMG) as b:
                dve.wait_ge(s_cell, START + NT * b)
                norm.vector(dve, 2 * b, [X[:, bass.ds(o, HALF)] for o in halves(b)], xpad_in)
                for h in range(2):
                    dve.wait_ge(norm.s_out, START + norm.ready(2 * b, h))
                for t in range(TAPS):
                    win = xpad[:, t // 3:t // 3 + ROWS, t % 3:t % 3 + COLS]
                    if t == 0:
                        dve.tensor_scalar(x13, win, taps[:, 0:1], dw_bias[:, 0:1], ALU.mult, ALU.add).then_inc(s_conv, 1)
                        continue
                    dve.wait_ge(s_conv, START + TAPS * b + t)
                    dve.scalar_tensor_tensor(out=x13, in0=win, scalar=taps[:, t:t + 1], in1=x13, op0=ALU.mult, op1=ALU.add).then_inc(s_conv, 1)
                dve.wait_ge(s_conv, START + TAPS * (b + 1))
                dve.wait_ge(s_log, START + 4 * b)
                norm.vector(dve, 2 * b + 1, [x1[:, h * HALF:(h + 1) * HALF] for h in range(2)], [y3[:, 0:HROWS], y3[:, HROWS:ROWS]])
                dve.wait_ge(s_logit, START + 4 * b + 4)
                positions(dve, b)
    norm.done(2)


def gather_samples(core, args, mem, table, index, weight):
    X, norm, S = core.x, core.norm, Sampling
    G, GC, GT, CORNERS, CELL, TILES = S.G, S.GC, S.GT, S.CORNERS, S.CELL, S.TILES
    GATES = (("i", 0.5), ("o", 0.5), ("c", 1.0))
    NG = len(GATES)
    W = NG * IMG
    SLOT = TILE // IMG
    UNROLL = 8
    NM = 2 * NG
    sb = lambda name, dims, dt=F32: core.sb(mem, f"dg_{name}", dims, dt)
    own = [sb(f"own_index{k}", [TILE, GT], I32) for k in range(2)]
    samples = [sb(f"samples{k}", [TILE, GT * CELL]) for k in range(2)]
    summed = [sb(f"summed{k}", [TILE, C]) for k in range(2)]
    turned = [sb(f"turned{k}", [C, TILE]) for k in range(2)]
    w_out, b_out = sb("w_out", [C, C]), sb("b_out", [C, 1])
    v = sb("v", [C, PIX])
    v3 = v[:, :].rearrange("c (b t) -> c b t", t=TILE)
    wu, wv, bias = sb("u_w", [C, NG, C]), sb("v_w", [C, NG, C]), sb("gate_bias", [C, NG])
    gx = sb("gate_inputs", [C, TILE, W])
    hs = sb("hidden", [C, TILE + 1, IMG])
    gates = sb("gates", [C, W])
    cell, hc, tc, ig, og = (sb(n, [C, IMG]) for n in ("cell", "hc", "tanh_cell", "ig", "og"))
    (s_par, s_half, s_zero, s_begun, s_own, s_weighted, s_turn, s_copy, s_out, s_end, s_gmm, s_gx,
     s_pre, s_tanh, s_ig, s_og, s_cell, s_tc, s_h, s_hc, s_carry, s_x) = (core.sem(f"dg_{n}") for n in (
        "params", "halved", "zero", "begun", "own_index", "weighted", "turned", "turned_copied", "out_product", "end", "gate_products",
        "gate_inputs", "preacts", "tanh", "ig", "og", "cell", "tanh_cell", "hidden", "hc", "carried", "x"))
    s_sum = [core.sem(f"dg_summed{k}") for k in range(2)]
    NS = 4
    s_got = [[core.sem(f"dg_samples{k}_{n}", raised=False) for n in range(NS)] for k in range(2)]
    PER = GT // NS
    NPAR = 2 + 3 * NG
    tokens = X[:, :].rearrange("c (b j t) -> c b j t", b=IMG, j=TPI)

    def phase_half(j, h):
        return tokens[:, 4 * h:4 * h + 4, bass.ds(j, 1), :].rearrange("c b j t -> c b (j t)")

    def slots(eng, steps, tile, finish):
        with eng.Fori(0, IMG // 2) as p:
            for k in range(2):
                tile(0, p, k)
        finish(0)
        with eng.Fori(1, TPI) as j:
            with eng.Fori(0, IMG // 2) as p:
                for k in range(2):
                    with eng.Fori(0, SLOT // UNROLL) as s:
                        for u in range(UNROLL):
                            at = (2 * p + k) * SLOT + s * UNROLL + u
                            steps((j - 1) * TILE + at, at, u)
                    tile(j, p, k)
            finish(j)
        with eng.Fori(0, TILE // UNROLL) as s:
            for u in range(UNROLL):
                steps((TPI - 1) * TILE + s * UNROLL + u, s * UNROLL + u, u)

    core.start_counts()
    with core.nc.Block() as block:
        @block.sync
        def _(sp):
            sp.dma_start(w_out[:, :], args["L0_conv_w_out"]).then_inc(s_par, 16)
            sp.dma_start(b_out[:, :], column(args["L0_conv_b_out"])).then_inc(s_par, 16)
            for n, (g, _) in enumerate(GATES):
                sp.dma_start(wu[:, n, :], args[f"L0_ffn_U_{g}"]).then_inc(s_par, 16)
                sp.dma_start(wv[:, n, :], args[f"L0_ffn_V_{g}"]).then_inc(s_par, 16)
                sp.dma_start(bias[:, n:n + 1], column(args[f"L0_ffn_b_{g}"])).then_inc(s_par, 16)

        @block.gpsimd
        def _(pool):
            pool.memset(hs[:, 0:1, :], 0.0).then_inc(s_zero, 1)
            pool.memset(hc[:, :], 0.0).then_inc(s_zero, 1)
            rows = index[:, :, :, :].rearrange("p t b s -> p (t b s)")
            with pool.Fori(0, TILES // 2) as p:
                for k in range(2):
                    pool.wait_ge(s_sum[k], START + p)
                    pool.sem_inc(s_begun, 1)
                    pool.tensor_copy(own[k][:, :], rows[:, bass.ds((2 * p + k) * GT, GT)]).then_inc(s_own, 1)
                    pool.wait_ge(s_own, START + 2 * p + k + 1)
                    pool.sem_inc(s_begun, 1)
                    for s in range(GT):
                        pool.indirect_dma_start(samples[k][:, s * CELL:(s + 1) * CELL], None, table[:, :],
                                                bass.IndirectOffsetOnAxis(ap=own[k][:, s:s + 1], axis=0)).then_inc(s_got[k][s // PER], 16)

        @block.tensor
        def _(pe):
            def steps(t, at, u):
                bank = core.bank[4 + u % 2]
                pe.matmul(bank[:, 0:W], core.ident[:, :], gx[:, bass.ds(at, 1), :].rearrange("c o w -> c (o w)"), start=True, stop=False)
                pe.wait_ge(s_h, START + t)
                for g in range(NG):
                    mm = pe.matmul(bank[:, g * IMG:(g + 1) * IMG], wv[:, g, :], hs[:, bass.ds(at, 1), :].rearrange("c o w -> c (o w)"),
                                   start=False, stop=(g == NG - 1))
                mm.then_inc(s_pre, 1)

            def tile(j, p, k):
                q = j * (IMG // 2) + p
                pe.wait_ge(s_sum[k], START + q + 1)
                pe.transpose(core.bank[6][:, k * TILE:(k + 1) * TILE], summed[k][:, :], core.ident[:, :]).then_inc(s_turn, 1)
                pe.wait_ge(s_copy, START + 2 * q + k + 1)
                pe.matmul(core.bank[7][:, k * TILE:(k + 1) * TILE], w_out[:, :], turned[k][:, :], start=True, stop=True).then_inc(s_out, 1)

            def finish(j):
                pe.wait_ge(s_end, START + IMG * (j + 1))
                norm.tensor(pe, j, [phase_half(j, h) for h in range(2)])
                for h in range(2):
                    pe.wait_ge(norm.s_out, START + norm.ready(j, h))
                    for g in range(NG):
                        m = NG * h + g
                        pe.wait_ge(s_gx, START + NM * j + max(0, m - 3))
                        pe.matmul(core.bank[4 + m % 4][:, :], wu[:, g, :], v[:, h * HALF:(h + 1) * HALF], start=True, stop=True).then_inc(s_gmm, 1)
                pe.wait_ge(s_gx, START + NM * (j + 1))
                pe.wait_ge(s_carry, START + j)

            pe.wait_ge(s_par, START + 16 * NPAR)
            pe.wait_ge(s_half, START + 2)
            pe.wait_ge(s_zero, START + 2)
            slots(pe, steps, tile, finish)

        @block.scalar
        def _(act):
            def steps(t, at, u):
                act.wait_ge(s_pre, START + t + 1)
                act.activation(gates[:, :], core.bank[4 + u % 2][:, 0:W], ACT.Tanh).then_inc(s_tanh, 1)
                act.wait_ge(s_cell, START + t + 1)
                act.activation(tc[:, :], cell[:, :], ACT.Tanh).then_inc(s_tc, 1)

            def tile(j, p, k):
                act.wait_ge(s_turn, START + 2 * (j * (IMG // 2) + p) + k + 1)
                act.activation(turned[k][:, :], core.bank[6][:, k * TILE:(k + 1) * TILE], ACT.Copy).then_inc(s_copy, 1)

            def finish(j):
                norm.scalar(act, j, 1e-5)
                for h in range(2):
                    for g, (_, scale) in enumerate(GATES):
                        m = NG * h + g
                        act.wait_ge(s_gmm, START + NM * j + m + 1)
                        act.activation(gx[:, :, g * IMG + 4 * h:g * IMG + 4 * h + 4].rearrange("c t b -> c b t"),
                                       core.bank[4 + m % 4][:, :].rearrange("c (b t) -> c b t", t=TILE), ACT.Identity,
                                       bias=bias[:, g:g + 1], scale=scale).then_inc(s_gx, 1)

            act.wait_ge(s_half, START + 2)
            slots(act, steps, tile, finish)

        @block.vector
        def _(dve):
            def steps(t, at, u):
                dve.wait_ge(s_tanh, START + t + 1)
                dve.scalar_tensor_tensor(out=ig[:, :], in0=gates[:, 0:IMG], scalar=1.0, in1=gates[:, 2 * IMG:W], op0=ALU.add, op1=ALU.mult).then_inc(s_ig, 1)
                dve.tensor_scalar(og[:, :], gates[:, IMG:2 * IMG], 0.5, 0.5, ALU.mult, ALU.add).then_inc(s_og, 1)
                dve.wait_ge(s_hc, START + t)
                dve.wait_ge(s_ig, START + t + 1)
                dve.scalar_tensor_tensor(out=cell[:, :], in0=ig[:, :], scalar=0.5, in1=hc[:, :], op0=ALU.mult, op1=ALU.add).then_inc(s_cell, 1)
                dve.wait_ge(s_og, START + t + 1)
                dve.wait_ge(s_tc, START + t + 1)
                now = hs[:, bass.ds(at + 1, 1), :].rearrange("c o w -> c (o w)")
                dve.tensor_tensor(now, og[:, :], tc[:, :], ALU.mult).then_inc(s_h, 1)
                dve.wait_ge(s_h, START + t + 1)
                dve.tensor_tensor(hc[:, :], now, cell[:, :], ALU.mult).then_inc(s_hc, 1)

            def tile(j, p, k):
                q = j * (IMG // 2) + p
                for s in range(NS):
                    dve.wait_ge(s_got[k][s], 16 * PER * (q + 1))
                by_value = samples[k][:, :].rearrange("p (s c) -> p s c", c=GC)
                flat = weight[:, :, :, :, :].rearrange("p t b s k -> p (t b s k)")
                w = flat[:, bass.ds((2 * q + k) * (GT * CORNERS), GT * CORNERS)].rearrange("p (s c) -> p s c", c=1).broadcast_to([TILE, GT * CORNERS, GC])
                dve.tensor_tensor(by_value, by_value, w, ALU.mult).then_inc(s_weighted, 1)
                dve.wait_ge(s_weighted, START + 2 * q + k + 1)
                dve.tensor_reduce(summed[k][:, :].rearrange("p (g c) -> p g c", g=G), samples[k][:, :].rearrange("p (g s c) -> p g c s", g=G, c=GC), AX.X, ALU.add).then_inc(s_sum[k], 1)
                xs = X[:, bass.ds((2 * p + k) * PIX + j * TILE, TILE)]
                dve.wait_ge(s_out, START + 2 * q + k + 1)
                dve.scalar_tensor_tensor(out=xs, in0=core.bank[7][:, k * TILE:(k + 1) * TILE], scalar=b_out[:, 0:1], in1=xs, op0=ALU.add, op1=ALU.add).then_inc(s_end, 1)

            def add_hidden(j):
                dve.wait_ge(s_h, START + TILE * (j + 1))
                xs = tokens[:, :, bass.ds(j, 1), :].rearrange("c b j t -> c b (j t)")
                dve.tensor_tensor(xs, xs, hs[:, 1:TILE + 1, :].rearrange("c t b -> c b t"), ALU.add).then_inc(s_x, 1)
                dve.tensor_copy(hs[:, 0:1, :], hs[:, TILE:TILE + 1, :]).then_inc(s_carry, 1)

            def finish(j):
                if not isinstance(j, int):
                    add_hidden(j - 1)
                dve.wait_ge(s_end, START + IMG * (j + 1))
                norm.vector(dve, j, [phase_half(j, h) for h in range(2)], [v3[:, 4 * h:4 * h + 4] for h in range(2)], TILE)

            dve.wait_ge(s_par, START + 16 * NPAR)
            dve.tensor_scalar(wv[:, 0:2, :], wv[:, 0:2, :], 0.5, None, ALU.mult).then_inc(s_half, 1)
            dve.tensor_scalar(bias[:, 0:2], bias[:, 0:2], 0.5, None, ALU.mult).then_inc(s_half, 1)
            dve.wait_ge(s_zero, START + 2)
            slots(dve, steps, tile, finish)
            add_hidden(TPI - 1)
    norm.done()


def divisive_mixer(core, args):
    nc, norm, X = core.nc, core.norm, core.x
    G = 8
    with ExitStack() as mem:
        v = core.sb(mem, "dv_v", [C, PIX])
        v2 = core.sb(mem, "dv_squares", [C, PAD, PAD])
        pool_w = core.sb(mem, "dv_pool_w", [C, C])
        taps = core.sb(mem, "dv_taps", [C, 9])
        vecs = core.sb(mem, "dv_vecs", [C, 3])
        beta = core.sb(mem, "dv_beta", [C, 1])
        acc = core.sb(mem, "dv_acc", [C, PIX])
        s_zero, s_par, s_beta, s_v2, s_pool, s_acc, s_den, s_log, s_rsqrt, s_end = (
            core.sem(f"dv_{n}") for n in ("zero", "params", "beta", "squares", "pooled", "acc", "den", "log", "rsqrt", "end"))
        TAPS = [t for t in range(9) if t != 4]
        NACC = len(TAPS) + 1
        NPAR = 4 + C // G
        acc3 = acc[:, :].rearrange("c (r w) -> c r w", w=COLS)
        v3 = v[:, :].rearrange("c (r w) -> c r w", w=COLS)
        core.start_counts()
        with nc.Block() as block:
            @block.gpsimd
            def _(pool):
                pool.memset(pool_w[:, :], 0.0).then_inc(s_zero, 1)
                pool.memset(v2[:, :, :], 0.0).then_inc(s_zero, 1)
                pool.wait_ge(s_par, START + 16 * NPAR)
                pool.tensor_scalar(beta[:, :], vecs[:, 0:1], 1e-6, None, ALU.add).then_inc(s_beta, 1)

            @block.sync
            def _(sp):
                sp.dma_start(taps[:, :], args["L1_conv_gamma_s"].rearrange("a b c o -> c (a b o)"), allow_slow_non_contiguous=True).then_inc(s_par, 16)
                for n, name in enumerate(("beta", "gamma_outside", "beta_outside")):
                    sp.dma_start(vecs[:, n:n + 1], column(args[f"L1_conv_{name}"])).then_inc(s_par, 16)
                sp.wait_ge(s_zero, START + 1)
                for g in range(C // G):
                    sp.dma_start(pool_w[G * g:G * g + G, G * g:G * g + G], args["L1_conv_gamma_k"][0, 0, :, G * g:G * g + G]).then_inc(s_par, 16)

            @block.tensor
            def _(pe):
                pe.wait_ge(s_par, START + 16 * NPAR)
                with pe.Fori(0, IMG) as b:
                    norm.tensor(pe, b, [X[:, bass.ds(o, HALF)] for o in halves(b)])
                    pe.wait_ge(s_den, START + b)
                    pe.wait_ge(s_v2, START + b + 1)
                    for h in range(2):
                        mm = pe.matmul(image(core.bank[4 + h]), pool_w[:, :], inner(v2, h), start=True, stop=True)
                    mm.then_inc(s_pool, 1)

            @block.scalar
            def _(act):
                act.preload_act_table_set(LOG_EXP)
                act.wait_ge(s_zero, START + 2)
                act.wait_ge(s_beta, START + 1)
                with act.Fori(0, IMG) as b:
                    norm.scalar(act, b, 1e-6)
                    act.wait_ge(norm.s_out, START + norm.ready(b, 1))
                    act.wait_ge(s_pool, START + b)
                    act.wait_ge(s_acc, START + NACC * b)
                    act.activation(v2[:, 1:1 + ROWS, 1:1 + COLS], v3, ACT.Square).then_inc(s_v2, 1)
                    act.wait_ge(s_den, START + b + 1)
                    act.activation(acc[:, :], acc[:, :], ACT.Ln, bias=beta[:, 0:1]).then_inc(s_log, 1)
                    act.wait_ge(s_log, START + b + 1)
                    act.activation(acc[:, :], acc[:, :], ACT.Exp, scale=-0.5).then_inc(s_rsqrt, 1)

            @block.vector
            def _(dve):
                dve.wait_ge(s_par, START + 16 * NPAR)
                with dve.Fori(0, IMG) as b:
                    dve.wait_ge(s_end, START + 2 * b)
                    norm.vector(dve, b, [X[:, bass.ds(o, HALF)] for o in halves(b)], [v3[:, 0:HROWS], v3[:, HROWS:ROWS]])
                    dve.wait_ge(s_v2, START + b + 1)
                    for n, t in enumerate(TAPS):
                        win = v2[:, t // 3:t // 3 + ROWS, t % 3:t % 3 + COLS]
                        if n == 0:
                            dve.tensor_scalar(acc3, win, taps[:, t:t + 1], None, ALU.mult).then_inc(s_acc, 1)
                            continue
                        dve.wait_ge(s_acc, START + NACC * b + n)
                        dve.scalar_tensor_tensor(out=acc3, in0=win, scalar=taps[:, t:t + 1], in1=acc3, op0=ALU.mult, op1=ALU.add).then_inc(s_acc, 1)
                    dve.wait_ge(s_acc, START + NACC * b + len(TAPS))
                    dve.wait_ge(s_pool, START + b + 1)
                    dve.tensor_tensor(acc[:, 0:HALF], acc[:, 0:HALF], core.bank[4][:, :], ALU.add).then_inc(s_acc, 1)
                    dve.tensor_tensor(acc[:, HALF:PIX], acc[:, HALF:PIX], core.bank[5][:, :], ALU.add).then_inc(s_den, 1)
                    dve.wait_ge(s_rsqrt, START + b + 1)
                    dve.scalar_tensor_tensor(out=acc[:, :], in0=v[:, :], scalar=vecs[:, 1:2], in1=acc[:, :], op0=ALU.mult, op1=ALU.mult).then_inc(s_end, 1)
                    dve.wait_ge(s_end, START + 2 * b + 1)
                    xs = X[:, bass.ds(b * PIX, PIX)]
                    dve.scalar_tensor_tensor(out=xs, in0=acc[:, :], scalar=vecs[:, 2:3], in1=xs, op0=ALU.add, op1=ALU.add).then_inc(s_end, 1)
        norm.done()


def routed_depth_ffn(core, args):
    nc, norm, X = core.nc, core.norm, core.x
    HID = args["L1_ffn_w1"].shape[1]
    NHC = HID // C
    CHOSEN = PIX // 2 - 1
    with ExitStack() as mem:
        v = core.sb(mem, "rd_v", [C, PIX])
        v3 = v[:, :].rearrange("c (r w) -> c r w", w=COLS)
        wr = core.sb(mem, "rd_wr", [C, 1])
        wr_wide = core.sb(mem, "rd_wr_wide", [C, C])
        br = core.sb(mem, "rd_br", [C, 1])
        w1 = core.sb(mem, "rd_w1", [C, HID])
        w2 = core.sb(mem, "rd_w2", [C, NHC, C])
        b1 = core.sb(mem, "rd_b1", [C, NHC])
        b2 = core.sb(mem, "rd_b2", [C, 1])
        ones = core.sb(mem, "rd_ones", [C, C], BF16)
        before = core.sb(mem, "rd_before", [C, C])
        weight = core.sb(mem, "rd_weight", [C, PIX])
        wcol = core.sb(mem, "rd_weight_col", [C, TPI])
        diag = core.sb(mem, "rd_diag", [C, TILE])
        equal = core.sb(mem, "rd_equal", [C, TILE])
        less = core.sb(mem, "rd_less", [C, TILE])
        ahead = core.sb(mem, "rd_ahead", [C, TPI, PIX], BF16)
        coef = core.sb(mem, "rd_coef", [C, PIX])
        hid = [core.sb(mem, f"rd_hidden{k}", [C, HALF]) for k in range(2)]
        y = [core.sb(mem, f"rd_y{h}", [C, HALF]) for h in range(2)]
        (s_par, s_const, s_wide, s_wmm, s_weight, s_diag, s_tie, s_ahead, s_rank, s_coef, s_h1, s_hid, s_y, s_ysum, s_end) = (
            core.sem(f"rd_{n}") for n in ("params", "const", "wide", "weight_product", "weight", "weight_col", "ties", "ahead", "rank",
                                          "coef", "hidden_product", "hidden", "y_product", "y_weighted", "end"))
        NPAR = 5 + NHC
        NH1 = 2 * NHC
        core.start_counts()
        with nc.Block() as block:
            @block.sync
            def _(sp):
                sp.dma_start(wr[:, :], args["L1_ffn_wr"]).then_inc(s_par, 16)
                sp.dma_start(br[:, :], args["L1_ffn_br"].rearrange("(a o) -> a o", o=1).broadcast_to([C, 1])).then_inc(s_par, 16)
                sp.dma_start(w1[:, :], args["L1_ffn_w1"]).then_inc(s_par, 16)
                sp.dma_start(w2[:, :, :], args["L1_ffn_w2"].rearrange("(k p) d -> p k d", p=C)).then_inc(s_par, 16)
                sp.dma_start(b2[:, :], column(args["L1_ffn_b2"])).then_inc(s_par, 16)
                for k in range(NHC):
                    sp.dma_start(b1[:, k:k + 1], column(args["L1_ffn_b1"][k * C:(k + 1) * C])).then_inc(s_par, 16)

            @block.gpsimd
            def _(pool):
                pool.memset(ones[:, :], 1.0).then_inc(s_const, 1)
                pool.memset(before[:, :], 1.0).then_inc(s_const, 1)
                pool.wait_ge(s_const, START + 2)
                pool.affine_select(out=before[:, :], in_=before[:, :], compare_op=ALU.is_gt, fill=0.0,
                                   base=0, pattern=[[1, C]], channel_multiplier=-1).then_inc(s_const, 1)

            @block.tensor
            def _(pe):
                pe.wait_ge(s_par, START + 16 * NPAR)
                pe.wait_ge(s_wide, START + 1)
                pe.wait_ge(s_const, START + 3)
                with pe.Fori(0, IMG) as b:
                    norm.tensor(pe, b, [X[:, bass.ds(o, HALF)] for o in halves(b)])
                    pe.wait_ge(s_ysum, START + 2 * b)
                    for h in range(2):
                        pe.wait_ge(norm.s_out, START + norm.ready(b, h))
                        pe.matmul(core.bank[4 + h][:, :], wr_wide[:, :], v[:, h * HALF:(h + 1) * HALF], start=True, stop=True).then_inc(s_wmm, 1)

                    def first(h, k):
                        m = NHC * h + k
                        pe.wait_ge(s_hid, START + NH1 * b + max(0, m - 1))
                        pe.matmul(core.bank[6 + m % 2][:, :], w1[:, k * C:(k + 1) * C], v[:, h * HALF:(h + 1) * HALF], start=True, stop=True).then_inc(s_h1, 1)

                    first(0, 0)
                    first(0, 1)
                    pe.wait_ge(s_weight, START + 2 * b + 2)
                    pe.wait_ge(s_ahead, START + TPI * (b + 1))
                    for h in range(2):
                        for j in range(TPI):
                            mm = pe.matmul(core.bank[4 + h][:, :], ones[:, :], ahead[:, j, h * HALF:(h + 1) * HALF], start=(j == 0), stop=(j == TPI - 1))
                        mm.then_inc(s_rank, 1)
                    for h in range(2):
                        pe.wait_ge(s_coef, START + 2 * b + h + 1)
                        for k in range(NHC):
                            m = NHC * h + k
                            pe.wait_ge(s_hid, START + NH1 * b + m + 1)
                            pe.matmul(core.bank[4 + h][:, :], w2[:, k, :], hid[m % 2][:, :], start=(k == 0), stop=(k == NHC - 1)).then_inc(s_y, 1)
                            if m + 2 < NH1:
                                first(*divmod(m + 2, NHC))

            @block.scalar
            def _(act):
                act.wait_ge(s_par, START + 16 * NPAR)
                with act.Fori(0, IMG) as b:
                    norm.scalar(act, b, 1e-5)
                    act.wait_ge(s_coef, START + 2 * b)
                    for h in range(2):
                        act.wait_ge(s_wmm, START + 2 * b + h + 1)
                        act.activation(weight[:, h * HALF:(h + 1) * HALF], core.bank[4 + h][:, :], ACT.Identity, bias=br[:, 0:1]).then_inc(s_weight, 1)
                    for m in range(NH1):
                        act.wait_ge(s_h1, START + NH1 * b + m + 1)
                        act.wait_ge(s_y, START + NH1 * b + max(0, m - 1))
                        act.activation(hid[m % 2][:, :], core.bank[6 + m % 2][:, :], ACT.Gelu_apprx_tanh, bias=b1[:, m % NHC:m % NHC + 1]).then_inc(s_hid, 1)

            @block.vector
            def _(dve):
                dve.wait_ge(s_par, START + 16 * NPAR)
                dve.tensor_copy(wr_wide[:, :], wr[:, 0:1].broadcast_to([C, C])).then_inc(s_wide, 1)
                dve.wait_ge(s_const, START + 3)
                with dve.Fori(0, IMG) as b:
                    dve.wait_ge(s_y, START + NH1 * b)
                    norm.vector(dve, b, [X[:, bass.ds(o, HALF)] for o in halves(b)], [v3[:, 0:HROWS], v3[:, HROWS:ROWS]])
                    dve.wait_ge(s_weight, START + 2 * b + 2)
                    dve.wait_ge(s_rank, START + 2 * b)
                    for j in range(TPI):
                        own = weight[:, j * TILE:(j + 1) * TILE]
                        me = wcol[:, j:j + 1]
                        if j:
                            dve.wait_ge(s_diag, START + TPI * b + j)
                        dve.scalar_tensor_tensor(out=diag[:, :], in0=own, scalar=1.0, in1=core.ident[:, :], op0=ALU.mult, op1=ALU.mult, accum_out=me).then_inc(s_diag, 1)
                        dve.wait_ge(s_diag, START + TPI * b + j + 1)
                        if j:
                            dve.tensor_scalar(ahead[:, j, 0:j * TILE], weight[:, 0:j * TILE], me, None, ALU.is_lt)
                        if j + 1 < TPI:
                            dve.tensor_scalar(ahead[:, j, (j + 1) * TILE:PIX], weight[:, (j + 1) * TILE:PIX], me, None, ALU.is_le)
                        dve.scalar_tensor_tensor(out=equal[:, :], in0=own, scalar=me, in1=before[:, :], op0=ALU.is_equal, op1=ALU.mult).then_inc(s_tie, 1)
                        dve.wait_ge(s_tie, START + TPI * b + j + 1)
                        dve.scalar_tensor_tensor(out=ahead[:, j, j * TILE:(j + 1) * TILE], in0=own, scalar=me, in1=equal[:, :], op0=ALU.is_lt, op1=ALU.add).then_inc(s_ahead, 1)
                    for h in range(2):
                        dve.wait_ge(s_rank, START + 2 * b + h + 1)
                        dve.scalar_tensor_tensor(out=coef[:, h * HALF:(h + 1) * HALF], in0=core.bank[4 + h][:, :], scalar=float(CHOSEN), in1=weight[:, h * HALF:(h + 1) * HALF],
                                                 op0=ALU.is_lt, op1=ALU.mult).then_inc(s_coef, 1)
                    for h in range(2):
                        xs = X[:, bass.ds(b * PIX + h * HALF, HALF)]
                        dve.wait_ge(s_y, START + NH1 * b + NHC * (h + 1))
                        dve.wait_ge(s_coef, START + 2 * b + h + 1)
                        dve.scalar_tensor_tensor(out=y[h][:, :], in0=core.bank[4 + h][:, :], scalar=b2[:, 0:1], in1=coef[:, h * HALF:(h + 1) * HALF],
                                                 op0=ALU.add, op1=ALU.mult).then_inc(s_ysum, 1)
                        dve.tensor_tensor(xs, xs, v[:, h * HALF:(h + 1) * HALF], ALU.add).then_inc(s_end, 1)
                        dve.wait_ge(s_ysum, START + 2 * b + h + 1)
                        dve.wait_ge(s_end, START + 2 * b + h + 1)
                        dve.tensor_tensor(xs, xs, y[h][:, :], ALU.add)
        norm.done()


def scan_mixer(core, args):
    nc, norm, X = core.nc, core.norm, core.x
    GROUPS = 4
    GC = COLS // GROUPS
    RL, IL = ROWS + 1, IMG + 1
    PC = ROWS * GC
    PAIRS = IMG // 2
    NW = 5
    LAM, OUT = 1, 3
    with ExitStack() as mem:
        v = core.sb(mem, "ss_v", [C, TOK])
        vg = v[:, :].rearrange("c (i r w) -> c i r w", r=ROWS, w=COLS)
        w_all = core.sb(mem, "ss_w_all", [C, 3 * C])
        wide = core.sb(mem, "ss_w_wide", [C, NW, C])
        bias = core.sb(mem, "ss_bias", [C, NW])
        out_w = core.sb(mem, "ss_out_w", [C, C])
        vecs = core.sb(mem, "ss_vecs", [C, 3])
        by_rows = lambda name: core.sb(mem, name, [C, IMG, GC, RL])
        by_images = lambda name: core.sb(mem, name, [C, ROWS, GC, IL])
        inp = by_rows("ss_inp")
        lam = [by_rows(f"ss_lam{d}") for d in range(2)]
        og = [by_rows(f"ss_out_gate{d}") for d in range(2)]
        feed, fwd, rev = by_rows("ss_feed"), by_rows("ss_fwd"), by_rows("ss_rev")
        lam_i, feed_i, fwd_i, rev_i = (by_images(f"ss_{n}_i") for n in ("lam", "feed", "fwd", "rev"))
        sig = core.sb(mem, "ss_sigmoid", [C, HALF])
        y = core.sb(mem, "ss_y", [C, PIX])
        y3 = y[:, :].rearrange("c (r w) -> c r w", w=COLS)
        flat = lambda t: t[:, :, :, :].rearrange("c a b l -> c (a b l)")
        back = lambda t: flat(t)[:, ::-1]
        (s_par, s_zero, s_wide, s_mm, s_act, s_inp, s_feed, s_feed_i, s_lam_i, s_rows, s_rows_sum, s_images, s_images_sum,
         s_sum, s_prod, s_group, s_affine, s_omm, s_end) = (core.sem(f"ss_{n}") for n in (
            "params", "zero", "wide", "products", "gates", "inp", "feed", "feed_by_images", "lam_by_images", "row_scans", "row_sums",
            "image_scans", "image_sums", "state", "gated", "group", "affine", "out_product", "end"))
        NPAR = 6 + 8
        core.start_counts()
        with nc.Block() as block:
            @block.sync
            def _(sp):
                sp.dma_start(w_all[:, :], args["L2_conv_in_w"]).then_inc(s_par, 16)
                sp.dma_start(out_w[:, :], args["L2_conv_out_w"]).then_inc(s_par, 16)
                for n, name in enumerate(("gamma", "beta", "out_b")):
                    sp.dma_start(vecs[:, n:n + 1], column(args[f"L2_conv_{name}"])).then_inc(s_par, 16)
                in_b = args["L2_conv_in_b"]
                sp.dma_start(bias[:, 0:1], column(in_b[0:C])).then_inc(s_par, 16)
                for d in range(2):
                    for e in range(2):
                        sp.dma_start(bias[e:C:2, OUT + d:OUT + d + 1], column(in_b[C + d:2 * C:2]), allow_slow_non_contiguous=True).then_inc(s_par, 16)
                        sp.dma_start(bias[e:C:2, LAM + d:LAM + d + 1], column(in_b[2 * C + d:3 * C:2]), allow_slow_non_contiguous=True).then_inc(s_par, 16)

            @block.gpsimd
            def _(pool):
                for t in (inp, *lam, *og, feed, fwd, rev, lam_i, feed_i, fwd_i, rev_i):
                    pool.memset(flat(t), 0.0).then_inc(s_zero, 1)
                for q in range(GROUPS):
                    for d in range(2):
                        n = 2 * q + d
                        pool.wait_ge(s_images, START + n)
                        pool.wait_ge(s_act, START + NW * PAIRS * (q + 1))
                        pool.tensor_copy(lam_i[:, :, :, 0:IMG], lam[d][:, :, :, 0:ROWS].rearrange("c i w r -> c r w i")).then_inc(s_lam_i, 1)
                        pool.wait_ge(s_rows, START + n + 1)
                        pool.tensor_tensor(flat(fwd), flat(fwd), flat(rev), ALU.add).then_inc(s_rows_sum, 1)
                        pool.wait_ge(s_images, START + n + 1)
                        pool.tensor_tensor(flat(fwd_i), flat(fwd_i), flat(rev_i), ALU.add).then_inc(s_images_sum, 1)

            @block.tensor
            def _(pe):
                with pe.Fori(0, IMG) as b:
                    norm.tensor(pe, b, [X[:, bass.ds(o, HALF)] for o in halves(b)])
                pe.wait_ge(norm.s_out, START + norm.ready(IMG - 1, 1))
                pe.wait_ge(s_wide, START + NW)
                with pe.Fori(0, GROUPS) as q:
                    for p in range(PAIRS):
                        pe.wait_ge(s_act, START + NW * (PAIRS * q + p))
                        pe.wait_ge(s_inp, START + PAIRS * q + p)
                        for w in range(NW):
                            for i in range(2):
                                mm = pe.matmul(core.bank[w][:, i * PC:(i + 1) * PC].rearrange("c (r w) -> c r w", w=GC), wide[:, w, :],
                                               vg[:, 2 * p + i, :, bass.ds(q * GC, GC)], start=True, stop=True)
                            mm.then_inc(s_mm, 1)
                pe.wait_ge(s_group, START + GROUPS)
                norm.done()
                with pe.Fori(0, IMG) as b:
                    norm.tensor(pe, b, [v[:, bass.ds(o, HALF)] for o in halves(b)])
                    pe.wait_ge(s_end, START + 2 * b)
                    for h in range(2):
                        pe.wait_ge(s_affine, START + 2 * b + h + 1)
                        pe.matmul(core.bank[4 + h][:, :], out_w[:, :], y[:, h * HALF:(h + 1) * HALF], start=True, stop=True).then_inc(s_omm, 1)
                norm.base -= 2 * IMG

            @block.scalar
            def _(act):
                act.preload_act_table_set(LOG_EXP)
                with act.Fori(0, IMG) as b:
                    norm.scalar(act, b, 1e-6)
                act.wait_ge(s_zero, START + 12)
                act.wait_ge(s_par, START + 16 * NPAR)
                act.preload_act_table(ACT.Sigmoid)
                with act.Fori(0, GROUPS) as q:
                    act.wait_ge(s_group, START + q)
                    for p in range(PAIRS):
                        for w in range(NW):
                            m = NW * (PAIRS * q + p) + w
                            act.wait_ge(s_mm, START + m + 1)
                            if w == 0:
                                act.wait_ge(s_inp, START + PAIRS * q + p)
                                act.activation(sig[:, :], core.bank[0][:, :], ACT.Sigmoid, bias=bias[:, 0:1]).then_inc(s_act, 1)
                                continue
                            dst = (*lam, *og)[w - 1][:, 2 * p:2 * p + 2, :, 0:ROWS]
                            act.activation(dst, core.bank[w][:, :].rearrange("c (i r w) -> c i w r", i=2, w=GC), ACT.Sigmoid, bias=bias[:, w:w + 1]).then_inc(s_act, 1)
                    for d in range(2):
                        act.wait_ge(s_images, START + 2 * q + d)
                        act.wait_ge(s_feed, START + 2 * q + d + 1)
                        act.activation(feed_i[:, :, :, 0:IMG], feed[:, :, :, 0:ROWS].rearrange("c i w r -> c r w i"), ACT.Copy).then_inc(s_feed_i, 1)
                norm.done()
                act.preload_act_table_set(LOG_EXP)
                with act.Fori(0, IMG) as b:
                    norm.scalar(act, b, 1e-5)
                    for h in range(2):
                        half = y[:, h * HALF:(h + 1) * HALF]
                        act.wait_ge(norm.s_out, START + norm.ready(b, h))
                        act.activation(half, half, ACT.Identity, bias=vecs[:, 1:2], scale=vecs[:, 0:1]).then_inc(s_affine, 1)
                norm.base -= 2 * IMG

            @block.vector
            def _(dve):
                dve.wait_ge(s_par, START + 16 * NPAR)
                dve.tensor_copy(wide[:, 0, :], w_all[:, 0:C]).then_inc(s_wide, 1)
                for d in range(2):
                    for w, at in ((LAM + d, 2 * C + d), (OUT + d, C + d)):
                        src = w_all[:, at:at - d + C:2].rearrange("c (n e) -> c n e", e=1).broadcast_to([C, C // 2, 2])
                        dve.tensor_copy(wide[:, w, :].rearrange("c (n e) -> c n e", e=2), src).then_inc(s_wide, 1)
                with dve.Fori(0, IMG) as b:
                    norm.vector(dve, b, [X[:, bass.ds(o, HALF)] for o in halves(b)],
                                [v[:, bass.ds(o, HALF)].rearrange("c (r w) -> c r w", w=COLS) for o in halves(b)])
                dve.wait_ge(s_zero, START + 12)
                with dve.Fori(0, GROUPS) as q:
                    for p in range(PAIRS):
                        dve.wait_ge(s_act, START + NW * (PAIRS * q + p) + 1)
                        for i in range(2):
                            at = slice(i * PC, (i + 1) * PC)
                            ins = dve.scalar_tensor_tensor(out=inp[:, 2 * p + i, :, 0:ROWS].rearrange("c w r -> c r w"),
                                                           in0=core.bank[0][:, at].rearrange("c (r w) -> c r w", w=GC), scalar=bias[:, 0:1],
                                                           in1=sig[:, at].rearrange("c (r w) -> c r w", w=GC), op0=ALU.add, op1=ALU.mult)
                        ins.then_inc(s_inp, 1)
                    dve.wait_ge(s_inp, START + PAIRS * (q + 1))
                    dve.wait_ge(s_act, START + NW * PAIRS * (q + 1))
                    for d in range(2):
                        n = 2 * q + d
                        dve.wait_ge(s_feed_i, START + n)
                        dve.scalar_tensor_tensor(out=flat(feed), in0=flat(lam[d]), scalar=1.0, in1=flat(inp), op0=ALU.subtract, op1=ALU.mult).then_inc(s_feed, 1)
                        dve.wait_ge(s_feed, START + n + 1)
                        dve.wait_ge(s_prod, START + n)
                        dve.tensor_tensor_scan(flat(fwd), flat(lam[d]), flat(feed), 0.0, ALU.mult, ALU.subtract)
                        dve.tensor_tensor_scan(back(rev), back(lam[d]), back(feed), 0.0, ALU.mult, ALU.subtract).then_inc(s_rows, 1)
                        dve.wait_ge(s_feed_i, START + n + 1)
                        dve.wait_ge(s_lam_i, START + n + 1)
                        dve.tensor_tensor_scan(flat(fwd_i), flat(lam_i), flat(feed_i), 0.0, ALU.mult, ALU.subtract)
                        dve.tensor_tensor_scan(back(rev_i), back(lam_i), back(feed_i), 0.0, ALU.mult, ALU.subtract).then_inc(s_images, 1)
                        dve.wait_ge(s_rows_sum, START + n + 1)
                        dve.wait_ge(s_images_sum, START + n + 1)
                        state = fwd[:, :, :, 0:ROWS]
                        dve.tensor_tensor(state, state, fwd_i[:, :, :, 0:IMG].rearrange("c r w i -> c i w r"), ALU.add).then_inc(s_sum, 1)
                        dve.wait_ge(s_sum, START + n + 1)
                        dve.tensor_tensor(flat(og[d]), flat(og[d]), flat(fwd), ALU.mult).then_inc(s_prod, 1)
                    dve.wait_ge(s_prod, START + 2 * q + 2)
                    dve.tensor_tensor(vg[:, :, :, bass.ds(q * GC, GC)].rearrange("c i r w -> c i w r"), og[0][:, :, :, 0:ROWS], og[1][:, :, :, 0:ROWS], ALU.add).then_inc(s_group, 1)
                dve.wait_ge(s_group, START + GROUPS)
                norm.done()
                with dve.Fori(0, IMG) as b:
                    dve.wait_ge(s_omm, START + 2 * b)
                    norm.vector(dve, b, [v[:, bass.ds(o, HALF)] for o in halves(b)], [y3[:, 0:HROWS], y3[:, HROWS:ROWS]])
                    for h in range(2):
                        xs = X[:, bass.ds(b * PIX + h * HALF, HALF)]
                        dve.wait_ge(s_omm, START + 2 * b + h + 1)
                        dve.scalar_tensor_tensor(out=xs, in0=core.bank[4 + h][:, :], scalar=vecs[:, 2:3], in1=xs, op0=ALU.add, op1=ALU.add).then_inc(s_end, 1)
                norm.base -= 2 * IMG
        norm.done(2)


class Router:

    def __init__(self, core, mem, name, gate_w, gate_b):
        self.core, self.E = core, gate_w.shape[1]
        self.gate_w, self.gate_b = gate_w, gate_b
        E, self.TILES = self.E, TOK // TILE
        self.w = core.sb(mem, f"{name}_gate_w", [C, C])
        self.b = core.sb(mem, f"{name}_gate_b", [C, 1])
        self.turn = [core.sb(mem, f"{name}_logits_t{h}", [C, HALF]) for h in range(2)]
        self.p = core.sb(mem, f"{name}_probs", [TILE, self.TILES * E])
        self.q = core.sb(mem, f"{name}_scratch", [TILE, self.TILES * E])
        self.hot = core.sb(mem, f"{name}_hot", [TILE, self.TILES * E])
        self.weights = core.sb(mem, f"{name}_weights", [TILE, self.TILES * E])
        self.order = core.sb(mem, f"{name}_order", [TILE, E])
        self.top = core.sb(mem, f"{name}_top", [TILE, self.TILES])
        (self.s_par, self.s_mm, self.s_t, self.s_tt, self.s_logit, self.s_step, self.s_exp, self.s_order, self.s_zero) = (
            core.sem(f"{name}_route_{n}") for n in ("params", "product", "biased", "turned", "logits", "steps", "exp", "order", "zero"))

    def load(self, sp):
        sp.wait_ge(self.s_zero, START + 2)
        sp.dma_start(self.w[:, 0:self.E], self.gate_w).then_inc(self.s_par, 16)
        sp.dma_start(self.b[0:self.E, :], column(self.gate_b)).then_inc(self.s_par, 16)

    def gpsimd(self, pool):
        pool.memset(self.w[:, :], 0.0).then_inc(self.s_zero, 1)
        pool.memset(self.b[:, :], 0.0).then_inc(self.s_zero, 1)
        for e in range(self.E):
            pool.memset(self.order[:, e:e + 1], float(self.E - e)).then_inc(self.s_order, 1)

    def tensor(self, pe, b, src):
        for h in range(2):
            pe.wait_ge(self.s_t, START + 2 * b)
            pe.matmul(self.core.bank[4 + h][:, :], self.w[:, :], src[h], start=True, stop=True).then_inc(self.s_mm, 1)
        pe.wait_ge(self.s_logit, START + 2 * b)
        for h in range(2):
            pe.wait_ge(self.s_t, START + 2 * b + h + 1)
            for j in range(4):
                mm = pe.transpose(self.core.bank[6 + h][:, j * TILE:(j + 1) * TILE], self.turn[h][:, j * TILE:(j + 1) * TILE], self.core.ident[:, :])
            mm.then_inc(self.s_tt, 1)

    def scalar(self, act, b):
        for h in range(2):
            act.wait_ge(self.s_tt, START + 2 * b)
            act.wait_ge(self.s_mm, START + 2 * b + h + 1)
            act.activation(self.turn[h][:, :], self.core.bank[4 + h][:, :], ACT.Identity, bias=self.b[:, 0:1]).then_inc(self.s_t, 1)

    def vector(self, dve, b):
        for h in range(2):
            dve.wait_ge(self.s_tt, START + 2 * b + h + 1)
            turned = self.core.bank[6 + h][:, :].rearrange("p (t e) -> p t e", e=TILE)[:, :, 0:self.E]
            dve.tensor_copy(self.p[:, bass.ds((2 * b + h) * (4 * self.E), 4 * self.E)].rearrange("p (t e) -> p t e", e=self.E), turned).then_inc(self.s_logit, 1)

    def choose_scalar(self, act):
        act.wait_ge(self.s_step, START + 2)
        act.activation(self.p[:, :], self.p[:, :], ACT.Exp).then_inc(self.s_exp, 1)

    def choose_vector(self, dve):
        E, T, s = self.E, self.TILES, self.s_step
        by = lambda t: t[:, :].rearrange("p (t e) -> p t e", e=E)
        p, q, hot, out = (by(t) for t in (self.p, self.q, self.hot, self.weights))
        top = self.top[:, :]
        wide = top.rearrange("p (t e) -> p t e", e=1).broadcast_to([TILE, T, E])
        order = self.order[:, :].rearrange("p (t e) -> p t e", t=1).broadcast_to([TILE, T, E])
        dve.wait_ge(self.s_order, START + E)
        dve.wait_ge(self.s_logit, START + 2 * IMG)
        dve.tensor_reduce(top, p, AX.X, ALU.max).then_inc(s, 1)
        dve.wait_ge(s, START + 1)
        dve.tensor_tensor(p, p, wide, ALU.subtract).then_inc(s, 1)
        dve.wait_ge(self.s_exp, START + 1)
        dve.tensor_reduce(top, p, AX.X, ALU.add).then_inc(s, 1)
        dve.wait_ge(s, START + 3)
        dve.reciprocal(top, top).then_inc(s, 1)
        dve.wait_ge(s, START + 4)
        dve.tensor_tensor(p, p, wide, ALU.mult).then_inc(s, 1)
        n = 5
        for k, src in enumerate((p, q)):
            dve.wait_ge(s, START + n)
            dve.tensor_reduce(top, src, AX.X, ALU.max).then_inc(s, 1)
            dve.wait_ge(s, START + n + 1)
            dve.tensor_tensor(hot, src, wide, ALU.is_equal).then_inc(s, 1)
            dve.wait_ge(s, START + n + 2)
            dve.tensor_tensor(hot, hot, order, ALU.mult).then_inc(s, 1)
            dve.wait_ge(s, START + n + 3)
            dve.tensor_reduce(top, hot, AX.X, ALU.max).then_inc(s, 1)
            dve.wait_ge(s, START + n + 4)
            dve.tensor_tensor(hot, hot, wide, ALU.is_equal).then_inc(s, 1)
            dve.wait_ge(s, START + n + 5)
            n += 6
            if k == 0:
                dve.scalar_tensor_tensor(out=q, in0=hot, scalar=-2.0, in1=p, op0=ALU.mult, op1=ALU.add).then_inc(s, 1)
                dve.tensor_tensor(out, hot, p, ALU.mult).then_inc(s, 1)
                n += 1
            else:
                dve.tensor_tensor(hot, hot, p, ALU.mult).then_inc(s, 1)
        dve.wait_ge(s, START + n)
        dve.tensor_tensor(out, out, hot, ALU.add).then_inc(s, 1)
        dve.wait_ge(s, START + n + 1)
        dve.tensor_reduce(top, out, AX.X, ALU.add).then_inc(s, 1)
        dve.wait_ge(s, START + n + 2)
        dve.reciprocal(top, top).then_inc(s, 1)
        dve.wait_ge(s, START + n + 3)
        dve.tensor_tensor(out, out, wide, ALU.mult).then_inc(s, 1)
        dve.wait_ge(s, START + n + 4)

    def weight(self, tile, e):
        return self.weights[:, bass.ds(tile * self.E + e, 1)]


class Turner:

    def __init__(self, core, mem, name, acc):
        self.core, self.acc = core, acc
        self.stage = [core.sb(mem, f"{name}_turn{h}", [TILE, HALF]) for h in range(2)]
        self.s_stage, self.s_turn, self.s_end = (core.sem(f"{name}_turn_{n}") for n in ("staged", "turned", "added"))

    def scalar(self, act):
        with act.Fori(0, IMG) as b:
            act.wait_ge(self.s_turn, START + 2 * b)
            for h in range(2):
                act.activation(self.stage[h][:, :], self.acc[:, bass.ds(b * PIX + h * HALF, HALF)], ACT.Copy).then_inc(self.s_stage, 1)

    def tensor(self, pe):
        with pe.Fori(0, IMG) as b:
            pe.wait_ge(self.s_end, START + 2 * b)
            for h in range(2):
                pe.wait_ge(self.s_stage, START + 2 * b + h + 1)
                for j in range(4):
                    mm = pe.transpose(self.core.bank[h][:, j * TILE:(j + 1) * TILE], self.stage[h][:, j * TILE:(j + 1) * TILE], self.core.ident[:, :])
                mm.then_inc(self.s_turn, 1)

    def vector(self, dve):
        with dve.Fori(0, IMG) as b:
            for h in range(2):
                xs = self.core.x[:, bass.ds(b * PIX + h * HALF, HALF)]
                dve.wait_ge(self.s_turn, START + 2 * b + h + 1)
                dve.tensor_tensor(xs, xs, self.core.bank[h][:, :], ALU.add).then_inc(self.s_end, 1)


def experts_ffn(core, args):
    nc, norm, X = core.nc, core.norm, core.x
    E, _, HID = args["L2_ffn_w1"].shape
    K = HID // C
    N = HALF // K
    STEPS = TOK // N
    T = N // TILE
    w1_e, w2_e = args["L2_ffn_w1"], args["L2_ffn_w2"]
    w3_e = args["L2_ffn_w3"].rearrange("e (k p) d -> e p k d", p=C)
    with ExitStack() as mem:
        router = Router(core, mem, "ex", args["L2_ffn_gate_w"], args["L2_ffn_gate_b"])
        v = core.sb(mem, "ex_v", [C, TOK])
        acc = core.sb(mem, "ex_acc", [TILE, TOK])
        turner = Turner(core, mem, "ex", acc)
        w1 = [core.sb(mem, f"ex_w1_{k}", [C, HID]) for k in range(2)]
        w2 = [core.sb(mem, f"ex_w2_{k}", [C, HID]) for k in range(2)]
        w3 = [core.sb(mem, f"ex_w3_{k}", [C, K, C]) for k in range(2)]
        act_h = [core.sb(mem, f"ex_silu{k}", [C, HALF]) for k in range(2)]
        hid = [core.sb(mem, f"ex_hidden{k}", [C, HALF]) for k in range(2)]
        s_w = [core.sem(f"ex_weights{k}") for k in range(2)]
        s_zero, s_h, s_silu, s_hid, s_o, s_sum = (core.sem(f"ex_{n}") for n in ("zero", "products", "silu", "hidden", "outputs", "summed"))
        gate, up, outs = core.bank[0:2], core.bank[2:4], core.bank[4:6]
        core.start_counts()
        with nc.Block() as block:
            @block.sync
            def _(sp):
                router.load(sp)

                def load(e, k):
                    sp.dma_start(w1[k][:, :], w1_e[e] if isinstance(e, int) else w1_e[bass.ds(e, 1)].rearrange("o c h -> c (o h)")).then_inc(s_w[k], 16)
                    sp.dma_start(w2[k][:, :], w2_e[e] if isinstance(e, int) else w2_e[bass.ds(e, 1)].rearrange("o c h -> c (o h)")).then_inc(s_w[k], 16)
                    sp.dma_start(w3[k][:, :, :], w3_e[e] if isinstance(e, int) else w3_e[bass.ds(e, 1)].rearrange("o p k d -> p (o k) d")).then_inc(s_w[k], 16)

                load(0, 0)
                load(1, 1)
                with sp.Fori(0, E // 2 - 1) as q:
                    for k in range(2):
                        sp.wait_ge(s_o, START + (2 * q + k + 1) * STEPS)
                        load(2 * q + 2 + k, k)

            @block.gpsimd
            def _(pool):
                router.gpsimd(pool)
                pool.memset(acc[:, :], 0.0).then_inc(s_zero, 1)

            @block.tensor
            def _(pe):
                pe.wait_ge(router.s_par, START + 32)
                with pe.Fori(0, IMG) as b:
                    norm.tensor(pe, b, [X[:, bass.ds(o, HALF)] for o in halves(b)])
                    for h in range(2):
                        pe.wait_ge(norm.s_out, START + norm.ready(b, h))
                    router.tensor(pe, b, [v[:, bass.ds(o, HALF)] for o in halves(b)])
                pe.wait_ge(router.s_logit, START + 2 * IMG)

                def hidden(e, j, r, k, free):
                    pe.wait_ge(s_hid, START + e * STEPS + free)
                    rhs = v[:, bass.ds(j * N, N)] if not isinstance(j, int) else v[:, j * N:(j + 1) * N]
                    for w, bank in ((w1[k], gate[r]), (w2[k], up[r])):
                        for c in range(K):
                            mm = pe.matmul(bank[:, c * N:(c + 1) * N], w[:, c * C:(c + 1) * C], rhs, start=True, stop=True)
                    mm.then_inc(s_h, 1)

                def output(e, j, r, k, free):
                    pe.wait_ge(s_sum, START + e * STEPS + free)
                    pe.wait_ge(s_hid, START + e * STEPS + j + 1)
                    for t in range(T):
                        for c in range(K):
                            mm = pe.matmul(outs[r][:, t * C:(t + 1) * C], hid[r][:, c * N + t * TILE:c * N + (t + 1) * TILE], w3[k][:, c, :],
                                           start=(c == 0), stop=(c == K - 1))
                    mm.then_inc(s_o, 1)

                with pe.Fori(0, E // 2) as q:
                    for k in range(2):
                        e = 2 * q + k
                        pe.wait_ge(s_w[k], START + 48 * q + 48)
                        hidden(e, 0, 0, k, 0)
                        with pe.Fori(0, STEPS // 2 - 1) as p:
                            hidden(e, 2 * p + 1, 1, k, 2 * p)
                            output(e, 2 * p, 0, k, 2 * p)
                            hidden(e, 2 * p + 2, 0, k, 2 * p + 1)
                            output(e, 2 * p + 1, 1, k, 2 * p)
                        hidden(e, STEPS - 1, 1, k, STEPS - 2)
                        output(e, STEPS - 2, 0, k, STEPS - 2)
                        output(e, STEPS - 1, 1, k, STEPS - 2)
                pe.wait_ge(s_sum, START + E * STEPS)
                turner.tensor(pe)

            @block.scalar
            def _(act):
                act.wait_ge(router.s_par, START + 32)
                act.preload_act_table_set(LOG_EXP)
                with act.Fori(0, IMG) as b:
                    norm.scalar(act, b, 1e-5)
                    router.scalar(act, b)
                router.choose_scalar(act)
                act.preload_act_table(ACT.Silu)
                with act.Fori(0, E * STEPS // 2) as p:
                    for r in range(2):
                        n = 2 * p + r
                        act.wait_ge(s_h, START + n + 1)
                        act.activation(act_h[r][:, :], gate[r][:, :], ACT.Silu).then_inc(s_silu, 1)
                act.wait_ge(s_sum, START + E * STEPS)
                turner.scalar(act)

            @block.vector
            def _(dve):
                with dve.Fori(0, IMG) as b:
                    norm.vector(dve, b, [X[:, bass.ds(o, HALF)] for o in halves(b)],
                                [v[:, bass.ds(o, HALF)].rearrange("c (r w) -> c r w", w=COLS) for o in halves(b)])
                    router.vector(dve, b)
                router.choose_vector(dve)
                dve.wait_ge(s_zero, START + 1)

                def gated(e, j, r):
                    n = e * STEPS + j
                    dve.wait_ge(s_silu, START + n + 1)
                    dve.tensor_tensor(hid[r][:, :], act_h[r][:, :], up[r][:, :], ALU.mult).then_inc(s_hid, 1)

                def add(e, j, r):
                    dve.wait_ge(s_o, START + e * STEPS + j + 1)
                    for t in range(T):
                        at = acc[:, bass.ds((j * T + t) * C, C)]
                        ins = dve.scalar_tensor_tensor(out=at, in0=outs[r][:, t * C:(t + 1) * C], scalar=router.weight(j * T + t, e), in1=at,
                                                       op0=ALU.mult, op1=ALU.add)
                    ins.then_inc(s_sum, 1)

                with dve.Fori(0, E) as e:
                    dve.wait_ge(s_sum, START + e * STEPS)
                    gated(e, 0, 0)
                    with dve.Fori(0, STEPS // 2 - 1) as p:
                        gated(e, 2 * p + 1, 1)
                        add(e, 2 * p, 0)
                        gated(e, 2 * p + 2, 0)
                        add(e, 2 * p + 1, 1)
                    gated(e, STEPS - 1, 1)
                    add(e, STEPS - 2, 0)
                    add(e, STEPS - 1, 1)
                turner.vector(dve)
        norm.done()


def sign_conv_mixer(core, args):
    nc, norm, X = core.nc, core.norm, core.x
    TAPS = 9
    with ExitStack() as mem:
        v = [core.sb(mem, f"sc_v{k}", [C, PAD, PAD]) for k in range(2)]
        w = core.sb(mem, "sc_w", [C, TAPS, C])
        pruning = core.sb(mem, "sc_pruning", [C, TAPS, C])
        signs = core.sb(mem, "sc_signs", [C, TAPS, C])
        size = core.sb(mem, "sc_size", [C, TAPS, C])
        clipped = core.sb(mem, "sc_clipped", [C, TAPS, C])
        total = core.sb(mem, "sc_total", [C, C])
        scale = core.sb(mem, "sc_scale", [C, C])
        (s_par, s_zero, s_act, s_w, s_tot, s_conv, s_end) = (
            core.sem(f"sc_{n}") for n in ("params", "zero", "signs", "weights", "scale", "convolved", "end"))
        core.start_counts()
        with nc.Block() as block:
            @block.sync
            def _(sp):
                sp.dma_start(w[:, :, :], args["L3_conv_w"].rearrange("a b i o -> i (a b) o")).then_inc(s_par, 16)
                sp.dma_start(pruning[:, :, :], args["L3_conv_pruning_mask"].rearrange("(t i) o -> i t o", i=C)).then_inc(s_par, 16)

            @block.gpsimd
            def _(pool):
                for k in range(2):
                    pool.memset(v[k][:, :, :], 0.0).then_inc(s_zero, 1)

            @block.tensor
            def _(pe):
                pe.wait_ge(s_w, START + 1)
                pe.matmul(core.bank[4][:, 0:C], core.mean_w[:, :], total[:, :], start=True, stop=True).then_inc(s_tot, 1)
                pe.wait_ge(s_w, START + 7)
                with pe.Fori(0, IMG // 2) as p:
                    for k in range(2):
                        b = 2 * p + k
                        norm.tensor(pe, b, [X[:, bass.ds(p * (2 * PIX) + (k * PIX + h * HALF), HALF)] for h in range(2)])
                        for h in range(2):
                            pe.wait_ge(norm.s_out, START + norm.ready(b, 1))
                            pe.wait_ge(s_end, START + 4 * p)
                            bank = core.bank[4 + 2 * k + h]
                            for t in range(TAPS):
                                mm = pe.matmul(image(bank), w[:, t, :], window(v[k], h, t), start=(t == 0), stop=(t == TAPS - 1))
                            mm.then_inc(s_conv, 1)

            @block.scalar
            def _(act):
                act.wait_ge(s_par, START + 32)
                act.activation(size[:, :, :], w[:, :, :], ACT.Abs).then_inc(s_act, 1)
                act.activation(signs[:, :, :], w[:, :, :], ACT.Sign).then_inc(s_act, 1)
                act.wait_ge(s_zero, START + 2)
                act.preload_act_table_set(LOG_EXP)
                with act.Fori(0, IMG) as b:
                    norm.scalar(act, b, 1e-6)

            @block.vector
            def _(dve):
                dve.wait_ge(s_act, START + 2)
                dve.tensor_reduce(total[:, :], size[:, :, :].rearrange("i t o -> i o t"), AX.X, ALU.add).then_inc(s_w, 1)
                dve.wait_ge(s_tot, START + 1)
                dve.tensor_scalar(scale[:, :], core.bank[4][:, 0:C], 1.0 / TAPS, None, ALU.mult).then_inc(s_w, 1)
                dve.tensor_scalar(clipped[:, :, :], w[:, :, :], -1.0, 1.0, ALU.max, ALU.min).then_inc(s_w, 1)
                dve.wait_ge(s_w, START + 3)
                dve.tensor_tensor(w[:, :, :], signs[:, :, :], scale[:, :].rearrange("i (t o) -> i t o", t=1).broadcast_to([C, TAPS, C]), ALU.mult).then_inc(s_w, 1)
                dve.wait_ge(s_w, START + 4)
                dve.tensor_tensor(w[:, :, :], w[:, :, :], clipped[:, :, :], ALU.subtract).then_inc(s_w, 1)
                dve.wait_ge(s_w, START + 5)
                dve.tensor_tensor(w[:, :, :], w[:, :, :], clipped[:, :, :], ALU.add).then_inc(s_w, 1)
                dve.wait_ge(s_w, START + 6)
                dve.tensor_tensor(w[:, :, :], w[:, :, :], pruning[:, :, :], ALU.mult).then_inc(s_w, 1)
                dve.wait_ge(s_zero, START + 2)
                norm.vector(dve, 0, [X[:, 0:HALF], X[:, HALF:PIX]], [inner(v[0], 0), inner(v[0], 1)])

                def finish(p, k):
                    for h in range(2):
                        xs = X[:, bass.ds(p * (2 * PIX) + (k * PIX + h * HALF), HALF)]
                        dve.wait_ge(s_conv, START + 4 * p + 2 * k + h + 1)
                        dve.tensor_tensor(xs, xs, core.bank[4 + 2 * k + h][:, :], ALU.add).then_inc(s_end, 1)

                with dve.Fori(0, IMG // 2 - 1) as p:
                    for k in range(2):
                        dve.wait_ge(s_conv, START + 4 * p + 2 * k)
                        norm.vector(dve, 2 * p + k + 1, [X[:, bass.ds(p * (2 * PIX) + ((k + 1) * PIX + h * HALF), HALF)] for h in range(2)],
                                    [inner(v[1 - k], 0), inner(v[1 - k], 1)])
                        finish(p, k)
                p = IMG // 2 - 1
                dve.wait_ge(s_conv, START + 4 * p)
                norm.vector(dve, 2 * p + 1, [X[:, 2 * p * PIX + PIX + h * HALF:2 * p * PIX + PIX + (h + 1) * HALF] for h in range(2)],
                            [inner(v[1], 0), inner(v[1], 1)])
                finish(p, 0)
                finish(p, 1)
        norm.done()


def normed_experts_ffn(core, args):
    nc, norm, X = core.nc, core.norm, core.x
    E, _, HID = args["L3_ffn_W1"].shape
    K = HID // C
    N = 2 * HALF // K
    STEPS = TOK // N
    T = N // TILE
    KB = K // 2
    w2_e = args["L3_ffn_W2"].rearrange("e (k p) d -> e p k d", p=C)
    with ExitStack() as mem:
        router = Router(core, mem, "nx", args["L3_ffn_Wr"], args["L3_ffn_br"])
        v = core.sb(mem, "nx_v", [C, PIX])
        v3 = v[:, :].rearrange("c (r w) -> c r w", w=COLS)
        u = core.sb(mem, "nx_u", [C, TOK])
        acc = core.sb(mem, "nx_acc", [TILE, TOK])
        turner = Turner(core, mem, "nx", acc)
        w1 = [core.sb(mem, f"nx_w1_{k}", [C, HID]) for k in range(2)]
        w2 = [core.sb(mem, f"nx_w2_{k}", [C, K, C]) for k in range(2)]
        b1 = [core.sb(mem, f"nx_b1_{k}", [C, K]) for k in range(2)]
        b2 = [core.sb(mem, f"nx_b2_{k}", [1, C]) for k in range(2)]
        gain = [core.sb(mem, f"nx_gain{k}", [C, 2]) for k in range(2)]
        ones = core.sb(mem, "nx_ones", [1, TILE])
        xe = [core.sb(mem, f"nx_scaled{r}", [C, N]) for r in range(2)]
        hid = [core.sb(mem, f"nx_hidden{r}", [C, K * N]) for r in range(2)]
        s_w = [core.sem(f"nx_weights{k}") for k in range(2)]
        s_zero, s_xe, s_h, s_hid, s_o, s_sum = (core.sem(f"nx_{n}") for n in ("zero", "scaled", "products", "hidden", "outputs", "summed"))
        pre = [core.bank[0:2], core.bank[2:4]]
        outs = core.bank[4:6]
        NDMA = 6
        core.start_counts()
        with nc.Block() as block:
            @block.sync
            def _(sp):
                router.load(sp)

                def row(a, e):
                    return a[e:e + 1] if isinstance(e, int) else a[bass.ds(e, 1)]

                def load(e, k):
                    sp.dma_start(w1[k][:, :], row(args["L3_ffn_W1"], e).rearrange("o c h -> c (o h)")).then_inc(s_w[k], 16)
                    sp.dma_start(w2[k][:, :, :], row(w2_e, e).rearrange("o p k d -> p (o k) d")).then_inc(s_w[k], 16)
                    sp.dma_start(b1[k][:, :], row(args["L3_ffn_b1"], e).rearrange("o (k p) -> p (o k)", p=C), allow_slow_non_contiguous=True).then_inc(s_w[k], 16)
                    sp.dma_start(b2[k][:, :], row(args["L3_ffn_b2"], e)).then_inc(s_w[k], 16)
                    for n, name in enumerate(("g", "b")):
                        sp.dma_start(gain[k][:, n:n + 1], row(args[f"L3_ffn_ln_{name}"], e).rearrange("o c -> c o"), allow_slow_non_contiguous=True).then_inc(s_w[k], 16)

                load(0, 0)
                load(1, 1)
                with sp.Fori(0, E // 2 - 1) as q:
                    for k in range(2):
                        sp.wait_ge(s_o, START + (2 * q + k + 1) * STEPS)
                        load(2 * q + 2 + k, k)

            @block.gpsimd
            def _(pool):
                router.gpsimd(pool)
                pool.memset(ones[:, :], 1.0).then_inc(s_zero, 1)
                pool.memset(acc[:, :], 0.0).then_inc(s_zero, 1)

            @block.tensor
            def _(pe):
                pe.wait_ge(router.s_par, START + 32)
                with pe.Fori(0, IMG) as b:
                    norm.tensor(pe, 2 * b, [X[:, bass.ds(o, HALF)] for o in halves(b)])
                    for h in range(2):
                        pe.wait_ge(norm.s_out, START + norm.ready(2 * b, h))
                    router.tensor(pe, b, [v[:, h * HALF:(h + 1) * HALF] for h in range(2)])
                    norm.tensor(pe, 2 * b + 1, [v[:, h * HALF:(h + 1) * HALF] for h in range(2)])
                pe.wait_ge(router.s_logit, START + 2 * IMG)
                pe.wait_ge(norm.s_out, START + norm.ready(2 * IMG - 1, 1))
                pe.wait_ge(s_zero, START + 2)

                def hidden(e, j, r, k, free):
                    pe.wait_ge(s_hid, START + e * STEPS + free)
                    pe.wait_ge(s_xe, START + e * STEPS + j + 1)
                    for c in range(K):
                        mm = pe.matmul(pre[r][c // KB][:, c % KB * N:(c % KB + 1) * N], w1[k][:, c * C:(c + 1) * C], xe[r][:, :], start=True, stop=True)
                    mm.then_inc(s_h, 1)

                def output(e, j, r, k, free):
                    pe.wait_ge(s_sum, START + e * STEPS + free)
                    pe.wait_ge(s_hid, START + e * STEPS + j + 1)
                    for t in range(T):
                        out = outs[r][:, t * C:(t + 1) * C]
                        pe.matmul(out, ones[:, :], b2[k][:, :], start=True, stop=False)
                        for c in range(K):
                            mm = pe.matmul(out, hid[r][:, c * N + t * TILE:c * N + (t + 1) * TILE], w2[k][:, c, :], start=False, stop=(c == K - 1))
                    mm.then_inc(s_o, 1)

                with pe.Fori(0, E // 2) as q:
                    for k in range(2):
                        e = 2 * q + k
                        pe.wait_ge(s_w[k], START + 16 * NDMA * (q + 1))
                        hidden(e, 0, 0, k, 0)
                        with pe.Fori(0, STEPS // 2 - 1) as p:
                            hidden(e, 2 * p + 1, 1, k, 2 * p)
                            output(e, 2 * p, 0, k, 2 * p)
                            hidden(e, 2 * p + 2, 0, k, 2 * p + 1)
                            output(e, 2 * p + 1, 1, k, 2 * p)
                        hidden(e, STEPS - 1, 1, k, STEPS - 2)
                        output(e, STEPS - 2, 0, k, STEPS - 2)
                        output(e, STEPS - 1, 1, k, STEPS - 2)
                pe.wait_ge(s_sum, START + E * STEPS)
                turner.tensor(pe)

            @block.scalar
            def _(act):
                act.wait_ge(router.s_par, START + 32)
                act.preload_act_table_set(LOG_EXP)
                with act.Fori(0, IMG) as b:
                    norm.scalar(act, 2 * b, 1e-5)
                    router.scalar(act, b)
                    norm.scalar(act, 2 * b + 1, 1e-5)
                router.choose_scalar(act)
                act.preload_act_table(ACT.Gelu)

                def gelu(e, j, r, k, free):
                    act.wait_ge(s_h, START + e * STEPS + j + 1)
                    act.wait_ge(s_o, START + e * STEPS + free)
                    for c in range(K):
                        ins = act.activation(hid[r][:, c * N:(c + 1) * N], pre[r][c // KB][:, c % KB * N:(c % KB + 1) * N], ACT.Gelu, bias=b1[k][:, c:c + 1])
                    ins.then_inc(s_hid, 1)

                with act.Fori(0, E // 2) as q:
                    for k in range(2):
                        e = 2 * q + k
                        act.wait_ge(s_w[k], START + 16 * NDMA * (q + 1))
                        gelu(e, 0, 0, k, 0)
                        with act.Fori(0, STEPS // 2 - 1) as p:
                            gelu(e, 2 * p + 1, 1, k, 2 * p)
                            gelu(e, 2 * p + 2, 0, k, 2 * p + 1)
                        gelu(e, STEPS - 1, 1, k, STEPS - 2)
                act.wait_ge(s_sum, START + E * STEPS)
                turner.scalar(act)

            @block.vector
            def _(dve):
                with dve.Fori(0, IMG) as b:
                    norm.vector(dve, 2 * b, [X[:, bass.ds(o, HALF)] for o in halves(b)], [v3[:, 0:HROWS], v3[:, HROWS:ROWS]])
                    router.vector(dve, b)
                    dve.wait_ge(norm.s_out, START + norm.ready(2 * b, 1))
                    norm.vector(dve, 2 * b + 1, [v[:, h * HALF:(h + 1) * HALF] for h in range(2)],
                                [u[:, bass.ds(o, HALF)].rearrange("c (r w) -> c r w", w=COLS) for o in halves(b)])
                router.choose_vector(dve)
                dve.wait_ge(s_zero, START + 2)
                dve.wait_ge(norm.s_out, START + norm.ready(2 * IMG - 1, 1))

                def scaled(e, j, r, k):
                    src = u[:, bass.ds(j * N, N)] if not isinstance(j, int) else u[:, j * N:(j + 1) * N]
                    dve.tensor_scalar(xe[r][:, :], src, gain[k][:, 0:1], gain[k][:, 1:2], ALU.mult, ALU.add).then_inc(s_xe, 1)

                def add(e, j, r):
                    dve.wait_ge(s_o, START + e * STEPS + j + 1)
                    for t in range(T):
                        at = acc[:, bass.ds((j * T + t) * C, C)]
                        ins = dve.scalar_tensor_tensor(out=at, in0=outs[r][:, t * C:(t + 1) * C], scalar=router.weight(j * T + t, e), in1=at,
                                                       op0=ALU.mult, op1=ALU.add)
                    ins.then_inc(s_sum, 1)

                with dve.Fori(0, E // 2) as q:
                    for k in range(2):
                        e = 2 * q + k
                        dve.wait_ge(s_w[k], START + 16 * NDMA * (q + 1))
                        dve.wait_ge(s_sum, START + e * STEPS)
                        scaled(e, 0, 0, k)
                        scaled(e, 1, 1, k)
                        with dve.Fori(0, STEPS // 2 - 1) as p:
                            dve.wait_ge(s_h, START + e * STEPS + 2 * p + 1)
                            scaled(e, 2 * p + 2, 0, k)
                            add(e, 2 * p, 0)
                            dve.wait_ge(s_h, START + e * STEPS + 2 * p + 2)
                            scaled(e, 2 * p + 3, 1, k)
                            add(e, 2 * p + 1, 1)
                        add(e, STEPS - 2, 0)
                        add(e, STEPS - 1, 1)
                turner.vector(dve)
        norm.done(2)


BRANCHES = [deformable_mixer_and_recurrence, divisive_mixer, routed_depth_ffn, scan_mixer, experts_ffn, sign_conv_mixer, normed_experts_ffn]


def program(nc, args, out, first=0, last=len(BRANCHES)):
    with ExitStack() as ctx:
        core = Core(nc, ctx)
        load_x(core, args["x"])
        for branch in BRANCHES[first:last]:
            branch(core, args)
        store_x(core, out)


def kernel(**inputs):
    import numpy as np
    import concourse.bacc as bacc
    from concourse.bass_utils import run_bass_kernel_spmd

    nc = bacc.Bacc("TRN2", target_bir_lowering=False, num_devices=1)
    arrays, args = {}, {}
    for name, value in inputs.items():
        a = np.ascontiguousarray(value)
        arrays[f"in_{name}"] = a
        args[name] = nc.dram_tensor(f"in_{name}", a.shape, mybir.dt.from_np(a.dtype), kind="ExternalInput").ap()
    out = nc.dram_tensor("out_0_dram", (IMG, ROWS, COLS, C), F32, kind="ExternalOutput").ap()
    program(nc, args, out)
    r = run_bass_kernel_spmd(nc, [arrays], core_ids=[0])
    return r.results[0]["out_0_dram"]
```

```python
from contextlib import ExitStack
from itertools import count

import concourse.bass as bass
from concourse import mybir

F32 = mybir.dt.float32
BF16 = mybir.dt.bfloat16
I32 = mybir.dt.int32
ALU = mybir.AluOpType
ACT = mybir.ActivationFunctionType
AX = mybir.AxisListType

C = 128
IMG, ROWS, COLS = 8, 32, 32
PIX = ROWS * COLS
TOK = IMG * PIX
HALF = PIX // 2
HROWS = ROWS // 2
PAD = ROWS + 2
TILE = 128
TPI = PIX // TILE

START = 1
INDIRECT = 18
LOG_EXP = "natural_log_exp_and_others"


def halves(b):
    return [b * PIX + h * HALF for h in range(2)]


class Core:

    def __init__(self, nc, ctx):
        self.nc, self.ctx, self.new_sems = nc, ctx, []
        self.branch = ctx
        self.untouched = [ctx.enter_context(nc.semaphore(f"indirect{n}")) for n in range(INDIRECT)]
        self.x = self.sb(ctx, "x_t", [C, TOK])
        self.ident = self.sb(ctx, "ident", [C, C])
        self.mean_w = self.sb(ctx, "mean_w", [C, C])
        self.bank = [ctx.enter_context(nc.psum_tensor(f"bank{n}", [C, HALF], F32)) for n in range(8)]
        self.norm = Norm(self)

    def sb(self, mem, name, shape, dtype=F32):
        return mem.enter_context(self.nc.sbuf_tensor(name, shape, dtype))

    def sem(self, name):
        s = self.branch.enter_context(self.nc.semaphore(name))
        self.new_sems.append(s)
        return s

    def indirect_sem(self):
        return self.untouched.pop(0)

    def run(self, branch, *args):
        with ExitStack() as self.branch:
            branch(self, *args)

    def start_counts(self):
        raised, self.new_sems = self.new_sems, []
        with self.nc.Block() as block:
            @block.sync
            def _(sp):
                for s in raised:
                    sp.sem_clear(s)
                    sp.sem_inc(s, START)


class Norm:

    def __init__(self, core):
        ctx = core.ctx
        self.core, self.base = core, 0
        self.mean, self.var = core.bank[0:2], core.bank[2:4]
        self.cent = [core.sb(ctx, f"norm_cent{h}", [C, HALF]) for h in range(2)]
        self.sq = [core.sb(ctx, f"norm_sq{h}", [C, HALF]) for h in range(2)]
        self.rstd = [core.sb(ctx, f"norm_rstd{h}", [C, HALF]) for h in range(2)]
        self.eps = {e: core.sb(ctx, f"norm_eps{n}", [C, 1]) for n, e in enumerate((1e-6, 1e-5))}
        self.s_mean = core.sem("norm_mean")
        self.s_cent = core.sem("norm_centred")
        self.s_sq = core.sem("norm_squared")
        self.s_var = core.sem("norm_variance")
        self.s_log = core.sem("norm_log")
        self.s_rstd = core.sem("norm_rstd_ready")
        self.s_out = core.sem("norm_out")

    def tensor(self, pe, i, src):
        n = self.base + 2 * i
        pe.wait_ge(self.s_cent, START + n)
        for h in range(2):
            out = self.mean[h][:, :] if len(src[h].shape) == 2 else self.mean[h][:, :].rearrange("c (b t) -> c b t", b=src[h].shape[1])
            pe.matmul(out, self.core.mean_w[:, :], src[h], start=True, stop=True).then_inc(self.s_mean, 1)
        pe.wait_ge(self.s_log, START + n)
        for h in range(2):
            pe.wait_ge(self.s_sq, START + n + h + 1)
            pe.matmul(self.var[h][:, :], self.core.mean_w[:, :], self.sq[h][:, :], start=True, stop=True).then_inc(self.s_var, 1)

    def scalar(self, act, i, eps):
        n = self.base + 2 * i
        act.wait_ge(self.s_var, START + n)
        for h in range(2):
            act.wait_ge(self.s_cent, START + n + h + 1)
            act.activation(self.sq[h][:, :], self.cent[h][:, :], ACT.Square).then_inc(self.s_sq, 1)
        act.wait_ge(self.s_out, START + n)
        for h in range(2):
            act.wait_ge(self.s_var, START + n + h + 1)
            act.activation(self.rstd[h][:, :], self.var[h][:, :], ACT.Ln, bias=self.eps[eps][:, 0:1]).then_inc(self.s_log, 1)
        for h in range(2):
            act.wait_ge(self.s_log, START + n + h + 1)
            act.activation(self.rstd[h][:, :], self.rstd[h][:, :], ACT.Exp, scale=-0.5).then_inc(self.s_rstd, 1)

    def vector(self, dve, i, src, dst, cols=COLS):
        self.centre(dve, i, src, cols)
        self.finish(dve, i, dst, cols)

    def centre(self, dve, i, src, cols=COLS):
        n = self.base + 2 * i
        dve.wait_ge(self.s_out, START + n)
        for h in range(2):
            dve.wait_ge(self.s_mean, START + n + h + 1)
            as_src = (lambda t: t) if len(src[h].shape) == 2 else (lambda t: t.rearrange("c (r w) -> c r w", w=cols))
            dve.tensor_tensor(as_src(self.cent[h][:, :]), src[h], as_src(self.mean[h][:, :]), ALU.subtract).then_inc(self.s_cent, 1)

    def finish(self, dve, i, dst, cols=COLS):
        n = self.base + 2 * i
        for h in range(2):
            dve.wait_ge(self.s_rstd, START + n + h + 1)
            dve.tensor_tensor(dst[h], image(self.cent[h], cols), image(self.rstd[h], cols), ALU.mult).then_inc(self.s_out, 1)

    def ready(self, i, h):
        return self.base + 2 * i + h + 1

    def done(self, times=1):
        self.base += 2 * IMG * times


def ahead(eng, count, first, start, rest):
    start(0)
    with eng.Fori(0, count - 1) as i:
        first(i)
        start(i + 1)
        rest(i)
    first(count - 1)
    rest(count - 1)


def x_halves(core, b):
    return [core.x[:, bass.ds(o, HALF)] for o in halves(b)]


def image(half, cols=COLS):
    return half[:, :].rearrange("c (r w) -> c r w", w=cols)


def inner(padded, h):
    return padded[:, 1 + HROWS * h:1 + HROWS * (h + 1), 1:1 + COLS]


def window(padded, h, tap):
    dy, dx = divmod(tap, 3)
    return padded[:, HROWS * h + dy:HROWS * (h + 1) + dy, dx:dx + COLS]


def column(vec):
    return vec.rearrange("(c o) -> c o", o=1)


def load_x(core, x):
    nc = core.nc
    rows = x.rearrange("i r w c -> (i r w) c").rearrange("(i j p) c -> i p j c", p=TILE, j=TPI)
    with ExitStack() as mem:
        raw = [core.sb(mem, f"raw{k}", [TILE, TPI, C]) for k in range(2)]
        s_const, s_raw, s_turn, s_copied = (core.sem(f"load_{n}") for n in ("const", "raw", "turned", "copied"))
        s_raws = [s_raw, core.sem("load_raw1")]
        core.start_counts()
        with nc.Block() as block:
            @block.gpsimd
            def _(pool):
                pool.memset(core.ident[:, :], 0.0).then_inc(s_const, 1)
                pool.memset(core.mean_w[:, :], 1.0 / C).then_inc(s_const, 1)
                for e, t in core.norm.eps.items():
                    pool.memset(t[:, :], e).then_inc(s_const, 1)
                pool.wait_ge(s_const, START + 4)
                pool.affine_select(out=core.ident[:, :], in_=core.ident[:, :], compare_op=ALU.not_equal, fill=1.0,
                                   base=0, pattern=[[-1, C]], channel_multiplier=1).then_inc(s_const, 1)

            @block.sync
            def _(sp):
                with sp.Fori(0, IMG // 2) as p:
                    for k in range(2):
                        sp.wait_ge(s_turn, START + 4 * p + 2 * k)
                        sp.dma_start(raw[k][:, :, :], rows[2 * p + k]).then_inc(s_raws[k], 16)

            @block.tensor
            def _(pe):
                pe.wait_ge(s_const, START + 5)
                with pe.Fori(0, IMG // 2) as p:
                    for k in range(2):
                        pe.wait_ge(s_raws[k], START + 16 * p + 16)
                        for h in range(2):
                            if k:
                                pe.wait_ge(s_copied, START + 4 * p + h + 1)
                            else:
                                pe.wait_ge(s_copied, START + 4 * p)
                            for j in range(4):
                                mm = pe.transpose(core.bank[h][:, j * TILE:(j + 1) * TILE], raw[k][:, 4 * h + j, :], core.ident[:, :])
                            mm.then_inc(s_turn, 1)

            @block.vector
            def _(dve):
                with dve.Fori(0, IMG // 2) as p:
                    for k in range(2):
                        for h in range(2):
                            dve.wait_ge(s_turn, START + 4 * p + 2 * k + h + 1)
                            dve.tensor_copy(core.x[:, bass.ds(p * (2 * PIX) + (k * PIX + h * HALF), HALF)], core.bank[h][:, :]).then_inc(s_copied, 1)


def store_x(core, out):
    nc = core.nc
    rows = out.rearrange("i r w c -> (i r w) c").rearrange("(i h j p) c -> i h p j c", p=TILE, j=4, h=2)
    with ExitStack() as mem:
        flat = [core.sb(mem, f"flat{h}", [TILE, 4, C]) for h in range(2)]
        s_turn, s_copied = core.sem("store_turned"), core.sem("store_copied")
        s_stored = [core.sem(f"store_done{h}") for h in range(2)]
        stage = [core.sb(mem, f"store_in{h}", [C, HALF]) for h in range(2)]
        s_stage = core.sem("store_staged")
        core.start_counts()
        with nc.Block() as block:
            @block.vector
            def _(dve):
                with dve.Fori(0, IMG) as b:
                    dve.wait_ge(s_turn, START + 2 * b)
                    for h in range(2):
                        dve.tensor_copy(stage[h][:, :], core.x[:, bass.ds(b * PIX + h * HALF, HALF)]).then_inc(s_stage, 1)

            @block.tensor
            def _(pe):
                with pe.Fori(0, IMG) as b:
                    pe.wait_ge(s_copied, START + 2 * b)
                    for h in range(2):
                        pe.wait_ge(s_stage, START + 2 * b + h + 1)
                        for j in range(4):
                            mm = pe.transpose(core.bank[h][:, j * TILE:(j + 1) * TILE], stage[h][:, j * TILE:(j + 1) * TILE], core.ident[:, :])
                        mm.then_inc(s_turn, 1)

            @block.scalar
            def _(act):
                with act.Fori(0, IMG) as b:
                    for h in range(2):
                        act.wait_ge(s_stored[h], START + 16 * b)
                        act.wait_ge(s_turn, START + 2 * b + h + 1)
                        act.activation(flat[h][:, :, :], core.bank[h][:, :].rearrange("p (j c) -> p j c", c=C), ACT.Copy).then_inc(s_copied, 1)

            @block.sync
            def _(sp):
                with sp.Fori(0, IMG) as b:
                    for h in range(2):
                        sp.wait_ge(s_copied, START + 2 * b + h + 1)
                        sp.dma_start(rows[b, h], flat[h][:, :, :]).then_inc(s_stored[h], 16)
                for h in range(2):
                    sp.wait_ge(s_stored[h], START + 16 * IMG)


class Sampling:
    G, TAPS, XY = 8, 9, 2
    GC = C // G
    GT = G * TAPS
    CORNERS = 4
    CELL = CORNERS * GC
    CROWS = 3
    CW = COLS + 3
    CH = -(-(ROWS + 2) // CROWS) * CROWS
    BW, BH = CW, CH + 2
    CELLS = CH * CW * G
    TILES = TOK // TILE
    NOFF = GT * XY
    NLOG = NOFF + GT


def deformable_mixer_and_recurrence(core, args):
    S = Sampling
    table = core.nc.dram_tensor("corner_table", (IMG * S.CELLS, S.CELL), F32).ap()
    with ExitStack() as keep:
        index = core.sb(keep, "df_index", [TILE, TPI, IMG, S.GT], I32)
        weight = core.sb(keep, "df_weight", [TILE, TPI, IMG, S.GT, S.CORNERS])
        with ExitStack() as mem:
            sample_positions(core, args, mem, table, index, weight)
        with ExitStack() as mem:
            gather_samples(core, args, mem, table, index, weight)


def sample_positions(core, args, mem, table, index, weight):
    nc, norm, X, S = core.nc, core.norm, core.x, Sampling
    G, TAPS, XY, GC, GT, CORNERS, CROWS, CW, CH, BW, BH = S.G, S.TAPS, S.XY, S.GC, S.GT, S.CORNERS, S.CROWS, S.CW, S.CH, S.BW, S.BH
    CELLS, NOFF, NLOG = S.CELLS, S.NOFF, S.NLOG
    table_rows = table.rearrange("(i t p g) d -> i t p (g d)", g=G, p=CROWS * CW, i=IMG)
    sb = lambda name, dims, dt=F32: core.sb(mem, f"df_{name}", dims, dt)
    xpad = sb("padded", [C, BH, BW])
    inside = sb("inside", [1, BH, BW])
    ones = sb("ones", [1, TILE])
    w_in, b_in = sb("w_in", [C, C]), sb("b_in", [1, C])
    taps, dw_bias = sb("taps", [C, TAPS]), sb("dw_bias", [C, 1])
    gamma, beta = sb("gamma", [C, 1]), sb("beta", [C, 1])
    w_log, b_log = sb("w_log", [C, NLOG]), sb("b_log", [1, NLOG])
    THALF = TPI // 2
    cells = [sb(f"cells{k}", [CROWS * CW, G * CORNERS * GC]) for k in range(2)]
    x1 = sb("x1", [C, PIX])
    logit = sb("logits", [TILE, TPI, NLOG])
    pos = sb("pos", [TILE, THALF, GT, XY])
    whole = sb("whole", [TILE, THALF, GT, XY], I32)
    low = sb("low", [TILE, THALF, GT, XY])
    above = sb("above", [TILE, THALF, GT, XY])
    base = sb("base", [TILE, TPI, GT, XY])
    steps = sb("steps", [TILE, TPI * GT], I32)
    part = sb("part", [TILE, 3], I32)
    partf = sb("partf", [TILE, 2])
    row0 = sb("row0", [TILE, THALF * GT])
    mask = sb("mask", [TILE, THALF * G, TAPS])
    top = sb("top", [TILE, THALF * G])
    wy = [sb(f"wy{k}", [TILE, THALF, GT]) for k in range(2)]
    first = FirstTiles(core, args, mem, table, index, weight)
    (s_par, s_zero, s_iota, s_pixel, s_base, s_cell, s_copy, s_conv, s_gelu, s_log, s_logit, s_step, s_exp, s_done) = (
        core.sem(f"df_{n}") for n in ("params", "zero", "iota", "pixel", "base", "cells", "cells_copied", "convolved", "gelu", "logit_products",
                                      "logits", "steps", "exp", "positions"))
    s_table = [core.sem(f"df_table{k}") for k in range(2)]
    NT = CH // CROWS
    EARLY = 4
    NSTEP = 16
    xpad_in = [xpad[:, 1 + HROWS * h:1 + HROWS * (h + 1), 1:1 + COLS] for h in range(2)]
    x13 = x1[:, :].rearrange("c (r w) -> c r w", w=COLS)
    all_ = lambda t: t[:, :, :, :].rearrange("p t s d -> p (t s d)")
    along = lambda t, d: t[:, :, :, d:d + 1].rearrange("p t s d -> p t (s d)")
    NPAR = 10
    core.start_counts()
    with nc.Block() as block:
        @block.sync
        def _(sp):
            p = lambda n: args[f"L0_conv_{n}"]
            row = lambda a: a.rearrange("(o n) -> o n", o=1)
            for dst, src in ((w_in[:, :], p("w_in")), (b_in[:, :], row(p("b_in"))), (dw_bias[:, :], column(p("dw_bias"))),
                             (gamma[:, :], column(p("ln_gamma"))), (beta[:, :], column(p("ln_beta"))),
                             (w_log[:, 0:NOFF], p("w_off")), (w_log[:, NOFF:NLOG], p("w_mask")),
                             (b_log[:, 0:NOFF], row(p("b_off"))), (b_log[:, NOFF:NLOG], row(p("b_mask")))):
                sp.dma_start(dst, src).then_inc(s_par, 16)
            sp.dma_start(taps[:, :], p("dw_kernel").rearrange("a b o c -> c (a b o)"), allow_slow_non_contiguous=True).then_inc(s_par, 16)
            first.load(sp)
            sp.wait_ge(first.s_fill, START + 16 * IMG)
            with sp.Fori(0, IMG) as b:
                for t in range(NT):
                    sp.wait_ge(s_copy, START + NT * b + t + 1)
                    sp.dma_start(table_rows[bass.ds(b, 1), t].rearrange("o p d -> p (o d)"), cells[t % 2][:, :]).then_inc(s_table[t % 2], 16)
            for k in range(2):
                sp.wait_ge(s_table[k], START + 16 * NT // 2 * IMG)

        @block.gpsimd
        def _(pool):
            pool.memset(first.samples[0][:, :], 0.0).then_inc(first.s_zero, 1)
            pool.memset(xpad[:, :, :], 0.0).then_inc(s_zero, 1)
            pool.memset(inside[:, :, :], 0.0).then_inc(s_zero, 1)
            pool.memset(ones[:, :], 1.0).then_inc(s_zero, 1)
            pool.wait_ge(s_zero, START + 3)
            pool.memset(inside[:, 1:1 + ROWS, 1:1 + COLS], 1.0).then_inc(s_zero, 1)
            pool.iota(part[:, 0:1], pattern=[[0, 1]], base=0, channel_multiplier=1).then_inc(s_iota, 1)
            for n, pattern in enumerate(([[0, TPI], [0, G], [0, 3], [1, 3]], [[TILE // COLS, TPI], [0, G], [1, 3], [0, 3]], [[0, TPI], [1, G], [0, 3], [0, 3]])):
                if n:
                    pool.wait_ge(s_base, START + n)
                pool.iota(steps[:, :], pattern=pattern, base=0, channel_multiplier=0).then_inc(s_iota, 1)
            pool.wait_ge(first.s_fill, START + 16 * IMG)
            with pool.Fori(0, IMG) as b:
                for k in range(2):
                    pool.wait_ge(s_table[k], START + 16 * (NT // 2) * (b + 1))
                pool.wait_ge(s_done, START + 2 * b + 1)
                first.gather(pool, b)

        @block.tensor
        def _(pe):
            pe.wait_ge(s_par, START + 16 * NPAR)
            pe.wait_ge(s_zero, START + 4)
            def prepare(b):
                norm.tensor(pe, 2 * b, [X[:, bass.ds(o, HALF)] for o in halves(b)])
                for h in range(2):
                    pe.wait_ge(norm.s_out, START + norm.ready(2 * b, h))

                def make_cells(t):
                    bank = core.bank[4 + t % 2]
                    pe.wait_ge(s_copy, START + NT * b + max(0, t - 1))
                    for k in range(CORNERS):
                        dy, dx = divmod(k, 2)
                        at = slice((CROWS * t + dy) * BW + dx, (CROWS * (t + 1) + dy) * BW + dx)
                        out = bank[0:CROWS * CW, k * C:(k + 1) * C]
                        pe.matmul(out, xpad[:, :, :].rearrange("c h w -> c (h w)")[:, at], w_in[:, :], start=True, stop=False)
                        mm = pe.matmul(out, inside[:, :, :].rearrange("c h w -> c (h w)")[:, at], b_in[:, :], start=False, stop=True)
                    mm.then_inc(s_cell, 1)

                for t in range(EARLY):
                    make_cells(t)
                pe.wait_ge(s_conv, START + TAPS * (b + 1))
                norm.tensor(pe, 2 * b + 1, [x1[:, h * HALF:(h + 1) * HALF] for h in range(2)])
                for j in range(TPI):
                    if j % 4 == 0:
                        pe.wait_ge(s_gelu, START + 2 * b + j // 4 + 1)
                    if j % 2 == 0:
                        pe.wait_ge(s_logit, START + 4 * b + max(0, j // 2 - 1))
                    out = core.bank[6 + j // 2 % 2][:, j % 2 * NLOG:(j % 2 + 1) * NLOG]
                    pe.matmul(out, x1[:, j * TILE:(j + 1) * TILE], w_log[:, :], start=True, stop=False)
                    mm = pe.matmul(out, ones[:, :], b_log[:, :], start=False, stop=True)
                    if j % 2:
                        mm.then_inc(s_log, 1)
                for t in range(EARLY, NT):
                    make_cells(t)

            first.pipeline(pe, prepare, first.tensor)

        @block.scalar
        def _(act):
            act.wait_ge(s_par, START + 16 * NPAR)
            def prepare(b):
                norm.scalar(act, 2 * b, 1e-6)

                def copy_cells(t):
                    act.wait_ge(s_cell, START + NT * b + t + 1)
                    act.wait_ge(s_table[t % 2], START + 16 * (NT // 2 * b + t // 2))
                    act.activation(cells[t % 2][:, :].rearrange("p (g k c) -> p k g c", g=G, k=CORNERS),
                                   core.bank[4 + t % 2][0:CROWS * CW, :].rearrange("p (k g c) -> p k g c", g=G, k=CORNERS), ACT.Copy).then_inc(s_copy, 1)

                for t in range(EARLY):
                    copy_cells(t)
                norm.scalar(act, 2 * b + 1, 1e-6)
                for h in range(2):
                    half = x1[:, h * HALF:(h + 1) * HALF]
                    act.wait_ge(norm.s_out, START + norm.ready(2 * b + 1, h))
                    act.activation(half, half, ACT.Gelu, scale=gamma[:, 0:1], bias=beta[:, 0:1]).then_inc(s_gelu, 1)
                act.wait_ge(s_done, START + 2 * b)
                for j in range(4):
                    act.wait_ge(s_log, START + 4 * b + j + 1)
                    act.activation(logit[:, 2 * j:2 * j + 2, :], core.bank[6 + j % 2][:, 0:2 * NLOG].rearrange("p (t n) -> p t n", n=NLOG), ACT.Copy).then_inc(s_logit, 1)
                for h in range(2):
                    act.wait_ge(s_step, START + NSTEP * (2 * b + h) + 3)
                    act.activation(mask[:, :, :], mask[:, :, :], ACT.Exp).then_inc(s_exp, 1)
                    for t in range(EARLY, NT if h == 0 else EARLY):
                        copy_cells(t)

            first.pipeline(act, prepare, first.scalar)

        def positions(dve, b, h):
            count = 0
            at = slice(h * THALF, (h + 1) * THALF)

            def step(ins):
                nonlocal count
                count += 1
                return ins.then_inc(s_step, 1)

            def after(n):
                dve.wait_ge(s_step, START + NSTEP * (2 * b + h) + n)

            ml = logit[:, at, NOFF:NLOG].rearrange("p t (g k) -> p t g k", k=TAPS)
            mg = mask[:, :, :].rearrange("p (t g) k -> p t g k", g=G)
            m3 = mask[:, :, :].rearrange("p (t g) k -> p t (g k)", g=G)
            top_t = top[:, :].rearrange("p (t g) -> p t g", g=G)
            top_wide = top[:, :].rearrange("p (n k) -> p n k", k=1).broadcast_to([TILE, THALF * G, TAPS])
            by_tile = lambda t: t.rearrange("p t s d -> p t (s d)")
            dve.wait_ge(s_done, START + 2 * b + h)
            step(dve.tensor_reduce(top_t, ml, AX.X, ALU.max))
            step(dve.tensor_tensor(by_tile(pos[:, :, :, :]), logit[:, at, 0:NOFF], by_tile(base[:, at, :, :]), ALU.add))
            after(1)
            step(dve.tensor_tensor(mg, ml, top_t.rearrange("p t (g k) -> p t g k", k=1).broadcast_to([TILE, THALF, G, TAPS]), ALU.subtract))
            after(2)
            step(dve.tensor_scalar(all_(pos), all_(pos), 0.0, float(COLS + 1), ALU.max, ALU.min))
            after(4)
            step(dve.tensor_copy(all_(whole), all_(pos)))
            after(5)
            step(dve.tensor_copy(all_(low), all_(whole)))
            after(6)
            step(dve.tensor_tensor(all_(above), all_(low), all_(pos), ALU.is_gt))
            after(7)
            step(dve.tensor_tensor(all_(low), all_(low), all_(above), ALU.subtract))
            after(8)
            step(dve.tensor_tensor(all_(pos), all_(pos), all_(low), ALU.subtract))
            after(9)
            step(dve.tensor_scalar(all_(above), all_(pos), -1.0, 1.0, ALU.mult, ALU.add))
            flat = lambda t: t[:, :, :].rearrange("p t s -> p (t s)")
            step(dve.scalar_tensor_tensor(out=flat(wy[0]), in0=along(low, 1), scalar=float(CW), in1=along(low, 0), op0=ALU.mult, op1=ALU.add))
            after(11)
            step(dve.scalar_tensor_tensor(out=index[:, at, bass.ds(b, 1), :].rearrange("p t b s -> p t (b s)"), in0=wy[0][:, :, :], scalar=float(G),
                                          in1=row0[:, :].rearrange("p (t s) -> p t s", s=GT), op0=ALU.mult, op1=ALU.add))
            dve.wait_ge(s_exp, START + 2 * b + h + 1)
            step(dve.tensor_reduce(top[:, :], mask[:, :, :], AX.X, ALU.add))
            after(13)
            step(dve.reciprocal(top[:, :], top[:, :]))
            after(12)
            if h:
                dve.tensor_scalar(row0[:, :], row0[:, :], float(CELLS), None, ALU.add)
            after(14)
            step(dve.tensor_tensor(mask[:, :, :], mask[:, :, :], top_wide, ALU.mult))
            after(15)
            dve.tensor_tensor(flat(wy[0]), along(above, 1), m3.rearrange("p t s -> p (t s)"), ALU.mult)
            step(dve.tensor_tensor(flat(wy[1]), along(pos, 1), m3.rearrange("p t s -> p (t s)"), ALU.mult))
            after(16)
            for k in range(CORNERS):
                dy, dx = divmod(k, 2)
                out = weight[:, at, bass.ds(b, 1), :, k:k + 1].rearrange("p t b s k -> p t (b s k)")
                ins = dve.tensor_tensor(out, wy[dy][:, :, :], (pos if dx else above)[:, :, :, 0:1].rearrange("p t s d -> p t (s d)"), ALU.mult)
            ins.then_inc(s_done, 1)
            assert count == NSTEP

        @block.vector
        def _(dve):
            dve.wait_ge(s_iota, START + 1)
            dve.tensor_scalar(part[:, 1:2], part[:, 0:1], COLS - 1, None, ALU.bitwise_and).then_inc(s_pixel, 1)
            dve.tensor_scalar(part[:, 2:3], part[:, 0:1], COLS.bit_length() - 1, None, ALU.logical_shift_right).then_inc(s_pixel, 1)
            dve.wait_ge(s_pixel, START + 2)
            dve.tensor_copy(partf[:, :], part[:, 1:3]).then_inc(s_pixel, 1)
            dve.wait_ge(s_pixel, START + 3)
            flat_steps = steps[:, :].rearrange("p (t s) -> p t s", s=GT)
            for d in range(XY):
                dve.wait_ge(s_iota, START + 2 + d)
                dve.tensor_scalar(along(base, d), flat_steps, partf[:, d:d + 1], None, ALU.add).then_inc(s_base, 1)
            dve.wait_ge(s_iota, START + 4)
            dve.tensor_copy(row0[:, :], steps[:, 0:THALF * GT]).then_inc(s_base, 1)
            dve.wait_ge(s_base, START + 3)
            dve.wait_ge(s_par, START + 16 * NPAR)
            dve.wait_ge(s_zero, START + 4)
            def prepare(b):
                dve.wait_ge(s_cell, START + NT * b)
                norm.vector(dve, 2 * b, [X[:, bass.ds(o, HALF)] for o in halves(b)], xpad_in)
                for h in range(2):
                    dve.wait_ge(norm.s_out, START + norm.ready(2 * b, h))
                dve.wait_ge(s_log, START + 4 * b)
                for t in range(TAPS):
                    win = xpad[:, t // 3:t // 3 + ROWS, t % 3:t % 3 + COLS]
                    if t == 0:
                        dve.tensor_scalar(x13, win, taps[:, 0:1], dw_bias[:, 0:1], ALU.mult, ALU.add).then_inc(s_conv, 1)
                        continue
                    dve.wait_ge(s_conv, START + TAPS * b + t)
                    dve.scalar_tensor_tensor(out=x13, in0=win, scalar=taps[:, t:t + 1], in1=x13, op0=ALU.mult, op1=ALU.add).then_inc(s_conv, 1)
                dve.wait_ge(s_conv, START + TAPS * (b + 1))
                norm.vector(dve, 2 * b + 1, [x1[:, h * HALF:(h + 1) * HALF] for h in range(2)], [x13[:, 0:HROWS], x13[:, HROWS:ROWS]])
                dve.wait_ge(s_logit, START + 4 * b + 4)
                for h in range(2):
                    positions(dve, b, h)

            first.pipeline(dve, prepare, lambda d, b: first.vector(d, b, s_done))
    norm.done(2)


class FirstTiles:

    def __init__(self, core, args, mem, table, index, weight):
        self.core, self.args, self.table, self.index, self.weight = core, args, table, index, weight
        S = Sampling
        sb = lambda name, dims, dt=F32: core.sb(mem, f"first_{name}", dims, dt)
        self.N = S.GT // 2
        self.own = [sb(f"own_index{k}", [TILE, self.N], I32) for k in range(2)]
        self.samples = [sb(f"samples{k}", [TILE, self.N * S.CELL]) for k in range(2)]
        self.summed = sb("summed", [TILE, C])
        self.turned = sb("turned", [C, TILE])
        self.w_out, self.b_out = sb("w_out", [C, C]), sb("b_out", [C, 1])
        self.s_par, self.s_begun, self.s_own, self.s_weighted, self.s_turn, self.s_copy, self.s_out, self.s_end = (
            core.sem(f"first_{n}") for n in ("params", "begun", "own_index", "weighted", "turned", "turned_copied", "out_product", "end"))
        self.s_sum = [core.sem(f"first_summed{k}") for k in range(2)]
        self.s_zero, self.s_fill = core.sem("first_zero"), core.sem("first_filled")
        self.s_got = [core.indirect_sem() for k in range(2)]

    def pipeline(self, eng, prepare, tile):
        prepare(0)
        with eng.Fori(1, IMG) as b:
            prepare(b)
            tile(eng, b - 1)
        tile(eng, IMG - 1)

    def load(self, sp):
        S, FILL = Sampling, 1280
        PARTS = S.CELLS * S.CELL // (4 * FILL)
        image_table = self.table.rearrange("(i p r) d -> i p (r d)", i=IMG, p=PARTS)
        sp.wait_ge(self.s_zero, START + 1)
        zeros = self.samples[0][0:PARTS, 0:FILL].rearrange("p (o f) -> p o f", o=1).broadcast_to([PARTS, 4, FILL])
        for b in range(IMG):
            sp.dma_start(image_table[b].rearrange("p (o f) -> p o f", o=4), zeros).then_inc(self.s_fill, 16)
        sp.dma_start(self.w_out[:, :], self.args["L0_conv_w_out"]).then_inc(self.s_par, 16)
        sp.dma_start(self.b_out[:, :], column(self.args["L0_conv_b_out"])).then_inc(self.s_par, 16)

    def gather(self, pool, b):
        S, N = Sampling, self.N
        for k in range(2):
            pool.wait_ge(self.s_sum[k], START + b)
            pool.sem_inc(self.s_begun, 1)
            pool.tensor_copy(self.own[k][:, :], self.index[:, 0, bass.ds(b, 1), k * N:(k + 1) * N].rearrange("p o s -> p (o s)")).then_inc(self.s_own, 1)
            pool.wait_ge(self.s_own, START + 2 * b + k + 1)
            pool.sem_inc(self.s_begun, 1)
            for s in range(N):
                pool.indirect_dma_start(self.samples[k][:, s * S.CELL:(s + 1) * S.CELL], None, self.table[:, :],
                                        bass.IndirectOffsetOnAxis(ap=self.own[k][:, s:s + 1], axis=0)).then_inc(self.s_got[k], 16)

    def tensor(self, pe, b):
        pe.wait_ge(self.s_par, START + 32)
        pe.wait_ge(self.s_sum[1], START + b + 1)
        pe.transpose(self.core.bank[2][:, 0:TILE], self.summed[:, :], self.core.ident[:, :]).then_inc(self.s_turn, 1)
        pe.wait_ge(self.s_copy, START + b + 1)
        pe.matmul(self.core.bank[3][:, 0:TILE], self.w_out[:, :], self.turned[:, :], start=True, stop=True).then_inc(self.s_out, 1)

    def scalar(self, act, b):
        act.wait_ge(self.s_turn, START + b + 1)
        act.activation(self.turned[:, :], self.core.bank[2][:, 0:TILE], ACT.Copy).then_inc(self.s_copy, 1)

    def vector(self, dve, b, s_done):
        S, N = Sampling, self.N
        G, HALFC = S.G // 2, C // 2
        dve.wait_ge(s_done, START + 2 * b + 1)
        dve.wait_ge(self.s_turn, START + b)
        for k in range(2):
            dve.wait_ge(self.s_got[k], 16 * N * (b + 1))
            by_value = self.samples[k][:, :].rearrange("p (s c) -> p s c", c=S.GC)
            w = (self.weight[:, 0, bass.ds(b, 1), k * N:(k + 1) * N, :].rearrange("p o s (k c) -> p (o s k) c", c=1)
                 .broadcast_to([TILE, N * S.CORNERS, S.GC]))
            dve.tensor_tensor(by_value, by_value, w, ALU.mult).then_inc(self.s_weighted, 1)
            dve.wait_ge(self.s_weighted, START + 2 * b + k + 1)
            dve.tensor_reduce(self.summed[:, k * HALFC:(k + 1) * HALFC].rearrange("p (g c) -> p g c", g=G),
                              self.samples[k][:, :].rearrange("p (g s c) -> p g c s", g=G, c=S.GC), AX.X, ALU.add).then_inc(self.s_sum[k], 1)
        xs = self.core.x[:, bass.ds(b * PIX, TILE)]
        dve.wait_ge(self.s_out, START + b + 1)
        dve.scalar_tensor_tensor(out=xs, in0=self.core.bank[3][:, 0:TILE], scalar=self.b_out[:, 0:1], in1=xs, op0=ALU.add, op1=ALU.add).then_inc(self.s_end, 1)


def gather_samples(core, args, mem, table, index, weight):
    X, norm, S = core.x, core.norm, Sampling
    G, GC, GT, CORNERS, CELL, TILES = S.G, S.GC, S.GT, S.CORNERS, S.CELL, S.TILES
    GATES = (("i", 0.5), ("o", 0.5), ("c", 1.0))
    NG = len(GATES)
    W = NG * IMG
    SLOT = TILE // IMG
    UNROLL = 8
    NM = 2 * NG
    sb = lambda name, dims, dt=F32: core.sb(mem, f"dg_{name}", dims, dt)
    own = [sb(f"own_index{k}", [TILE, GT], I32) for k in range(2)]
    samples = [sb(f"samples{k}", [TILE, GT * CELL]) for k in range(2)]
    summed = [sb(f"summed{k}", [TILE, C]) for k in range(2)]
    turned = [sb(f"turned{k}", [C, TILE]) for k in range(2)]
    w_out, b_out = sb("w_out", [C, C]), sb("b_out", [C, 1])
    v = sb("v", [C, PIX])
    v3 = v[:, :].rearrange("c (b t) -> c b t", t=TILE)
    wu, wv, bias = sb("u_w", [C, NG, C]), sb("v_w", [C, NG, C]), sb("gate_bias", [C, NG])
    gx = sb("gate_inputs", [C, TILE, W])
    hs = sb("hidden", [C, TILE + 1, IMG])
    gates = sb("gates", [C, W])
    cell, hc, tc, ig, og = (sb(n, [C, IMG]) for n in ("cell", "hc", "tanh_cell", "ig", "og"))
    (s_par, s_half, s_zero, s_begun, s_own, s_weighted, s_turn, s_copy, s_out, s_end, s_gmm, s_gx,
     s_pre, s_tanh, s_ig, s_og, s_cell, s_tc, s_h, s_hc, s_carry, s_x) = (core.sem(f"dg_{n}") for n in (
        "params", "halved", "zero", "begun", "own_index", "weighted", "turned", "turned_copied", "out_product", "end", "gate_products",
        "gate_inputs", "preacts", "tanh", "ig", "og", "cell", "tanh_cell", "hidden", "hc", "carried", "x"))
    s_sum = [core.sem(f"dg_summed{k}") for k in range(2)]
    NS = 4
    s_got = [[core.indirect_sem() for n in range(NS)] for k in range(2)]
    PER = GT // NS
    NPAR = 2 + 3 * NG
    tokens = X[:, :].rearrange("c (b j t) -> c b j t", b=IMG, j=TPI)

    def phase_half(j, h):
        return tokens[:, 4 * h:4 * h + 4, bass.ds(j, 1), :].rearrange("c b j t -> c b (j t)")

    def slots(eng, steps, tile, finish):
        finish(0)
        with eng.Fori(1, TPI) as j:
            with eng.Fori(0, IMG // 2) as p:
                for k in range(2):
                    with eng.Fori(0, SLOT // UNROLL) as s:
                        for u in range(UNROLL):
                            at = (2 * p + k) * SLOT + s * UNROLL + u
                            steps((j - 1) * TILE + at, at, u)
                    tile(j, p, k)
            finish(j)
        with eng.Fori(0, TILE // UNROLL) as s:
            for u in range(UNROLL):
                steps((TPI - 1) * TILE + s * UNROLL + u, s * UNROLL + u, u)

    core.start_counts()
    with core.nc.Block() as block:
        @block.sync
        def _(sp):
            sp.dma_start(w_out[:, :], args["L0_conv_w_out"]).then_inc(s_par, 16)
            sp.dma_start(b_out[:, :], column(args["L0_conv_b_out"])).then_inc(s_par, 16)
            for n, (g, _) in enumerate(GATES):
                sp.dma_start(wu[:, n, :], args[f"L0_ffn_U_{g}"]).then_inc(s_par, 16)
                sp.dma_start(wv[:, n, :], args[f"L0_ffn_V_{g}"]).then_inc(s_par, 16)
                sp.dma_start(bias[:, n:n + 1], column(args[f"L0_ffn_b_{g}"])).then_inc(s_par, 16)

        @block.gpsimd
        def _(pool):
            pool.memset(hs[:, 0:1, :], 0.0).then_inc(s_zero, 1)
            pool.memset(hc[:, :], 0.0).then_inc(s_zero, 1)
            rows = index[:, :, :, :].rearrange("p t b s -> p (t b s)")
            with pool.Fori(0, (TILES - IMG) // 2) as p:
                for k in range(2):
                    pool.wait_ge(s_sum[k], START + p)
                    pool.sem_inc(s_begun, 1)
                    pool.tensor_copy(own[k][:, :], rows[:, bass.ds((2 * p + k + IMG) * GT, GT)]).then_inc(s_own, 1)
                    pool.wait_ge(s_own, START + 2 * p + k + 1)
                    pool.sem_inc(s_begun, 1)
                    for s in range(GT):
                        pool.indirect_dma_start(samples[k][:, s * CELL:(s + 1) * CELL], None, table[:, :],
                                                bass.IndirectOffsetOnAxis(ap=own[k][:, s:s + 1], axis=0)).then_inc(s_got[k][s // PER], 16)

        @block.tensor
        def _(pe):
            def steps(t, at, u):
                bank = core.bank[4 + u % 2]
                pe.matmul(bank[:, 0:W], core.ident[:, :], gx[:, bass.ds(at, 1), :].rearrange("c o w -> c (o w)"), start=True, stop=False)
                pe.wait_ge(s_h, START + t)
                for g in range(NG):
                    mm = pe.matmul(bank[:, g * IMG:(g + 1) * IMG], wv[:, g, :], hs[:, bass.ds(at, 1), :].rearrange("c o w -> c (o w)"),
                                   start=False, stop=(g == NG - 1))
                mm.then_inc(s_pre, 1)

            def tile(j, p, k):
                q = (j - 1) * (IMG // 2) + p
                pe.wait_ge(s_sum[k], START + q + 1)
                pe.transpose(core.bank[6][:, k * TILE:(k + 1) * TILE], summed[k][:, :], core.ident[:, :]).then_inc(s_turn, 1)
                pe.wait_ge(s_copy, START + 2 * q + k + 1)
                pe.matmul(core.bank[7][:, k * TILE:(k + 1) * TILE], w_out[:, :], turned[k][:, :], start=True, stop=True).then_inc(s_out, 1)

            def finish(j):
                pe.wait_ge(s_end, START + IMG * j)
                norm.tensor(pe, j, [phase_half(j, h) for h in range(2)])
                for h in range(2):
                    pe.wait_ge(norm.s_out, START + norm.ready(j, h))
                    for g in range(NG):
                        m = NG * h + g
                        pe.wait_ge(s_gx, START + NM * j + max(0, m - 3))
                        pe.matmul(core.bank[4 + m % 4][:, :], wu[:, g, :], v[:, h * HALF:(h + 1) * HALF], start=True, stop=True).then_inc(s_gmm, 1)
                pe.wait_ge(s_gx, START + NM * (j + 1))
                pe.wait_ge(s_carry, START + j)

            pe.wait_ge(s_par, START + 16 * NPAR)
            pe.wait_ge(s_half, START + 2)
            pe.wait_ge(s_zero, START + 2)
            slots(pe, steps, tile, finish)

        @block.scalar
        def _(act):
            def steps(t, at, u):
                act.wait_ge(s_pre, START + t + 1)
                act.activation(gates[:, :], core.bank[4 + u % 2][:, 0:W], ACT.Tanh).then_inc(s_tanh, 1)
                act.wait_ge(s_cell, START + t + 1)
                act.activation(tc[:, :], cell[:, :], ACT.Tanh).then_inc(s_tc, 1)

            def tile(j, p, k):
                act.wait_ge(s_turn, START + 2 * ((j - 1) * (IMG // 2) + p) + k + 1)
                act.activation(turned[k][:, :], core.bank[6][:, k * TILE:(k + 1) * TILE], ACT.Copy).then_inc(s_copy, 1)

            def finish(j):
                norm.scalar(act, j, 1e-5)
                for h in range(2):
                    for g, (_, scale) in enumerate(GATES):
                        m = NG * h + g
                        act.wait_ge(s_gmm, START + NM * j + m + 1)
                        act.activation(gx[:, :, g * IMG + 4 * h:g * IMG + 4 * h + 4].rearrange("c t b -> c b t"),
                                       core.bank[4 + m % 4][:, :].rearrange("c (b t) -> c b t", t=TILE), ACT.Identity,
                                       bias=bias[:, g:g + 1], scale=scale).then_inc(s_gx, 1)

            act.wait_ge(s_half, START + 2)
            slots(act, steps, tile, finish)

        @block.vector
        def _(dve):
            def steps(t, at, u):
                dve.wait_ge(s_tanh, START + t + 1)
                dve.scalar_tensor_tensor(out=ig[:, :], in0=gates[:, 0:IMG], scalar=1.0, in1=gates[:, 2 * IMG:W], op0=ALU.add, op1=ALU.mult).then_inc(s_ig, 1)
                dve.tensor_scalar(og[:, :], gates[:, IMG:2 * IMG], 0.5, 0.5, ALU.mult, ALU.add).then_inc(s_og, 1)
                dve.wait_ge(s_hc, START + t)
                dve.wait_ge(s_ig, START + t + 1)
                dve.scalar_tensor_tensor(out=cell[:, :], in0=ig[:, :], scalar=0.5, in1=hc[:, :], op0=ALU.mult, op1=ALU.add).then_inc(s_cell, 1)
                dve.wait_ge(s_og, START + t + 1)
                dve.wait_ge(s_tc, START + t + 1)
                now = hs[:, bass.ds(at + 1, 1), :].rearrange("c o w -> c (o w)")
                dve.tensor_tensor(now, og[:, :], tc[:, :], ALU.mult).then_inc(s_h, 1)
                dve.wait_ge(s_h, START + t + 1)
                dve.tensor_tensor(hc[:, :], now, cell[:, :], ALU.mult).then_inc(s_hc, 1)

            def tile(j, p, k):
                q = (j - 1) * (IMG // 2) + p
                for s in range(NS):
                    dve.wait_ge(s_got[k][s], 16 * PER * (q + 1))
                by_value = samples[k][:, :].rearrange("p (s c) -> p s c", c=GC)
                flat = weight[:, :, :, :, :].rearrange("p t b s k -> p (t b s k)")
                w = flat[:, bass.ds((2 * q + k + IMG) * (GT * CORNERS), GT * CORNERS)].rearrange("p (s c) -> p s c", c=1).broadcast_to([TILE, GT * CORNERS, GC])
                dve.tensor_tensor(by_value, by_value, w, ALU.mult).then_inc(s_weighted, 1)
                dve.wait_ge(s_weighted, START + 2 * q + k + 1)
                dve.tensor_reduce(summed[k][:, :].rearrange("p (g c) -> p g c", g=G), samples[k][:, :].rearrange("p (g s c) -> p g c s", g=G, c=GC), AX.X, ALU.add).then_inc(s_sum[k], 1)
                xs = X[:, bass.ds((2 * p + k) * PIX + j * TILE, TILE)]
                dve.wait_ge(s_out, START + 2 * q + k + 1)
                dve.scalar_tensor_tensor(out=xs, in0=core.bank[7][:, k * TILE:(k + 1) * TILE], scalar=b_out[:, 0:1], in1=xs, op0=ALU.add, op1=ALU.add).then_inc(s_end, 1)

            def add_hidden(j):
                dve.wait_ge(s_h, START + TILE * (j + 1))
                xs = tokens[:, :, bass.ds(j, 1), :].rearrange("c b j t -> c b (j t)")
                dve.tensor_tensor(xs, xs, hs[:, 1:TILE + 1, :].rearrange("c t b -> c b t"), ALU.add).then_inc(s_x, 1)
                dve.tensor_copy(hs[:, 0:1, :], hs[:, TILE:TILE + 1, :]).then_inc(s_carry, 1)

            def finish(j):
                if not isinstance(j, int):
                    add_hidden(j - 1)
                dve.wait_ge(s_end, START + IMG * j)
                norm.vector(dve, j, [phase_half(j, h) for h in range(2)], [v3[:, 4 * h:4 * h + 4] for h in range(2)], TILE)

            dve.wait_ge(s_par, START + 16 * NPAR)
            dve.tensor_scalar(wv[:, 0:2, :], wv[:, 0:2, :], 0.5, None, ALU.mult).then_inc(s_half, 1)
            dve.tensor_scalar(bias[:, 0:2], bias[:, 0:2], 0.5, None, ALU.mult).then_inc(s_half, 1)
            dve.wait_ge(s_zero, START + 2)
            slots(dve, steps, tile, finish)
            add_hidden(TPI - 1)
    norm.done()


def divisive_mixer(core, args):
    nc, norm, X = core.nc, core.norm, core.x
    G = 8
    with ExitStack() as mem:
        v = core.sb(mem, "dv_v", [C, PIX])
        v2 = core.sb(mem, "dv_squares", [C, PAD, PAD])
        pool_w = core.sb(mem, "dv_pool_w", [C, C])
        taps = core.sb(mem, "dv_taps", [C, 9])
        vecs = core.sb(mem, "dv_vecs", [C, 3])
        beta = core.sb(mem, "dv_beta", [C, 1])
        acc = core.sb(mem, "dv_acc", [C, PIX])
        s_zero, s_par, s_beta, s_v2, s_pool, s_acc, s_den, s_log, s_rsqrt, s_end = (
            core.sem(f"dv_{n}") for n in ("zero", "params", "beta", "squares", "pooled", "acc", "den", "log", "rsqrt", "end"))
        TAPS = [t for t in range(9) if t != 4]
        NACC = len(TAPS) + 1
        NPAR = 4 + C // G
        acc3 = acc[:, :].rearrange("c (r w) -> c r w", w=COLS)
        v3 = v[:, :].rearrange("c (r w) -> c r w", w=COLS)
        core.start_counts()
        with nc.Block() as block:
            @block.gpsimd
            def _(pool):
                pool.memset(pool_w[:, :], 0.0).then_inc(s_zero, 1)
                pool.memset(v2[:, :, :], 0.0).then_inc(s_zero, 1)
                pool.wait_ge(s_par, START + 16 * NPAR)
                pool.tensor_scalar(beta[:, :], vecs[:, 0:1], 1e-6, None, ALU.add).then_inc(s_beta, 1)

            @block.sync
            def _(sp):
                sp.dma_start(taps[:, :], args["L1_conv_gamma_s"].rearrange("a b c o -> c (a b o)"), allow_slow_non_contiguous=True).then_inc(s_par, 16)
                for n, name in enumerate(("beta", "gamma_outside", "beta_outside")):
                    sp.dma_start(vecs[:, n:n + 1], column(args[f"L1_conv_{name}"])).then_inc(s_par, 16)
                sp.wait_ge(s_zero, START + 1)
                for g in range(C // G):
                    sp.dma_start(pool_w[G * g:G * g + G, G * g:G * g + G], args["L1_conv_gamma_k"][0, 0, :, G * g:G * g + G]).then_inc(s_par, 16)

            @block.tensor
            def _(pe):
                pe.wait_ge(s_par, START + 16 * NPAR)

                def pool_squares(b):
                    pe.wait_ge(s_den, START + b)
                    pe.wait_ge(s_v2, START + b + 1)
                    for h in range(2):
                        mm = pe.matmul(image(core.bank[4 + h]), pool_w[:, :], inner(v2, h), start=True, stop=True)
                    mm.then_inc(s_pool, 1)

                ahead(pe, IMG, lambda b: None, lambda b: norm.tensor(pe, b, x_halves(core, b)), pool_squares)

            @block.scalar
            def _(act):
                act.preload_act_table_set(LOG_EXP)
                act.wait_ge(s_zero, START + 2)
                act.wait_ge(s_beta, START + 1)

                def squares(b):
                    act.wait_ge(norm.s_out, START + norm.ready(b, 1))
                    act.wait_ge(s_pool, START + b)
                    act.wait_ge(s_acc, START + NACC * b)
                    act.activation(v2[:, 1:1 + ROWS, 1:1 + COLS], v3, ACT.Square).then_inc(s_v2, 1)

                def rsqrt(b):
                    act.wait_ge(s_den, START + b + 1)
                    act.activation(acc[:, :], acc[:, :], ACT.Ln, bias=beta[:, 0:1]).then_inc(s_log, 1)
                    act.wait_ge(s_log, START + b + 1)
                    act.activation(acc[:, :], acc[:, :], ACT.Exp, scale=-0.5).then_inc(s_rsqrt, 1)

                ahead(act, IMG, squares, lambda b: norm.scalar(act, b, 1e-6), rsqrt)

            @block.vector
            def _(dve):
                dve.wait_ge(s_par, START + 16 * NPAR)

                def normalise(b):
                    dve.wait_ge(s_end, START + 2 * b)
                    norm.finish(dve, b, [v3[:, 0:HROWS], v3[:, HROWS:ROWS]])

                def surround_and_sum(b):
                    dve.wait_ge(s_v2, START + b + 1)
                    for n, t in enumerate(TAPS):
                        win = v2[:, t // 3:t // 3 + ROWS, t % 3:t % 3 + COLS]
                        if n == 0:
                            dve.tensor_scalar(acc3, win, taps[:, t:t + 1], None, ALU.mult).then_inc(s_acc, 1)
                            continue
                        dve.wait_ge(s_acc, START + NACC * b + n)
                        dve.scalar_tensor_tensor(out=acc3, in0=win, scalar=taps[:, t:t + 1], in1=acc3, op0=ALU.mult, op1=ALU.add).then_inc(s_acc, 1)
                    dve.wait_ge(s_acc, START + NACC * b + len(TAPS))
                    dve.wait_ge(s_pool, START + b + 1)
                    dve.tensor_tensor(acc[:, 0:HALF], acc[:, 0:HALF], core.bank[4][:, :], ALU.add).then_inc(s_acc, 1)
                    dve.tensor_tensor(acc[:, HALF:PIX], acc[:, HALF:PIX], core.bank[5][:, :], ALU.add).then_inc(s_den, 1)
                    dve.wait_ge(s_rsqrt, START + b + 1)
                    dve.scalar_tensor_tensor(out=acc[:, :], in0=v[:, :], scalar=vecs[:, 1:2], in1=acc[:, :], op0=ALU.mult, op1=ALU.mult).then_inc(s_end, 1)
                    dve.wait_ge(s_end, START + 2 * b + 1)
                    xs = X[:, bass.ds(b * PIX, PIX)]
                    dve.scalar_tensor_tensor(out=xs, in0=acc[:, :], scalar=vecs[:, 2:3], in1=xs, op0=ALU.add, op1=ALU.add).then_inc(s_end, 1)

                ahead(dve, IMG, normalise, lambda b: norm.centre(dve, b, x_halves(core, b)), surround_and_sum)
        norm.done()


def routed_depth_ffn(core, args):
    nc, norm, X = core.nc, core.norm, core.x
    HID = args["L1_ffn_w1"].shape[1]
    NHC = HID // C
    CHOSEN = PIX // 2 - 1
    with ExitStack() as mem:
        v = core.sb(mem, "rd_v", [C, TOK])
        half = lambda b, h: v[:, bass.ds(b * PIX + h * HALF, HALF)]
        wr = core.sb(mem, "rd_wr", [C, 1])
        wr_wide = core.sb(mem, "rd_wr_wide", [C, C])
        br = core.sb(mem, "rd_br", [C, 1])
        w1 = core.sb(mem, "rd_w1", [C, HID])
        w2 = core.sb(mem, "rd_w2", [C, NHC, C])
        b1 = core.sb(mem, "rd_b1", [C, NHC])
        b2 = core.sb(mem, "rd_b2", [C, 1])
        ones = core.sb(mem, "rd_ones", [C, C], BF16)
        before = core.sb(mem, "rd_before", [C, C])
        weight = core.sb(mem, "rd_weight", [C, PIX])
        wcol = core.sb(mem, "rd_weight_col", [C, TPI])
        diag = core.sb(mem, "rd_diag", [C, TILE])
        equal = core.sb(mem, "rd_equal", [C, TILE])
        less = core.sb(mem, "rd_less", [C, TILE])
        precedes = core.sb(mem, "rd_ahead", [C, TPI, PIX], BF16)
        coef = core.sb(mem, "rd_coef", [C, PIX])
        hid = [core.sb(mem, f"rd_hidden{k}", [C, HALF]) for k in range(2)]
        y = [core.sb(mem, f"rd_y{h}", [C, HALF]) for h in range(2)]
        (s_par, s_const, s_wide, s_wmm, s_weight, s_diag, s_tie, s_ahead, s_rank, s_coef, s_h1, s_hid, s_y, s_ysum, s_end) = (
            core.sem(f"rd_{n}") for n in ("params", "const", "wide", "weight_product", "weight", "weight_col", "ties", "ahead", "rank",
                                          "coef", "hidden_product", "hidden", "y_product", "y_weighted", "end"))
        NPAR = 5 + NHC
        NH1 = 2 * NHC
        core.start_counts()
        with nc.Block() as block:
            @block.sync
            def _(sp):
                sp.dma_start(wr[:, :], args["L1_ffn_wr"]).then_inc(s_par, 16)
                sp.dma_start(br[:, :], args["L1_ffn_br"].rearrange("(a o) -> a o", o=1).broadcast_to([C, 1])).then_inc(s_par, 16)
                sp.dma_start(w1[:, :], args["L1_ffn_w1"]).then_inc(s_par, 16)
                sp.dma_start(w2[:, :, :], args["L1_ffn_w2"].rearrange("(k p) d -> p k d", p=C)).then_inc(s_par, 16)
                sp.dma_start(b2[:, :], column(args["L1_ffn_b2"])).then_inc(s_par, 16)
                for k in range(NHC):
                    sp.dma_start(b1[:, k:k + 1], column(args["L1_ffn_b1"][k * C:(k + 1) * C])).then_inc(s_par, 16)

            @block.gpsimd
            def _(pool):
                pool.memset(ones[:, :], 1.0).then_inc(s_const, 1)
                pool.memset(before[:, :], 1.0).then_inc(s_const, 1)
                pool.wait_ge(s_const, START + 2)
                pool.affine_select(out=before[:, :], in_=before[:, :], compare_op=ALU.is_gt, fill=0.0,
                                   base=0, pattern=[[1, C]], channel_multiplier=-1).then_inc(s_const, 1)

            @block.tensor
            def _(pe):
                pe.wait_ge(s_par, START + 16 * NPAR)
                pe.wait_ge(s_wide, START + 1)
                pe.wait_ge(s_const, START + 3)

                def hidden_product(b, h, k):
                    m = NHC * h + k
                    pe.wait_ge(s_hid, START + NH1 * b + max(0, m - 1))
                    pe.matmul(core.bank[6 + m % 2][:, :], w1[:, k * C:(k + 1) * C], half(b, h), start=True, stop=True).then_inc(s_h1, 1)

                def weights(b):
                    for h in range(2):
                        pe.wait_ge(s_weight, START + 2 * b)
                        pe.matmul(core.bank[2 + h][:, :], wr_wide[:, :], half(b, h), start=True, stop=True).then_inc(s_wmm, 1)
                    hidden_product(b, 0, 0)
                    hidden_product(b, 0, 1)

                def outputs_and_ranks(b):
                    pe.wait_ge(s_ysum, START + 2 * b)
                    for h in range(2):
                        for k in range(NHC):
                            m = NHC * h + k
                            pe.wait_ge(s_hid, START + NH1 * b + m + 1)
                            pe.matmul(core.bank[4 + h][:, :], w2[:, k, :], hid[m % 2][:, :], start=(k == 0), stop=(k == NHC - 1)).then_inc(s_y, 1)
                            if m + 2 < NH1:
                                hidden_product(b, *divmod(m + 2, NHC))
                    pe.wait_ge(s_coef, START + 2 * b)
                    pe.wait_ge(s_ahead, START + TPI * (b + 1))
                    for h in range(2):
                        for j in range(TPI):
                            mm = pe.matmul(core.bank[h][:, :], ones[:, :], precedes[:, j, h * HALF:(h + 1) * HALF], start=(j == 0), stop=(j == TPI - 1))
                        mm.then_inc(s_rank, 1)

                ahead(pe, IMG, lambda b: None, lambda b: norm.tensor(pe, b, x_halves(core, b)), lambda b: None)
                pe.wait_ge(norm.s_out, START + norm.ready(IMG - 1, 1))
                with pe.Fori(0, IMG) as b:
                    weights(b)
                    outputs_and_ranks(b)

            @block.scalar
            def _(act):
                act.wait_ge(s_par, START + 16 * NPAR)

                act.preload_act_table_set(LOG_EXP)
                with act.Fori(0, IMG) as b:
                    norm.scalar(act, b, 1e-5)
                act.preload_act_table(ACT.Gelu_apprx_tanh)
                with act.Fori(0, IMG) as b:
                    act.wait_ge(s_coef, START + 2 * b)
                    for h in range(2):
                        act.wait_ge(s_wmm, START + 2 * b + h + 1)
                        act.activation(weight[:, h * HALF:(h + 1) * HALF], core.bank[2 + h][:, :], ACT.Identity, bias=br[:, 0:1]).then_inc(s_weight, 1)
                    for m in range(NH1):
                        act.wait_ge(s_h1, START + NH1 * b + m + 1)
                        act.wait_ge(s_y, START + NH1 * b + max(0, m - 1))
                        act.activation(hid[m % 2][:, :], core.bank[6 + m % 2][:, :], ACT.Gelu_apprx_tanh, bias=b1[:, m % NHC:m % NHC + 1]).then_inc(s_hid, 1)

            @block.vector
            def _(dve):
                dve.wait_ge(s_par, START + 16 * NPAR)
                dve.tensor_copy(wr_wide[:, :], wr[:, 0:1].broadcast_to([C, C])).then_inc(s_wide, 1)
                dve.wait_ge(s_const, START + 3)
                ahead(dve, IMG, lambda b: norm.finish(dve, b, [image(half(b, h)) for h in range(2)]), lambda b: norm.centre(dve, b, x_halves(core, b)), lambda b: None)
                dve.wait_ge(norm.s_out, START + norm.ready(IMG - 1, 1))
                with dve.Fori(0, IMG) as b:
                    dve.wait_ge(s_weight, START + 2 * b + 2)
                    dve.wait_ge(s_rank, START + 2 * b)
                    for j in range(TPI):
                        own = weight[:, j * TILE:(j + 1) * TILE]
                        me = wcol[:, j:j + 1]
                        if j:
                            dve.wait_ge(s_diag, START + TPI * b + j)
                        dve.scalar_tensor_tensor(out=diag[:, :], in0=own, scalar=1.0, in1=core.ident[:, :], op0=ALU.mult, op1=ALU.mult, accum_out=me).then_inc(s_diag, 1)
                        dve.wait_ge(s_diag, START + TPI * b + j + 1)
                        if j:
                            dve.tensor_scalar(precedes[:, j, 0:j * TILE], weight[:, 0:j * TILE], me, None, ALU.is_lt)
                        if j + 1 < TPI:
                            dve.tensor_scalar(precedes[:, j, (j + 1) * TILE:PIX], weight[:, (j + 1) * TILE:PIX], me, None, ALU.is_le)
                        dve.scalar_tensor_tensor(out=equal[:, :], in0=own, scalar=me, in1=before[:, :], op0=ALU.is_equal, op1=ALU.mult).then_inc(s_tie, 1)
                        dve.wait_ge(s_tie, START + TPI * b + j + 1)
                        dve.scalar_tensor_tensor(out=precedes[:, j, j * TILE:(j + 1) * TILE], in0=own, scalar=me, in1=equal[:, :], op0=ALU.is_lt, op1=ALU.add).then_inc(s_ahead, 1)
                    for h in range(2):
                        dve.wait_ge(s_rank, START + 2 * b + h + 1)
                        dve.scalar_tensor_tensor(out=coef[:, h * HALF:(h + 1) * HALF], in0=core.bank[h][:, :], scalar=float(CHOSEN), in1=weight[:, h * HALF:(h + 1) * HALF],
                                                 op0=ALU.is_lt, op1=ALU.mult).then_inc(s_coef, 1)
                    for h in range(2):
                        xs = X[:, bass.ds(b * PIX + h * HALF, HALF)]
                        dve.wait_ge(s_y, START + NH1 * b + NHC * (h + 1))
                        dve.wait_ge(s_coef, START + 2 * b + h + 1)
                        dve.scalar_tensor_tensor(out=y[h][:, :], in0=core.bank[4 + h][:, :], scalar=b2[:, 0:1], in1=coef[:, h * HALF:(h + 1) * HALF],
                                                 op0=ALU.add, op1=ALU.mult).then_inc(s_ysum, 1)
                        dve.tensor_tensor(xs, xs, half(b, h), ALU.add).then_inc(s_end, 1)
                        dve.wait_ge(s_ysum, START + 2 * b + h + 1)
                        dve.wait_ge(s_end, START + 2 * b + h + 1)
                        dve.tensor_tensor(xs, xs, y[h][:, :], ALU.add)
        norm.done()


def scan_mixer(core, args):
    nc, norm, X = core.nc, core.norm, core.x
    GROUPS = 4
    GC = COLS // GROUPS
    RL, IL = ROWS + 1, IMG + 1
    PC = ROWS * GC
    PAIRS = IMG // 2
    NW = 5
    LAM, OUT = 1, 3
    with ExitStack() as mem:
        v = core.sb(mem, "ss_v", [C, TOK])
        vg = v[:, :].rearrange("c (i r w) -> c i r w", r=ROWS, w=COLS)
        w_all = core.sb(mem, "ss_w_all", [C, 3 * C])
        wide = core.sb(mem, "ss_w_wide", [C, NW, C])
        bias = core.sb(mem, "ss_bias", [C, NW])
        out_w = core.sb(mem, "ss_out_w", [C, C])
        vecs = core.sb(mem, "ss_vecs", [C, 3])
        by_rows = lambda name: core.sb(mem, name, [C, IMG, GC, RL])
        by_images = lambda name: core.sb(mem, name, [C, ROWS, GC, IL])
        inp = by_rows("ss_inp")
        lam = [by_rows(f"ss_lam{d}") for d in range(2)]
        og = [by_rows(f"ss_out_gate{d}") for d in range(2)]
        feed, fwd, rev = by_rows("ss_feed"), by_rows("ss_fwd"), by_rows("ss_rev")
        lam_i, feed_i, fwd_i, rev_i = (by_images(f"ss_{n}_i") for n in ("lam", "feed", "fwd", "rev"))
        sig = core.sb(mem, "ss_sigmoid", [C, HALF])
        y = core.sb(mem, "ss_y", [C, PIX])
        y3 = y[:, :].rearrange("c (r w) -> c r w", w=COLS)
        flat = lambda t: t[:, :, :, :].rearrange("c a b l -> c (a b l)")
        back = lambda t: flat(t)[:, ::-1]
        (s_par, s_zero, s_wide, s_mm, s_act, s_inp, s_feed, s_feed_i, s_lam_i, s_rows, s_rows_sum, s_images, s_images_sum,
         s_sum, s_prod, s_group, s_affine, s_omm, s_end) = (core.sem(f"ss_{n}") for n in (
            "params", "zero", "wide", "products", "gates", "inp", "feed", "feed_by_images", "lam_by_images", "row_scans", "row_sums",
            "image_scans", "image_sums", "state", "gated", "group", "affine", "out_product", "end"))
        NPAR = 6 + 8
        core.start_counts()
        with nc.Block() as block:
            @block.sync
            def _(sp):
                sp.dma_start(w_all[:, :], args["L2_conv_in_w"]).then_inc(s_par, 16)
                sp.dma_start(out_w[:, :], args["L2_conv_out_w"]).then_inc(s_par, 16)
                for n, name in enumerate(("gamma", "beta", "out_b")):
                    sp.dma_start(vecs[:, n:n + 1], column(args[f"L2_conv_{name}"])).then_inc(s_par, 16)
                in_b = args["L2_conv_in_b"]
                sp.dma_start(bias[:, 0:1], column(in_b[0:C])).then_inc(s_par, 16)
                for d in range(2):
                    for e in range(2):
                        sp.dma_start(bias[e:C:2, OUT + d:OUT + d + 1], column(in_b[C + d:2 * C:2]), allow_slow_non_contiguous=True).then_inc(s_par, 16)
                        sp.dma_start(bias[e:C:2, LAM + d:LAM + d + 1], column(in_b[2 * C + d:3 * C:2]), allow_slow_non_contiguous=True).then_inc(s_par, 16)

            @block.gpsimd
            def _(pool):
                for t in (inp, *lam, *og, feed, fwd, rev, lam_i, feed_i, fwd_i, rev_i):
                    pool.memset(flat(t), 0.0).then_inc(s_zero, 1)
                for q in range(GROUPS):
                    for d in range(2):
                        n = 2 * q + d
                        pool.wait_ge(s_images, START + n)
                        pool.wait_ge(s_act, START + NW * PAIRS * (q + 1))
                        pool.tensor_copy(lam_i[:, :, :, 0:IMG], lam[d][:, :, :, 0:ROWS].rearrange("c i w r -> c r w i")).then_inc(s_lam_i, 1)
                        pool.wait_ge(s_rows, START + n + 1)
                        pool.tensor_tensor(flat(fwd), flat(fwd), flat(rev), ALU.add).then_inc(s_rows_sum, 1)
                        pool.wait_ge(s_images, START + n + 1)
                        pool.tensor_tensor(flat(fwd_i), flat(fwd_i), flat(rev_i), ALU.add).then_inc(s_images_sum, 1)

            @block.tensor
            def _(pe):
                with pe.Fori(0, IMG) as b:
                    norm.tensor(pe, b, [X[:, bass.ds(o, HALF)] for o in halves(b)])
                pe.wait_ge(norm.s_out, START + norm.ready(IMG - 1, 1))
                pe.wait_ge(s_wide, START + NW)
                with pe.Fori(0, GROUPS) as q:
                    for p in range(PAIRS):
                        pe.wait_ge(s_act, START + NW * (PAIRS * q + p))
                        pe.wait_ge(s_inp, START + PAIRS * q + p)
                        for w in range(NW):
                            for i in range(2):
                                mm = pe.matmul(core.bank[w][:, i * PC:(i + 1) * PC].rearrange("c (r w) -> c r w", w=GC), wide[:, w, :],
                                               vg[:, 2 * p + i, :, bass.ds(q * GC, GC)], start=True, stop=True)
                            mm.then_inc(s_mm, 1)
                pe.wait_ge(s_group, START + GROUPS)
                norm.done()
                with pe.Fori(0, IMG) as b:
                    norm.tensor(pe, b, [v[:, bass.ds(o, HALF)] for o in halves(b)])
                    pe.wait_ge(s_end, START + 2 * b)
                    for h in range(2):
                        pe.wait_ge(s_affine, START + 2 * b + h + 1)
                        pe.matmul(core.bank[4 + h][:, :], out_w[:, :], y[:, h * HALF:(h + 1) * HALF], start=True, stop=True).then_inc(s_omm, 1)
                norm.base -= 2 * IMG

            @block.scalar
            def _(act):
                act.preload_act_table_set(LOG_EXP)
                with act.Fori(0, IMG) as b:
                    norm.scalar(act, b, 1e-6)
                act.wait_ge(s_zero, START + 12)
                act.wait_ge(s_par, START + 16 * NPAR)
                act.preload_act_table(ACT.Sigmoid)
                with act.Fori(0, GROUPS) as q:
                    act.wait_ge(s_group, START + q)
                    for p in range(PAIRS):
                        for w in range(NW):
                            m = NW * (PAIRS * q + p) + w
                            act.wait_ge(s_mm, START + m + 1)
                            if w == 0:
                                act.wait_ge(s_inp, START + PAIRS * q + p)
                                act.activation(sig[:, :], core.bank[0][:, :], ACT.Sigmoid, bias=bias[:, 0:1]).then_inc(s_act, 1)
                                continue
                            dst = (*lam, *og)[w - 1][:, 2 * p:2 * p + 2, :, 0:ROWS]
                            act.activation(dst, core.bank[w][:, :].rearrange("c (i r w) -> c i w r", i=2, w=GC), ACT.Sigmoid, bias=bias[:, w:w + 1]).then_inc(s_act, 1)
                    for d in range(2):
                        act.wait_ge(s_images, START + 2 * q + d)
                        act.wait_ge(s_feed, START + 2 * q + d + 1)
                        act.activation(feed_i[:, :, :, 0:IMG], feed[:, :, :, 0:ROWS].rearrange("c i w r -> c r w i"), ACT.Copy).then_inc(s_feed_i, 1)
                norm.done()
                act.preload_act_table_set(LOG_EXP)
                with act.Fori(0, IMG) as b:
                    norm.scalar(act, b, 1e-5)
                    for h in range(2):
                        half = y[:, h * HALF:(h + 1) * HALF]
                        act.wait_ge(norm.s_out, START + norm.ready(b, h))
                        act.activation(half, half, ACT.Identity, bias=vecs[:, 1:2], scale=vecs[:, 0:1]).then_inc(s_affine, 1)
                norm.base -= 2 * IMG

            @block.vector
            def _(dve):
                dve.wait_ge(s_par, START + 16 * NPAR)
                dve.tensor_copy(wide[:, 0, :], w_all[:, 0:C]).then_inc(s_wide, 1)
                for d in range(2):
                    for w, at in ((LAM + d, 2 * C + d), (OUT + d, C + d)):
                        src = w_all[:, at:at - d + C:2].rearrange("c (n e) -> c n e", e=1).broadcast_to([C, C // 2, 2])
                        dve.tensor_copy(wide[:, w, :].rearrange("c (n e) -> c n e", e=2), src).then_inc(s_wide, 1)
                with dve.Fori(0, IMG) as b:
                    norm.vector(dve, b, [X[:, bass.ds(o, HALF)] for o in halves(b)],
                                [v[:, bass.ds(o, HALF)].rearrange("c (r w) -> c r w", w=COLS) for o in halves(b)])
                dve.wait_ge(s_zero, START + 12)
                with dve.Fori(0, GROUPS) as q:
                    for p in range(PAIRS):
                        dve.wait_ge(s_act, START + NW * (PAIRS * q + p) + 1)
                        for i in range(2):
                            at = slice(i * PC, (i + 1) * PC)
                            ins = dve.scalar_tensor_tensor(out=inp[:, 2 * p + i, :, 0:ROWS].rearrange("c w r -> c r w"),
                                                           in0=core.bank[0][:, at].rearrange("c (r w) -> c r w", w=GC), scalar=bias[:, 0:1],
                                                           in1=sig[:, at].rearrange("c (r w) -> c r w", w=GC), op0=ALU.add, op1=ALU.mult)
                        ins.then_inc(s_inp, 1)
                    dve.wait_ge(s_inp, START + PAIRS * (q + 1))
                    dve.wait_ge(s_act, START + NW * PAIRS * (q + 1))
                    for d in range(2):
                        n = 2 * q + d
                        dve.wait_ge(s_feed_i, START + n)
                        dve.scalar_tensor_tensor(out=flat(feed), in0=flat(lam[d]), scalar=1.0, in1=flat(inp), op0=ALU.subtract, op1=ALU.mult).then_inc(s_feed, 1)
                        dve.wait_ge(s_feed, START + n + 1)
                        dve.wait_ge(s_prod, START + n)
                        dve.tensor_tensor_scan(flat(fwd), flat(lam[d]), flat(feed), 0.0, ALU.mult, ALU.subtract)
                        dve.tensor_tensor_scan(back(rev), back(lam[d]), back(feed), 0.0, ALU.mult, ALU.subtract).then_inc(s_rows, 1)
                        dve.wait_ge(s_feed_i, START + n + 1)
                        dve.wait_ge(s_lam_i, START + n + 1)
                        dve.tensor_tensor_scan(flat(fwd_i), flat(lam_i), flat(feed_i), 0.0, ALU.mult, ALU.subtract)
                        dve.tensor_tensor_scan(back(rev_i), back(lam_i), back(feed_i), 0.0, ALU.mult, ALU.subtract).then_inc(s_images, 1)
                        dve.wait_ge(s_rows_sum, START + n + 1)
                        dve.wait_ge(s_images_sum, START + n + 1)
                        state = fwd[:, :, :, 0:ROWS]
                        dve.tensor_tensor(state, state, fwd_i[:, :, :, 0:IMG].rearrange("c r w i -> c i w r"), ALU.add).then_inc(s_sum, 1)
                        dve.wait_ge(s_sum, START + n + 1)
                        dve.tensor_tensor(flat(og[d]), flat(og[d]), flat(fwd), ALU.mult).then_inc(s_prod, 1)
                    dve.wait_ge(s_prod, START + 2 * q + 2)
                    dve.tensor_tensor(vg[:, :, :, bass.ds(q * GC, GC)].rearrange("c i r w -> c i w r"), og[0][:, :, :, 0:ROWS], og[1][:, :, :, 0:ROWS], ALU.add).then_inc(s_group, 1)
                dve.wait_ge(s_group, START + GROUPS)
                norm.done()
                with dve.Fori(0, IMG) as b:
                    dve.wait_ge(s_omm, START + 2 * b)
                    norm.vector(dve, b, [v[:, bass.ds(o, HALF)] for o in halves(b)], [y3[:, 0:HROWS], y3[:, HROWS:ROWS]])
                    for h in range(2):
                        xs = X[:, bass.ds(b * PIX + h * HALF, HALF)]
                        dve.wait_ge(s_omm, START + 2 * b + h + 1)
                        dve.scalar_tensor_tensor(out=xs, in0=core.bank[4 + h][:, :], scalar=vecs[:, 2:3], in1=xs, op0=ALU.add, op1=ALU.add).then_inc(s_end, 1)
                norm.base -= 2 * IMG
        norm.done(2)


class Grouped:

    PAIR = 2
    GROUP = 4

    def __init__(self, core, mem, name, gate_w, gate_b, hid):
        nc, self.core = core.nc, core
        self.E = E = gate_w.shape[1]
        self.gate_w, self.gate_b = gate_w, gate_b
        self.TILES = T = TOK // TILE
        self.BLOCKS = self.PAIR * T + E
        self.GROUPS = self.BLOCKS // self.GROUP
        assert self.BLOCKS % self.GROUP == 0 and T * E % HALF == 0
        rows = (self.BLOCKS * TILE, C)
        self.xs = nc.dram_tensor(f"{name}_slot_inputs", rows, F32).ap()
        self.ys = nc.dram_tensor(f"{name}_slot_outputs", rows, F32).ap()
        sb = lambda n, shape, dtype=F32: core.sb(mem, f"{name}_{n}", shape, dtype)
        self.w = sb("gate_w", [C, E])
        self.b = sb("gate_b", [TILE, E])
        self.v = sb("v", [C, PIX])
        self.rows = sb("rows", [TILE, TOK])
        self.p = sb("probs", [TILE, T * E])
        self.q = sb("scratch", [TILE, T * E])
        self.hot = [sb(f"hot{k}", [TILE, T * E]) for k in range(2)]
        self.both = sb("both", [TILE, T * E], BF16)
        self.order = sb("order", [TILE, E])
        self.top = sb("top", [TILE, T])
        self.share = sb("share", [TILE, T, self.PAIR])
        self.slot = sb("slot", [TILE, T, self.PAIR])
        self.index = sb("index", [TILE, T, self.PAIR], I32)
        self.limit_i = sb("limits_int", [TILE, self.BLOCKS], I32)
        self.limit = sb("limits", [TILE, self.BLOCKS])
        self.past = sb("past", [1, self.BLOCKS * E])
        self.expert = sb("expert", [1, self.BLOCKS])
        self.small = sb("small", [TILE, 4, E])
        self.ids = sb("ids", [1, 3, self.BLOCKS], I32)
        self.tri = sb("before", [TILE, TILE])
        self.tri16 = sb("before16", [TILE, TILE], BF16)
        self.ones16 = sb("ones16", [TILE, TILE], BF16)
        self.zero1 = sb("zero", [TILE, 1])
        self.xin = [sb(f"slots_in{k}", [TILE, self.GROUP, C]) for k in range(2)]
        self.yout = [sb(f"slots_out{k}", [TILE, self.GROUP, C]) for k in range(2)]
        self.own = [sb(f"own_index{k}", [TILE, self.GROUP * self.PAIR], I32) for k in range(2)]
        self.gathered = [sb(f"gathered{k}", [TILE, self.GROUP * self.PAIR * C]) for k in range(2)]
        self.xt = [sb(f"slots_t{k}", [C, TILE]) for k in range(2)]
        self.w1 = [sb(f"w1_of_block{k}", [C, hid]) for k in range(2)]
        (self.s_par, self.s_const, self.s_logit, self.s_logits, self.s_turn, self.s_rows, self.s_step, self.s_exp, self.s_both, self.s_count,
         self.s_index, self.s_ids, self.s_fill, self.s_stage, self.s_begun, self.s_own, self.s_t, self.s_xt, self.s_w1, self.s_h, self.s_act,
         self.s_hid, self.s_o, self.s_y) = (
            core.sem(f"{name}_{n}") for n in ("params", "const", "logit_products", "logits", "rows_turned", "rows_ready", "steps", "exp", "both",
                                              "counted", "index", "ids", "filled", "staged", "begun", "own_index", "slots_turned", "slots_t", "block_w1",
                                              "products", "activated", "hidden", "outputs", "outputs_out"))
        self.s_weighted, self.s_sum, self.s_end = ([core.sem(f"{name}_{n}{k}") for k in range(2)] for n in ("weighted", "summed", "end"))
        self.s_in = [core.sem(f"{name}_slots_in{k}") for k in range(2)]
        self.s_stored = [core.sem(f"{name}_stored{k}") for k in range(2)]
        self.s_scatter = [core.indirect_sem() for k in range(2)]
        self.s_got = [core.indirect_sem() for k in range(2)]

    NCONST = 6
    NIDS = 5

    def group_rows(self, dram, g):
        view = dram.rearrange("(g j p) c -> g p j c", j=self.GROUP, p=TILE)
        return view[g] if isinstance(g, int) else view[bass.ds(g, 1)].rearrange("o p j c -> p (o j) c")


    def load(self, sp):
        sp.dma_start(self.w[:, :], self.gate_w).then_inc(self.s_par, 16)
        sp.dma_start(self.b[:, :], self.gate_b.rearrange("(o e) -> o e", o=1).broadcast_to([TILE, self.E])).then_inc(self.s_par, 16)
        sp.wait_ge(self.s_const, START + self.NCONST)
        with sp.Fori(0, self.GROUPS) as g:
            sp.dma_start(self.group_rows(self.xs, g), self.xin[0][:, :, :]).then_inc(self.s_fill, 16)

    def constants(self, pool):
        pool.memset(self.xin[0][:, :, :], 0.0).then_inc(self.s_const, 1)
        pool.memset(self.ones16[:, :], 1.0).then_inc(self.s_const, 1)
        pool.memset(self.zero1[:, :], 0.0).then_inc(self.s_const, 1)
        pool.memset(self.tri[:, :], 1.0).then_inc(self.s_const, 1)
        pool.iota(self.limit_i[:, :], pattern=[[TILE, self.BLOCKS]], base=0, channel_multiplier=0).then_inc(self.s_const, 1)
        pool.wait_ge(self.s_const, START + 5)
        pool.affine_select(out=self.tri[:, :], in_=self.tri[:, :], compare_op=ALU.is_gt, fill=0.0,
                           base=0, pattern=[[1, TILE]], channel_multiplier=-1).then_inc(self.s_const, 1)
        for e in range(self.E):
            pool.memset(self.order[:, e:e + 1], float(self.E - e)).then_inc(self.s_const, 1)

    def route_tensor(self, pe, b, v):
        pe.wait_ge(self.s_logits, START + b)
        for j in range(TPI):
            mm = pe.matmul(self.core.bank[4][:, j * self.E:(j + 1) * self.E], v[:, j * TILE:(j + 1) * TILE], self.w[:, :], start=True, stop=True)
        mm.then_inc(self.s_logit, 1)

    def route_vector(self, dve, b):
        E = self.E
        dve.wait_ge(self.s_logit, START + b + 1)
        dve.tensor_tensor(self.p[:, bass.ds(b * (TPI * E), TPI * E)].rearrange("p (t e) -> p t e", e=E),
                          self.core.bank[4][:, 0:TPI * E].rearrange("p (t e) -> p t e", e=E),
                          self.b[:, :].rearrange("p (t e) -> p t e", t=1).broadcast_to([TILE, TPI, E]), ALU.add).then_inc(self.s_logits, 1)

    def rows_tensor(self, pe, b, src):
        for h in range(2):
            pe.wait_ge(self.s_rows, START + 2 * b)
            for j in range(4):
                mm = pe.transpose(self.core.bank[6 + h][:, j * TILE:(j + 1) * TILE], src[:, h * HALF + j * TILE:h * HALF + (j + 1) * TILE], self.core.ident[:, :])
            mm.then_inc(self.s_turn, 1)

    def rows_scalar(self, act, b):
        for h in range(2):
            act.wait_ge(self.s_turn, START + 2 * b + h + 1)
            act.activation(self.rows[:, bass.ds((2 * b + h) * HALF, HALF)], self.core.bank[6 + h][:, :], ACT.Copy).then_inc(self.s_rows, 1)


    def choose_scalar(self, act):
        act.wait_ge(self.s_step, START + 2)
        act.activation(self.p[:, :], self.p[:, :], ACT.Exp).then_inc(self.s_exp, 1)

    def choose_tensor(self, pe):
        pe.wait_ge(self.s_const, START + self.NCONST + self.E + 2)
        pe.wait_ge(self.s_rows, START + 2 * IMG)
        pe.wait_ge(self.s_both, START + 1)
        N = self.TILES * self.E // HALF
        for n in range(N):
            pe.matmul(self.core.bank[4 + n][:, :], self.tri16[:, :], self.both[:, n * HALF:(n + 1) * HALF], start=True, stop=True).then_inc(self.s_count, 1)
            pe.matmul(self.core.bank[6 + n][:, :], self.ones16[:, :], self.both[:, n * HALF:(n + 1) * HALF], start=True, stop=True).then_inc(self.s_count, 1)

    def choose_vector(self, dve):
        E, T, B, s = self.E, self.TILES, self.BLOCKS, self.s_step
        n = count(1)
        by = lambda t: t[:, :].rearrange("p (t e) -> p t e", e=E)
        p, q = by(self.p), by(self.q)
        top = self.top[:, :]
        wide = top.rearrange("p (t e) -> p t e", e=1).broadcast_to([TILE, T, E])
        order = self.order[:, :].rearrange("p (t e) -> p t e", t=1).broadcast_to([TILE, T, E])
        dve.wait_ge(self.s_const, START + self.NCONST + E)
        dve.tensor_copy(self.tri16[:, :], self.tri[:, :]).then_inc(self.s_const, 1)
        dve.tensor_copy(self.limit[:, :], self.limit_i[:, :]).then_inc(self.s_const, 1)
        dve.wait_ge(self.s_logits, START + IMG)
        dve.tensor_reduce(top, p, AX.X, ALU.max).then_inc(s, 1)
        dve.wait_ge(s, START + next(n))
        dve.tensor_tensor(p, p, wide, ALU.subtract).then_inc(s, 1)
        next(n)
        dve.wait_ge(self.s_exp, START + 1)
        dve.tensor_reduce(top, p, AX.X, ALU.add).then_inc(s, 1)
        dve.wait_ge(s, START + next(n))
        dve.reciprocal(top, top).then_inc(s, 1)
        dve.wait_ge(s, START + next(n))
        dve.tensor_tensor(p, p, wide, ALU.mult).then_inc(s, 1)
        dve.wait_ge(s, START + next(n))
        for k, src in enumerate((p, q)):
            hot = by(self.hot[k])
            dve.tensor_reduce(top, src, AX.X, ALU.max).then_inc(s, 1)
            dve.wait_ge(s, START + next(n))
            dve.tensor_copy(self.share[:, :, k], top).then_inc(s, 1)
            dve.tensor_tensor(hot, src, wide, ALU.is_equal).then_inc(s, 1)
            next(n)
            dve.wait_ge(s, START + next(n))
            dve.tensor_tensor(hot, hot, order, ALU.mult).then_inc(s, 1)
            dve.wait_ge(s, START + next(n))
            dve.tensor_reduce(top, hot, AX.X, ALU.max).then_inc(s, 1)
            dve.wait_ge(s, START + next(n))
            dve.tensor_tensor(hot, hot, wide, ALU.is_equal).then_inc(s, 1)
            dve.wait_ge(s, START + next(n))
            if k == 0:
                dve.scalar_tensor_tensor(out=q, in0=hot, scalar=-2.0, in1=p, op0=ALU.mult, op1=ALU.add).then_inc(s, 1)
                dve.wait_ge(s, START + next(n))
        dve.tensor_tensor(self.both[:, :], self.hot[0][:, :], self.hot[1][:, :], ALU.add).then_inc(self.s_both, 1)
        dve.tensor_tensor(top, self.share[:, :, 0], self.share[:, :, 1], ALU.add).then_inc(s, 1)
        dve.wait_ge(s, START + next(n))
        dve.reciprocal(top, top).then_inc(s, 1)
        dve.wait_ge(s, START + next(n))
        dve.tensor_tensor(self.share[:, :, :], self.share[:, :, :],
                          top.rearrange("p (t k) -> p t k", k=1).broadcast_to([TILE, T, self.PAIR]), ALU.mult).then_inc(s, 1)
        next(n)
        by_expert = lambda t: t.rearrange("p (e t) -> p e t", t=T)
        of_experts = lambda t: t.rearrange("p (e t) -> p e t", t=1).broadcast_to([TILE, E, T])
        zeros = lambda width: self.zero1[:, 0:1].broadcast_to([TILE, width])
        tokens, upto, begun = self.q[:, :], self.p[:, :], self.gathered[0][:, 0:T * E]
        number, blocks, ends, shift = (self.small[:, r, :] for r in range(4))
        BANKS = T * E // HALF
        TB = T // BANKS
        for m in range(BANKS):
            dve.wait_ge(self.s_count, START + 2 * m + 2)
            dve.tensor_copy(by_expert(tokens)[:, :, m * TB:(m + 1) * TB], self.core.bank[6 + m][:, :].rearrange("p (t e) -> p e t", e=E)).then_inc(s, 1)
            dve.wait_ge(s, START + next(n))
        dve.tensor_tensor_scan(upto, tokens, zeros(T * E), 0.0, ALU.add, ALU.add).then_inc(s, 1)
        dve.tensor_reduce(number, by_expert(tokens), AX.X, ALU.add).then_inc(s, 1)
        next(n)
        dve.wait_ge(s, START + next(n))
        dve.tensor_tensor(by_expert(begun), of_experts(number), self.limit[:, 0:T].rearrange("p (e t) -> p e t", e=1).broadcast_to([TILE, E, T]), ALU.is_gt).then_inc(s, 1)
        dve.tensor_tensor(tokens, upto, tokens, ALU.subtract).then_inc(s, 1)
        next(n)
        dve.wait_ge(s, START + next(n))
        dve.tensor_reduce(blocks, by_expert(begun), AX.X, ALU.add).then_inc(s, 1)
        dve.wait_ge(s, START + next(n))
        dve.tensor_scalar(blocks, blocks, float(TILE), None, ALU.mult).then_inc(s, 1)
        dve.wait_ge(s, START + next(n))
        dve.tensor_tensor_scan(ends, blocks, zeros(E), 0.0, ALU.add, ALU.add).then_inc(s, 1)
        dve.wait_ge(s, START + next(n))
        dve.tensor_tensor(shift, ends, blocks, ALU.subtract).then_inc(s, 1)
        dve.tensor_tensor(number, by_expert(upto)[:, :, T - 1], number, ALU.subtract).then_inc(s, 1)
        next(n)
        dve.wait_ge(s, START + next(n))
        dve.tensor_tensor(shift, shift, number, ALU.subtract).then_inc(s, 1)
        dve.wait_ge(s, START + next(n))
        dve.tensor_tensor(by_expert(tokens), by_expert(tokens), of_experts(shift), ALU.add).then_inc(s, 1)
        dve.wait_ge(s, START + next(n))
        for m in range(BANKS):
            dve.tensor_tensor(p[:, m * TB:(m + 1) * TB, :], self.core.bank[4 + m][:, :].rearrange("p (t e) -> p t e", e=E),
                              tokens.rearrange("p (e t) -> p t e", t=T)[:, m * TB:(m + 1) * TB, :], ALU.add).then_inc(s, 1)
            dve.wait_ge(s, START + next(n))
        for k in range(self.PAIR):
            dve.tensor_tensor(self.hot[k][:, :], self.hot[k][:, :], self.p[:, :], ALU.mult).then_inc(s, 1)
            dve.wait_ge(s, START + next(n))
            dve.tensor_reduce(self.slot[:, :, k], by(self.hot[k]), AX.X, ALU.add).then_inc(s, 1)
            dve.wait_ge(s, START + next(n))
        dve.tensor_copy(self.index[:, :, :], self.slot[:, :, :]).then_inc(self.s_index, 1)
        past = self.past[:, :].rearrange("p (s e) -> p s e", e=E)
        dve.tensor_tensor(past, ends[0:1].rearrange("p (s e) -> p s e", s=1).broadcast_to([1, B, E]),
                          self.limit[0:1, :].rearrange("p (s e) -> p s e", e=1).broadcast_to([1, B, E]), ALU.is_le).then_inc(s, 1)
        dve.wait_ge(s, START + next(n))
        dve.tensor_reduce(self.expert[:, :], past, AX.X, ALU.add).then_inc(s, 1)
        dve.wait_ge(s, START + next(n))
        dve.tensor_scalar(self.expert[:, :], self.expert[:, :], float(E - 1), None, ALU.min).then_inc(s, 1)
        dve.wait_ge(s, START + next(n))
        dve.tensor_copy(self.ids[:, 0, 1:B], self.expert[:, 0:B - 1]).then_inc(self.s_ids, 1)
        dve.tensor_copy(self.ids[:, 0, 0:1], self.expert[:, 0:1]).then_inc(self.s_ids, 1)
        dve.tensor_copy(self.ids[:, 1, :], self.expert[:, :]).then_inc(self.s_ids, 1)
        dve.tensor_copy(self.ids[:, 2, 0:B - 1], self.expert[:, 1:B]).then_inc(self.s_ids, 1)
        dve.tensor_copy(self.ids[:, 2, B - 1:B], self.expert[:, B - 1:B]).then_inc(self.s_ids, 1)


    def scatter_scalar(self, act):
        def stage(p, k):
            act.activation(self.yout[k][:, :, :], self.rows[:, bass.ds((2 * p + k) * HALF, HALF)].rearrange("p (j c) -> p j c", c=C), ACT.Copy).then_inc(self.s_stage, 1)

        act.wait_ge(self.s_rows, START + 2 * IMG)
        stage(0, 0)
        stage(0, 1)
        with act.Fori(1, IMG) as p:
            for k in range(2):
                act.wait_ge(self.s_scatter[k], 16 * self.GROUP * self.PAIR * p)
                stage(p, k)

    def scatter_gpsimd(self, pool):
        N = self.GROUP * self.PAIR
        pool.wait_ge(self.s_fill, START + 16 * self.GROUPS)
        pool.wait_ge(self.s_index, START + 1)
        with pool.Fori(0, IMG) as p:
            for k in range(2):
                pool.wait_ge(self.s_stage, START + 2 * p + k + 1)
                pool.sem_inc(self.s_begun, 1)
                pool.tensor_copy(self.own[k][:, :], self.indices(2 * p + k)).then_inc(self.s_own, 1)
                pool.wait_ge(self.s_own, START + 2 * p + k + 1)
                pool.sem_inc(self.s_begun, 1)
                for m in range(N):
                    pool.indirect_dma_start(self.xs[:, :], bass.IndirectOffsetOnAxis(ap=self.own[k][:, m:m + 1], axis=0),
                                            self.yout[k][:, m // self.PAIR, :], None).then_inc(self.s_scatter[k], 16)

    def indices(self, half):
        N = self.GROUP * self.PAIR
        return self.index[:, :, :].rearrange("p t k -> p (t k)")[:, bass.ds(half * N, N)]


    def groups(self, group):
        pairs = (self.GROUPS - 2) // 2
        def run(eng):
            group(0, 0, 0)
            with eng.Fori(0, pairs) as p:
                group(2 * p + 1, 1, p + 1)
                group(2 * p + 2, 0, p + 1)
            for g in range(2 * pairs + 1, self.GROUPS):
                group(g, g % 2, (g + 1) // 2)
        return run

    def experts_of(self, engine, row, g):
        _, ids = self.core.nc.values_load_multi_w_load_instructions(
            self.ids[0:1, row, bass.ds(g * self.GROUP, self.GROUP)], [engine], min_val=0, max_val=self.E - 1,
            skip_runtime_bounds_check_because="the ids are counts of experts, and their minimum with the last expert was taken")
        return ids

    def transfers(self, k):
        return len(range(k, self.GROUPS, 2))

    def blocks_sync(self, sp):
        for k in range(2):
            sp.wait_ge(self.s_scatter[k], 16 * self.GROUP * self.PAIR * IMG)

        def load(g, k):
            sp.dma_start(self.xin[k][:, :, :], self.group_rows(self.xs, g)).then_inc(self.s_in[k], 16)

        def store(g, k):
            sp.wait_ge(self.s_y, START + self.GROUP * (g + 1))
            sp.dma_start(self.group_rows(self.ys, g), self.yout[k][:, :, :]).then_inc(self.s_stored[k], 16)

        load(0, 0)

        def group(g, k, half):
            if not is_last(g, self.GROUPS):
                sp.wait_ge(self.s_t, START + self.GROUP * g)
                load(g + 1, 1 - k)
            if not is_first(g):
                store(g - 1, 1 - k)

        self.groups(group)(sp)
        store(self.GROUPS - 1, (self.GROUPS - 1) % 2)
        for k in range(2):
            sp.wait_ge(self.s_stored[k], START + 16 * self.transfers(k))

    def blocks_tensor(self, pe, first, second):
        G, BLOCKS, PE = self.GROUP, self.BLOCKS, mybir.EngineType.PE
        pe.wait_ge(self.s_ids, START + self.NIDS)

        def turn(n, j, k):
            pe.wait_ge(self.s_xt, START + lag(n))
            pe.transpose(self.core.bank[j % 2][:, 0:TILE], self.xin[k][:, j, :], self.core.ident[:, :]).then_inc(self.s_t, 1)

        def out(n, r, expert):
            pe.wait_ge(self.s_hid, START + n + 1)
            pe.wait_ge(self.s_y, START + lag(n))
            second(r, expert).then_inc(self.s_o, 1)

        pe.wait_ge(self.s_in[0], START + 16)
        turn(0, 0, 0)

        def group(g, k, half):
            before = self.experts_of(PE, 0, g)
            for j in range(G):
                n = G * g + j
                if not is_last(n, BLOCKS):
                    if j + 1 < G:
                        turn(n + 1, j + 1, k)
                    else:
                        pe.wait_ge(self.s_in[1 - k], START + 16 * (half + 1))
                        turn(n + 1, 0, 1 - k)
                pe.wait_ge(self.s_xt, START + n + 1)
                pe.wait_ge(self.s_w1, START + n + 1)
                pe.wait_ge(self.s_hid, START + lag(n))
                first(j % 2).then_inc(self.s_h, 1)
                if not is_first(n):
                    out(n - 1, (j - 1) % 2, before[j])

        self.groups(group)(pe)
        out(BLOCKS - 1, (BLOCKS - 1) % 2, self.experts_of(PE, 1, self.GROUPS - 1)[G - 1])

    def blocks_scalar(self, act, turned, activated, by_expert=False):
        def experts(row, g):
            return self.experts_of(mybir.EngineType.Activation, row, g) if by_expert else [None] * self.GROUP

        if by_expert:
            act.wait_ge(self.s_ids, START + self.NIDS)

        def turn(n, r, expert):
            act.wait_ge(self.s_t, START + n + 1)
            act.wait_ge(self.s_h, START + lag(n))
            turned(r, expert).then_inc(self.s_xt, 1)

        turn(0, 0, experts(1, 0)[0])

        def group(g, k, half):
            after, own = experts(2, g), experts(1, g)
            for j in range(self.GROUP):
                n = self.GROUP * g + j
                if not is_last(n, self.BLOCKS):
                    turn(n + 1, (j + 1) % 2, after[j])
                act.wait_ge(self.s_h, START + n + 1)
                activated(n, j % 2, own[j])

        self.groups(group)(act)

    def blocks_vector(self, dve, copy_w1, gated, out, by_expert=False):
        G, DVE = self.GROUP, mybir.EngineType.DVE
        dve.wait_ge(self.s_ids, START + self.NIDS)

        def weights(n, r, expert):
            dve.wait_ge(self.s_h, START + lag(n))
            copy_w1(r, expert).then_inc(self.s_w1, 1)

        def leave(n, j, k, expert):
            dve.wait_ge(self.s_o, START + n + 1)
            out(j % 2, self.yout[k][:, j, :], expert).then_inc(self.s_y, 1)

        weights(0, 0, self.experts_of(DVE, 1, 0)[0])

        def group(g, k, half):
            after = self.experts_of(DVE, 2, g)
            before = self.experts_of(DVE, 0, g) if by_expert else [None] * G
            for j in range(G):
                n = G * g + j
                if not is_last(n, self.BLOCKS):
                    weights(n + 1, (j + 1) % 2, after[j])
                gated(n, j % 2)
                if j == 1:
                    dve.wait_ge(self.s_stored[k], START + 16 * (half - k))
                if j:
                    leave(n - 1, j - 1, k, before[j])
                elif not is_first(n):
                    leave(n - 1, G - 1, 1 - k, before[j])

        self.groups(group)(dve)
        expert = self.experts_of(DVE, 1, self.GROUPS - 1)[G - 1] if by_expert else None
        leave(self.BLOCKS - 1, G - 1, (self.GROUPS - 1) % 2, expert)


    def combine_gpsimd(self, pool):
        for k in range(2):
            pool.wait_ge(self.s_stored[k], START + 16 * self.transfers(k))
        with pool.Fori(0, IMG) as p:
            for k in range(2):
                pool.wait_ge(self.s_sum[k], START + p)
                pool.sem_inc(self.s_begun, 1)
                pool.tensor_copy(self.own[k][:, :], self.indices(2 * p + k)).then_inc(self.s_own, 1)
                pool.wait_ge(self.s_own, START + 2 * IMG + 2 * p + k + 1)
                pool.sem_inc(self.s_begun, 1)
                for m in range(self.GROUP * self.PAIR):
                    pool.indirect_dma_start(self.gathered[k][:, m * C:(m + 1) * C], None, self.ys[:, :],
                                            bass.IndirectOffsetOnAxis(ap=self.own[k][:, m:m + 1], axis=0)).then_inc(self.s_got[k], 16)

    def combine_tensor(self, pe):
        with pe.Fori(0, IMG) as p:
            for k in range(2):
                pe.wait_ge(self.s_end[k], START + p)
                pe.wait_ge(self.s_weighted[k], START + p + 1)
                for j in range(self.GROUP):
                    for m in range(self.PAIR):
                        at = (j * self.PAIR + m) * C
                        mm = pe.matmul(self.core.bank[k][:, j * TILE:(j + 1) * TILE], self.gathered[k][:, at:at + C], self.core.ident[:, :],
                                       start=(m == 0), stop=(m == self.PAIR - 1))
                mm.then_inc(self.s_sum[k], 1)

    def combine_vector(self, dve):
        N = self.GROUP * self.PAIR
        share = self.share[:, :, :].rearrange("p t k -> p (t k)")
        with dve.Fori(0, IMG) as p:
            for k in range(2):
                dve.wait_ge(self.s_got[k], 16 * N * (p + 1))
                g = self.gathered[k][:, :].rearrange("p (m c) -> p m c", c=C)
                w = share[:, bass.ds((2 * p + k) * N, N)].rearrange("p (m c) -> p m c", c=1).broadcast_to([TILE, N, C])
                dve.tensor_tensor(g, g, w, ALU.mult).then_inc(self.s_weighted[k], 1)
                xs = self.core.x[:, bass.ds((2 * p + k) * HALF, HALF)]
                dve.wait_ge(self.s_sum[k], START + p + 1)
                dve.tensor_tensor(xs, xs, self.core.bank[k][:, :], ALU.add).then_inc(self.s_end[k], 1)


def is_first(n):
    return isinstance(n, int) and n == 0


def is_last(n, count):
    return isinstance(n, int) and n == count - 1


def lag(n):
    return max(n - 1, 0) if isinstance(n, int) else n - 1


def experts_ffn(core, args):
    nc, norm, X = core.nc, core.norm, core.x
    E, _, HID = args["L2_ffn_w1"].shape
    K = HID // C
    W = HID * 2
    with ExitStack() as mem:
        ex = Grouped(core, mem, "ex", args["L2_ffn_gate_w"], args["L2_ffn_gate_b"], W)
        w12 = core.sb(mem, "ex_w12", [C, E * W])
        w3 = core.sb(mem, "ex_w3", [C, E * HID])
        by_w = w12[:, :].rearrange("c (e n h) -> c e n h", e=E, n=2)
        by_w3 = w3[:, :].rearrange("p (e k d) -> p e k d", e=E, k=K)
        silu = [core.sb(mem, f"ex_silu{k}", [C, HID]) for k in range(2)]
        hid = [core.sb(mem, f"ex_hidden{k}", [C, HID]) for k in range(2)]
        s_w = core.sem("ex_weights")
        pre, outs = core.bank[2:4], core.bank[4:6]
        core.start_counts()
        with nc.Block() as block:
            @block.sync
            def _(sp):
                ex.load(sp)
                for k in range(K):
                    sp.dma_start(by_w3[:, :, k], args["L2_ffn_w3"].rearrange("e (k p) d -> k p e d", p=C)[k]).then_inc(s_w, 16)
                for n, name in enumerate(("w1", "w2")):
                    sp.dma_start(by_w[:, :, n], args[f"L2_ffn_{name}"].rearrange("e c h -> c e h")).then_inc(s_w, 16)
                ex.blocks_sync(sp)

            @block.gpsimd
            def _(pool):
                ex.constants(pool)
                ex.scatter_gpsimd(pool)
                ex.combine_gpsimd(pool)

            @block.tensor
            def _(pe):
                pe.wait_ge(ex.s_par, START + 32)

                def route(b):
                    for h in range(2):
                        pe.wait_ge(norm.s_out, START + norm.ready(b, h))
                    ex.route_tensor(pe, b, ex.v)
                    ex.rows_tensor(pe, b, ex.v)

                ahead(pe, IMG, lambda b: None, lambda b: norm.tensor(pe, b, x_halves(core, b)), route)
                ex.choose_tensor(pe)
                pe.wait_ge(s_w, START + 16 * (K + 2))

                def first(r):
                    for c in range(2 * K):
                        mm = pe.matmul(pre[r][:, c * TILE:(c + 1) * TILE], ex.w1[r][:, c * C:(c + 1) * C], ex.xt[r][:, :], start=True, stop=True)
                    return mm

                def second(r, expert):
                    for c in range(K):
                        mm = pe.matmul(outs[r][:, 0:C], hid[r][:, c * TILE:(c + 1) * TILE], w3[:, bass.ds(expert * HID + c * C, C)],
                                       start=(c == 0), stop=(c == K - 1))
                    return mm

                ex.blocks_tensor(pe, first, second)
                ex.combine_tensor(pe)

            @block.scalar
            def _(act):
                act.preload_act_table_set(LOG_EXP)
                ahead(act, IMG, lambda b: None, lambda b: norm.scalar(act, b, 1e-5), lambda b: ex.rows_scalar(act, b))
                ex.choose_scalar(act)
                act.preload_act_table(ACT.Silu)
                ex.scatter_scalar(act)

                def turned(r, expert):
                    return act.activation(ex.xt[r][:, :], core.bank[r][:, 0:TILE], ACT.Copy)

                def activated(n, r, expert):
                    act.wait_ge(ex.s_hid, START + lag(n))
                    act.activation(silu[r][:, :], pre[r][:, 0:HID], ACT.Silu).then_inc(ex.s_act, 1)

                ex.blocks_scalar(act, turned, activated)

            @block.vector
            def _(dve):
                dve.wait_ge(ex.s_par, START + 32)

                def normalise(b):
                    dve.wait_ge(ex.s_turn, START + 2 * b)
                    norm.finish(dve, b, [image(ex.v[:, h * HALF:(h + 1) * HALF]) for h in range(2)])

                ahead(dve, IMG, normalise, lambda b: norm.centre(dve, b, x_halves(core, b)), lambda b: ex.route_vector(dve, b))
                ex.choose_vector(dve)
                dve.wait_ge(s_w, START + 16 * (K + 2))

                def copy_w1(r, expert):
                    return dve.tensor_copy(ex.w1[r][:, :], w12[:, bass.ds(expert * W, W)])

                def gated(n, r):
                    dve.wait_ge(ex.s_act, START + n + 1)
                    dve.wait_ge(ex.s_o, START + lag(n))
                    dve.tensor_tensor(hid[r][:, :], silu[r][:, :], pre[r][:, HID:W], ALU.mult).then_inc(ex.s_hid, 1)

                def out(r, to, expert):
                    return dve.tensor_copy(to, outs[r][:, 0:C])

                ex.blocks_vector(dve, copy_w1, gated, out)
                ex.combine_vector(dve)
        norm.done()


def sign_conv_mixer(core, args):
    nc, norm, X = core.nc, core.norm, core.x
    TAPS = 9
    with ExitStack() as mem:
        v = [core.sb(mem, f"sc_v{k}", [C, PAD, PAD]) for k in range(2)]
        w = core.sb(mem, "sc_w", [C, TAPS, C])
        pruning = core.sb(mem, "sc_pruning", [C, TAPS, C])
        signs = core.sb(mem, "sc_signs", [C, TAPS, C])
        size = core.sb(mem, "sc_size", [C, TAPS, C])
        clipped = core.sb(mem, "sc_clipped", [C, TAPS, C])
        total = core.sb(mem, "sc_total", [C, C])
        scale = core.sb(mem, "sc_scale", [C, C])
        (s_par, s_zero, s_act, s_w, s_tot, s_conv, s_end) = (
            core.sem(f"sc_{n}") for n in ("params", "zero", "signs", "weights", "scale", "convolved", "end"))
        core.start_counts()
        with nc.Block() as block:
            @block.sync
            def _(sp):
                sp.dma_start(w[:, :, :], args["L3_conv_w"].rearrange("a b i o -> i (a b) o")).then_inc(s_par, 16)
                sp.dma_start(pruning[:, :, :], args["L3_conv_pruning_mask"].rearrange("(t i) o -> i t o", i=C)).then_inc(s_par, 16)

            @block.gpsimd
            def _(pool):
                for k in range(2):
                    pool.memset(v[k][:, :, :], 0.0).then_inc(s_zero, 1)

            @block.tensor
            def _(pe):
                pe.wait_ge(s_w, START + 1)
                pe.matmul(core.bank[4][:, 0:C], core.mean_w[:, :], total[:, :], start=True, stop=True).then_inc(s_tot, 1)
                pe.wait_ge(s_w, START + 7)

                def convolve(p, k):
                    pe.wait_ge(norm.s_out, START + norm.ready(2 * p + k, 1))
                    pe.wait_ge(s_end, START + 4 * p)
                    for h in range(2):
                        bank = core.bank[4 + 2 * k + h]
                        for t in range(TAPS):
                            mm = pe.matmul(image(bank), w[:, t, :], window(v[k], h, t), start=(t == 0), stop=(t == TAPS - 1))
                        mm.then_inc(s_conv, 1)

                norm.tensor(pe, 0, x_halves(core, 0))
                with pe.Fori(0, IMG // 2 - 1) as p:
                    for k in range(2):
                        norm.tensor(pe, 2 * p + k + 1, x_halves(core, 2 * p + k + 1))
                        convolve(p, k)
                norm.tensor(pe, IMG - 1, x_halves(core, IMG - 1))
                for k in range(2):
                    convolve(IMG // 2 - 1, k)

            @block.scalar
            def _(act):
                act.wait_ge(s_par, START + 32)
                act.activation(size[:, :, :], w[:, :, :], ACT.Abs).then_inc(s_act, 1)
                act.activation(signs[:, :, :], w[:, :, :], ACT.Sign).then_inc(s_act, 1)
                act.wait_ge(s_zero, START + 2)
                act.preload_act_table_set(LOG_EXP)
                with act.Fori(0, IMG) as b:
                    norm.scalar(act, b, 1e-6)

            @block.vector
            def _(dve):
                dve.wait_ge(s_act, START + 2)
                dve.tensor_reduce(total[:, :], size[:, :, :].rearrange("i t o -> i o t"), AX.X, ALU.add).then_inc(s_w, 1)
                dve.wait_ge(s_tot, START + 1)
                dve.tensor_scalar(scale[:, :], core.bank[4][:, 0:C], 1.0 / TAPS, None, ALU.mult).then_inc(s_w, 1)
                dve.tensor_scalar(clipped[:, :, :], w[:, :, :], -1.0, 1.0, ALU.max, ALU.min).then_inc(s_w, 1)
                dve.wait_ge(s_w, START + 3)
                dve.tensor_tensor(w[:, :, :], signs[:, :, :], scale[:, :].rearrange("i (t o) -> i t o", t=1).broadcast_to([C, TAPS, C]), ALU.mult).then_inc(s_w, 1)
                dve.wait_ge(s_w, START + 4)
                dve.tensor_tensor(w[:, :, :], w[:, :, :], clipped[:, :, :], ALU.subtract).then_inc(s_w, 1)
                dve.wait_ge(s_w, START + 5)
                dve.tensor_tensor(w[:, :, :], w[:, :, :], clipped[:, :, :], ALU.add).then_inc(s_w, 1)
                dve.wait_ge(s_w, START + 6)
                dve.tensor_tensor(w[:, :, :], w[:, :, :], pruning[:, :, :], ALU.mult).then_inc(s_w, 1)
                dve.wait_ge(s_zero, START + 2)
                norm.vector(dve, 0, [X[:, 0:HALF], X[:, HALF:PIX]], [inner(v[0], 0), inner(v[0], 1)])

                def finish(p, k):
                    for h in range(2):
                        xs = X[:, bass.ds(p * (2 * PIX) + (k * PIX + h * HALF), HALF)]
                        dve.wait_ge(s_conv, START + 4 * p + 2 * k + h + 1)
                        dve.tensor_tensor(xs, xs, core.bank[4 + 2 * k + h][:, :], ALU.add).then_inc(s_end, 1)

                with dve.Fori(0, IMG // 2 - 1) as p:
                    for k in range(2):
                        dve.wait_ge(s_conv, START + 4 * p + 2 * k)
                        norm.vector(dve, 2 * p + k + 1, [X[:, bass.ds(p * (2 * PIX) + ((k + 1) * PIX + h * HALF), HALF)] for h in range(2)],
                                    [inner(v[1 - k], 0), inner(v[1 - k], 1)])
                        finish(p, k)
                p = IMG // 2 - 1
                dve.wait_ge(s_conv, START + 4 * p)
                norm.vector(dve, 2 * p + 1, [X[:, 2 * p * PIX + PIX + h * HALF:2 * p * PIX + PIX + (h + 1) * HALF] for h in range(2)],
                            [inner(v[1], 0), inner(v[1], 1)])
                finish(p, 0)
                finish(p, 1)
        norm.done()


def normed_experts_ffn(core, args):
    nc, norm, X = core.nc, core.norm, core.x
    E, _, HID = args["L3_ffn_W1"].shape
    K = HID // C
    with ExitStack() as mem:
        ex = Grouped(core, mem, "nx", args["L3_ffn_Wr"], args["L3_ffn_br"], HID)
        u = core.sb(mem, "nx_u", [C, PIX])
        w1 = core.sb(mem, "nx_w1", [C, E * HID])
        w2 = core.sb(mem, "nx_w2", [C, E * HID])
        by_w2 = w2[:, :].rearrange("p (e k d) -> p e k d", e=E, k=K)
        b1 = core.sb(mem, "nx_b1", [C, E * K])
        b2 = core.sb(mem, "nx_b2", [TILE, E * C])
        gain = core.sb(mem, "nx_gain", [C, 2, E])
        hid = [core.sb(mem, f"nx_hidden{k}", [C, HID]) for k in range(2)]
        s_w = core.sem("nx_weights")
        pre, outs = core.bank[2:4], core.bank[4:6]
        NPAR = K + 5
        core.start_counts()
        with nc.Block() as block:
            @block.sync
            def _(sp):
                ex.load(sp)
                for n, name in enumerate(("g", "b")):
                    sp.dma_start(gain[:, n, :], args[f"L3_ffn_ln_{name}"].rearrange("e c -> c e"), allow_slow_non_contiguous=True).then_inc(s_w, 16)
                sp.dma_start(b1[:, :], args["L3_ffn_b1"].rearrange("e (k p) -> p (e k)", p=C), allow_slow_non_contiguous=True).then_inc(s_w, 16)
                sp.dma_start(b2[:, :], args["L3_ffn_b2"].rearrange("(o e) c -> o (e c)", o=1).broadcast_to([TILE, E * C])).then_inc(s_w, 16)
                sp.dma_start(w1[:, :].rearrange("c (e h) -> c e h", e=E), args["L3_ffn_W1"].rearrange("e c h -> c e h")).then_inc(s_w, 16)
                for k in range(K):
                    sp.dma_start(by_w2[:, :, k], args["L3_ffn_W2"].rearrange("e (k p) d -> k p e d", p=C)[k]).then_inc(s_w, 16)
                ex.blocks_sync(sp)

            @block.gpsimd
            def _(pool):
                ex.constants(pool)
                ex.scatter_gpsimd(pool)
                ex.combine_gpsimd(pool)

            @block.tensor
            def _(pe):
                pe.wait_ge(ex.s_par, START + 32)

                def route(b):
                    for h in range(2):
                        pe.wait_ge(norm.s_out, START + norm.ready(2 * b, h))
                    norm.tensor(pe, 2 * b + 1, [ex.v[:, h * HALF:(h + 1) * HALF] for h in range(2)])
                    ex.route_tensor(pe, b, ex.v)

                def rows(b):
                    for h in range(2):
                        pe.wait_ge(norm.s_out, START + norm.ready(2 * b + 1, h))
                    ex.rows_tensor(pe, b, u)

                ahead(pe, IMG, route, lambda b: norm.tensor(pe, 2 * b, x_halves(core, b)), rows)
                ex.choose_tensor(pe)
                pe.wait_ge(s_w, START + 16 * NPAR)

                def first(r):
                    for c in range(K):
                        mm = pe.matmul(pre[r][:, c * TILE:(c + 1) * TILE], ex.w1[r][:, c * C:(c + 1) * C], ex.xt[r][:, :], start=True, stop=True)
                    return mm

                def second(r, expert):
                    for c in range(K):
                        mm = pe.matmul(outs[r][:, 0:C], hid[r][:, c * TILE:(c + 1) * TILE], w2[:, bass.ds(expert * HID + c * C, C)],
                                       start=(c == 0), stop=(c == K - 1))
                    return mm

                ex.blocks_tensor(pe, first, second)
                ex.combine_tensor(pe)

            @block.scalar
            def _(act):
                act.preload_act_table_set(LOG_EXP)
                ahead(act, IMG, lambda b: norm.scalar(act, 2 * b + 1, 1e-5), lambda b: norm.scalar(act, 2 * b, 1e-5), lambda b: ex.rows_scalar(act, b))
                ex.choose_scalar(act)
                act.preload_act_table(ACT.Gelu)
                ex.scatter_scalar(act)
                act.wait_ge(s_w, START + 16 * NPAR)

                def turned(r, expert):
                    return act.activation(ex.xt[r][:, :], core.bank[r][:, 0:TILE], ACT.Identity, bias=gain[:, 1, bass.ds(expert, 1)], scale=gain[:, 0, bass.ds(expert, 1)])

                def activated(n, r, expert):
                    act.wait_ge(ex.s_o, START + lag(n))
                    for c in range(K):
                        ins = act.activation(hid[r][:, c * TILE:(c + 1) * TILE], pre[r][:, c * TILE:(c + 1) * TILE], ACT.Gelu, bias=b1[:, bass.ds(expert * K + c, 1)])
                    ins.then_inc(ex.s_hid, 1)

                ex.blocks_scalar(act, turned, activated, by_expert=True)

            @block.vector
            def _(dve):
                dve.wait_ge(ex.s_par, START + 32)

                def normalise(b):
                    norm.finish(dve, 2 * b, [image(ex.v[:, h * HALF:(h + 1) * HALF]) for h in range(2)])
                    for h in range(2):
                        dve.wait_ge(norm.s_out, START + norm.ready(2 * b, h))
                    norm.centre(dve, 2 * b + 1, [ex.v[:, h * HALF:(h + 1) * HALF] for h in range(2)])
                    dve.wait_ge(ex.s_turn, START + 2 * b)
                    norm.finish(dve, 2 * b + 1, [image(u[:, h * HALF:(h + 1) * HALF]) for h in range(2)])

                ahead(dve, IMG, normalise, lambda b: norm.centre(dve, 2 * b, x_halves(core, b)), lambda b: ex.route_vector(dve, b))
                ex.choose_vector(dve)
                dve.wait_ge(s_w, START + 16 * NPAR)

                def copy_w1(r, expert):
                    return dve.tensor_copy(ex.w1[r][:, :], w1[:, bass.ds(expert * HID, HID)])

                def out(r, to, expert):
                    return dve.tensor_tensor(to, outs[r][:, 0:C], b2[:, bass.ds(expert * C, C)], ALU.add)

                ex.blocks_vector(dve, copy_w1, lambda n, r: None, out, by_expert=True)
                ex.combine_vector(dve)
        norm.done(2)


BRANCHES = [deformable_mixer_and_recurrence, divisive_mixer, routed_depth_ffn, scan_mixer, experts_ffn, sign_conv_mixer, normed_experts_ffn]


def program(nc, args, out, first=0, last=len(BRANCHES)):
    with ExitStack() as ctx:
        core = Core(nc, ctx)
        core.run(load_x, args["x"])
        for branch in BRANCHES[first:last]:
            core.run(branch, args)
        core.run(store_x, out)


def kernel(**inputs):
    import numpy as np
    import concourse.bacc as bacc
    from concourse.bass_utils import run_bass_kernel_spmd

    nc = bacc.Bacc("TRN2", target_bir_lowering=False, num_devices=1)
    arrays, args = {}, {}
    for name, value in inputs.items():
        a = np.ascontiguousarray(value)
        arrays[f"in_{name}"] = a
        args[name] = nc.dram_tensor(f"in_{name}", a.shape, mybir.dt.from_np(a.dtype), kind="ExternalInput").ap()
    out = nc.dram_tensor("out_0_dram", (IMG, ROWS, COLS, C), F32, kind="ExternalOutput").ap()
    program(nc, args, out)
    r = run_bass_kernel_spmd(nc, [arrays], core_ids=[0])
    return r.results[0]["out_0_dram"]
```

```python
from contextlib import ExitStack
from itertools import count

import concourse.bass as bass
from concourse import mybir

F32 = mybir.dt.float32
BF16 = mybir.dt.bfloat16
I32 = mybir.dt.int32
ALU = mybir.AluOpType
ACT = mybir.ActivationFunctionType
AX = mybir.AxisListType

C = 128
IMG, ROWS, COLS = 8, 32, 32
PIX = ROWS * COLS
TOK = IMG * PIX
HALF = PIX // 2
HROWS = ROWS // 2
PAD = ROWS + 2
TILE = 128
TPI = PIX // TILE

START = 1
INDIRECT = 36
LOG_EXP = "natural_log_exp_and_others"


def halves(b):
    return [b * PIX + h * HALF for h in range(2)]


class Core:

    def __init__(self, nc, ctx, out):
        self.nc, self.ctx, self.out, self.new_sems = nc, ctx, out, []
        self.branch = ctx
        self.untouched = [ctx.enter_context(nc.semaphore(f"indirect{n}")) for n in range(INDIRECT)]
        self.x = self.sb(ctx, "x_t", [C, TOK])
        self.ident = self.sb(ctx, "ident", [C, C])
        self.mean_w = self.sb(ctx, "mean_w", [C, C])
        self.bank = [ctx.enter_context(nc.psum_tensor(f"bank{n}", [C, HALF], F32)) for n in range(8)]
        self.norm = Norm(self)

    def sb(self, mem, name, shape, dtype=F32):
        return mem.enter_context(self.nc.sbuf_tensor(name, shape, dtype))

    def sem(self, name):
        s = self.branch.enter_context(self.nc.semaphore(name))
        self.new_sems.append(s)
        return s

    def indirect_sem(self):
        return self.untouched.pop(0)

    def run(self, branch, *args):
        with ExitStack() as self.branch:
            branch(self, *args)

    def start_counts(self):
        raised, self.new_sems = self.new_sems, []
        with self.nc.Block() as block:
            @block.sync
            def _(sp):
                for s in raised:
                    sp.sem_clear(s)
                    sp.sem_inc(s, START)


class Norm:

    def __init__(self, core):
        ctx = core.ctx
        self.core, self.base = core, 0
        self.mean, self.var = core.bank[0:2], core.bank[2:4]
        self.cent = [core.sb(ctx, f"norm_cent{h}", [C, HALF]) for h in range(2)]
        self.sq = [core.sb(ctx, f"norm_sq{h}", [C, HALF]) for h in range(2)]
        self.rstd = [core.sb(ctx, f"norm_rstd{h}", [C, HALF]) for h in range(2)]
        self.eps = {e: core.sb(ctx, f"norm_eps{n}", [C, 1]) for n, e in enumerate((1e-6, 1e-5))}
        self.s_mean = core.sem("norm_mean")
        self.s_cent = core.sem("norm_centred")
        self.s_sq = core.sem("norm_squared")
        self.s_var = core.sem("norm_variance")
        self.s_log = core.sem("norm_log")
        self.s_rstd = core.sem("norm_rstd_ready")
        self.s_out = core.sem("norm_out")

    def tensor(self, pe, i, src):
        n = self.base + 2 * i
        pe.wait_ge(self.s_cent, START + n)
        for h in range(2):
            out = self.mean[h][:, :] if len(src[h].shape) == 2 else self.mean[h][:, :].rearrange("c (b t) -> c b t", b=src[h].shape[1])
            pe.matmul(out, self.core.mean_w[:, :], src[h], start=True, stop=True).then_inc(self.s_mean, 1)
        pe.wait_ge(self.s_log, START + n)
        for h in range(2):
            pe.wait_ge(self.s_sq, START + n + h + 1)
            pe.matmul(self.var[h][:, :], self.core.mean_w[:, :], self.sq[h][:, :], start=True, stop=True).then_inc(self.s_var, 1)

    def scalar(self, act, i, eps):
        n = self.base + 2 * i
        act.wait_ge(self.s_var, START + n)
        for h in range(2):
            act.wait_ge(self.s_cent, START + n + h + 1)
            act.activation(self.sq[h][:, :], self.cent[h][:, :], ACT.Square).then_inc(self.s_sq, 1)
        act.wait_ge(self.s_out, START + n)
        for h in range(2):
            act.wait_ge(self.s_var, START + n + h + 1)
            act.activation(self.rstd[h][:, :], self.var[h][:, :], ACT.Ln, bias=self.eps[eps][:, 0:1]).then_inc(self.s_log, 1)
        for h in range(2):
            act.wait_ge(self.s_log, START + n + h + 1)
            act.activation(self.rstd[h][:, :], self.rstd[h][:, :], ACT.Exp, scale=-0.5).then_inc(self.s_rstd, 1)

    def vector(self, dve, i, src, dst, cols=COLS):
        self.centre(dve, i, src, cols)
        self.finish(dve, i, dst, cols)

    def centre(self, dve, i, src, cols=COLS):
        n = self.base + 2 * i
        dve.wait_ge(self.s_out, START + n)
        for h in range(2):
            dve.wait_ge(self.s_mean, START + n + h + 1)
            as_src = (lambda t: t) if len(src[h].shape) == 2 else (lambda t: t.rearrange("c (r w) -> c r w", w=cols))
            dve.tensor_tensor(as_src(self.cent[h][:, :]), src[h], as_src(self.mean[h][:, :]), ALU.subtract).then_inc(self.s_cent, 1)

    def finish(self, dve, i, dst, cols=COLS):
        n = self.base + 2 * i
        for h in range(2):
            dve.wait_ge(self.s_rstd, START + n + h + 1)
            dve.tensor_tensor(dst[h], image(self.cent[h], cols), image(self.rstd[h], cols), ALU.mult).then_inc(self.s_out, 1)

    def ready(self, i, h):
        return self.base + 2 * i + h + 1

    def done(self, times=1):
        self.base += 2 * IMG * times


def ahead(eng, count, first, start, rest):
    start(0)
    with eng.Fori(0, count - 1) as i:
        first(i)
        start(i + 1)
        rest(i)
    first(count - 1)
    rest(count - 1)


def ahead_by_parity(eng, count, first, start, rest):
    def item(i, k):
        first(i, k)
        if not (isinstance(i, int) and i == count - 1):
            start(i + 1)
        rest(i, k)

    start(0)
    item(0, 0)
    item(1, 1)
    with eng.Fori(1, count // 2 - 1) as p:
        for k in range(2):
            item(2 * p + k, k)
    item(count - 2, 0)
    item(count - 1, 1)


def x_halves(core, b):
    return [core.x[:, bass.ds(o, HALF)] for o in halves(b)]


def image(half, cols=COLS):
    return half[:, :].rearrange("c (r w) -> c r w", w=cols)


def inner(padded, h):
    return padded[:, 1 + HROWS * h:1 + HROWS * (h + 1), 1:1 + COLS]


def window(padded, h, tap):
    dy, dx = divmod(tap, 3)
    return padded[:, HROWS * h + dy:HROWS * (h + 1) + dy, dx:dx + COLS]


def column(vec):
    return vec.rearrange("(c o) -> c o", o=1)


def load_x(core, x):
    nc = core.nc
    rows = x.rearrange("i r w c -> (i r w) c").rearrange("(i j p) c -> i p j c", p=TILE, j=TPI)
    with ExitStack() as mem:
        raw = [core.sb(mem, f"raw{k}", [TILE, TPI, C]) for k in range(2)]
        s_const, s_raw, s_turn, s_copied = (core.sem(f"load_{n}") for n in ("const", "raw", "turned", "copied"))
        s_raws = [s_raw, core.sem("load_raw1")]
        core.start_counts()
        with nc.Block() as block:
            @block.gpsimd
            def _(pool):
                pool.memset(core.ident[:, :], 0.0).then_inc(s_const, 1)
                pool.memset(core.mean_w[:, :], 1.0 / C).then_inc(s_const, 1)
                for e, t in core.norm.eps.items():
                    pool.memset(t[:, :], e).then_inc(s_const, 1)
                pool.wait_ge(s_const, START + 4)
                pool.affine_select(out=core.ident[:, :], in_=core.ident[:, :], compare_op=ALU.not_equal, fill=1.0,
                                   base=0, pattern=[[-1, C]], channel_multiplier=1).then_inc(s_const, 1)

            @block.sync
            def _(sp):
                with sp.Fori(0, IMG // 2) as p:
                    for k in range(2):
                        sp.wait_ge(s_turn, START + 4 * p + 2 * k)
                        sp.dma_start(raw[k][:, :, :], rows[2 * p + k]).then_inc(s_raws[k], 16)

            @block.tensor
            def _(pe):
                pe.wait_ge(s_const, START + 5)
                with pe.Fori(0, IMG // 2) as p:
                    for k in range(2):
                        pe.wait_ge(s_raws[k], START + 16 * p + 16)
                        for h in range(2):
                            if k:
                                pe.wait_ge(s_copied, START + 4 * p + h + 1)
                            else:
                                pe.wait_ge(s_copied, START + 4 * p)
                            for j in range(4):
                                mm = pe.transpose(core.bank[h][:, j * TILE:(j + 1) * TILE], raw[k][:, 4 * h + j, :], core.ident[:, :])
                            mm.then_inc(s_turn, 1)

            @block.vector
            def _(dve):
                with dve.Fori(0, IMG // 2) as p:
                    for k in range(2):
                        for h in range(2):
                            dve.wait_ge(s_turn, START + 4 * p + 2 * k + h + 1)
                            dve.tensor_copy(core.x[:, bass.ds(p * (2 * PIX) + (k * PIX + h * HALF), HALF)], core.bank[h][:, :]).then_inc(s_copied, 1)


class Output:

    def __init__(self, core, mem, out):
        self.core = core
        self.rows = out.rearrange("i r w c -> (i r w) c").rearrange("(i h j p) c -> i h p j c", p=TILE, j=4, h=2)
        self.sums = [core.sb(mem, f"out_sums{h}", [C, HALF]) for h in range(2)]
        self.flat = [core.sb(mem, f"out_rows{h}", [TILE, 4, C]) for h in range(2)]
        self.bank = core.bank[2:4]
        self.s_turn, self.s_copied, self.s_stored = ([core.sem(f"out_{n}{h}") for h in range(2)] for n in ("turned", "copied", "stored"))

    def tensor(self, pe, b, h):
        pe.wait_ge(self.s_copied[h], START + b)
        for j in range(4):
            mm = pe.transpose(self.bank[h][:, j * TILE:(j + 1) * TILE], self.sums[h][:, j * TILE:(j + 1) * TILE], self.core.ident[:, :])
        mm.then_inc(self.s_turn[h], 1)

    def scalar(self, act):
        with act.Fori(0, IMG) as b:
            for h in range(2):
                act.wait_ge(self.s_stored[h], START + 16 * b)
                act.wait_ge(self.s_turn[h], START + b + 1)
                act.activation(self.flat[h][:, :, :], self.bank[h][:, :].rearrange("p (j c) -> p j c", c=C), ACT.Copy).then_inc(self.s_copied[h], 1)

    def sync(self, sp):
        with sp.Fori(0, IMG) as b:
            for h in range(2):
                sp.wait_ge(self.s_copied[h], START + b + 1)
                sp.dma_start(self.rows[b, h], self.flat[h][:, :, :]).then_inc(self.s_stored[h], 16)
        for h in range(2):
            sp.wait_ge(self.s_stored[h], START + 16 * IMG)


class Sampling:
    G, TAPS, XY = 8, 9, 2
    GC = C // G
    GT = G * TAPS
    CORNERS = 4
    CELL = CORNERS * GC
    CROWS = 3
    CW = COLS + 3
    CH = -(-(ROWS + 2) // CROWS) * CROWS
    BW, BH = CW, CH + 2
    CELLS = CH * CW * G
    TILES = TOK // TILE
    NOFF = GT * XY
    NLOG = NOFF + GT


def deformable_mixer_and_recurrence(core, args):
    S = Sampling
    table = core.nc.dram_tensor("corner_table", (IMG * S.CELLS, S.CELL), F32).ap()
    with ExitStack() as keep:
        index = core.sb(keep, "df_index", [TILE, TPI, IMG, S.GT], I32)
        weight = core.sb(keep, "df_weight", [TILE, TPI, IMG, S.GT, S.CORNERS])
        with ExitStack() as mem:
            sample_positions(core, args, mem, table, index, weight)
        with ExitStack() as mem:
            gather_samples(core, args, mem, table, index, weight)


def sample_positions(core, args, mem, table, index, weight):
    nc, norm, X, S = core.nc, core.norm, core.x, Sampling
    G, TAPS, XY, GC, GT, CORNERS, CROWS, CW, CH, BW, BH = S.G, S.TAPS, S.XY, S.GC, S.GT, S.CORNERS, S.CROWS, S.CW, S.CH, S.BW, S.BH
    CELLS, NOFF, NLOG = S.CELLS, S.NOFF, S.NLOG
    table_rows = table.rearrange("(i t p g) d -> i t p (g d)", g=G, p=CROWS * CW, i=IMG)
    sb = lambda name, dims, dt=F32: core.sb(mem, f"df_{name}", dims, dt)
    xpad = sb("padded", [C, BH, BW])
    inside = sb("inside", [1, BH, BW])
    ones = sb("ones", [1, TILE])
    w_in, b_in = sb("w_in", [C, C]), sb("b_in", [1, C])
    taps, dw_bias = sb("taps", [C, TAPS]), sb("dw_bias", [C, 1])
    gamma, beta = sb("gamma", [C, 1]), sb("beta", [C, 1])
    w_log, b_log = sb("w_log", [C, NLOG]), sb("b_log", [1, NLOG])
    THALF = TPI // 2
    cells = [sb(f"cells{k}", [CROWS * CW, G * CORNERS * GC]) for k in range(2)]
    x1 = sb("x1", [C, PIX])
    logit = sb("logits", [TILE, TPI, NLOG])
    pos = sb("pos", [TILE, THALF, GT, XY])
    whole = sb("whole", [TILE, THALF, GT, XY], I32)
    low = sb("low", [TILE, THALF, GT, XY])
    above = sb("above", [TILE, THALF, GT, XY])
    base = sb("base", [TILE, TPI, GT, XY])
    steps = sb("steps", [TILE, TPI * GT], I32)
    part = sb("part", [TILE, 3], I32)
    partf = sb("partf", [TILE, 2])
    row0 = sb("row0", [TILE, THALF * GT])
    mask = sb("mask", [TILE, THALF * G, TAPS])
    top = sb("top", [TILE, THALF * G])
    wy = [sb(f"wy{k}", [TILE, THALF, GT]) for k in range(2)]
    first = FirstTiles(core, args, mem, table, index, weight)
    (s_par, s_zero, s_iota, s_pixel, s_base, s_cell, s_copy, s_conv, s_gelu, s_log, s_logit, s_step, s_exp, s_done) = (
        core.sem(f"df_{n}") for n in ("params", "zero", "iota", "pixel", "base", "cells", "cells_copied", "convolved", "gelu", "logit_products",
                                      "logits", "steps", "exp", "positions"))
    s_table = [core.sem(f"df_table{k}") for k in range(2)]
    NT = CH // CROWS
    EARLY = 4
    NSTEP = 16
    xpad_in = [xpad[:, 1 + HROWS * h:1 + HROWS * (h + 1), 1:1 + COLS] for h in range(2)]
    x13 = x1[:, :].rearrange("c (r w) -> c r w", w=COLS)
    all_ = lambda t: t[:, :, :, :].rearrange("p t s d -> p (t s d)")
    along = lambda t, d: t[:, :, :, d:d + 1].rearrange("p t s d -> p t (s d)")
    NPAR = 10
    core.start_counts()
    with nc.Block() as block:
        @block.sync
        def _(sp):
            p = lambda n: args[f"L0_conv_{n}"]
            row = lambda a: a.rearrange("(o n) -> o n", o=1)
            for dst, src in ((w_in[:, :], p("w_in")), (b_in[:, :], row(p("b_in"))), (dw_bias[:, :], column(p("dw_bias"))),
                             (gamma[:, :], column(p("ln_gamma"))), (beta[:, :], column(p("ln_beta"))),
                             (w_log[:, 0:NOFF], p("w_off")), (w_log[:, NOFF:NLOG], p("w_mask")),
                             (b_log[:, 0:NOFF], row(p("b_off"))), (b_log[:, NOFF:NLOG], row(p("b_mask")))):
                sp.dma_start(dst, src).then_inc(s_par, 16)
            sp.dma_start(taps[:, :], p("dw_kernel").rearrange("a b o c -> c (a b o)"), allow_slow_non_contiguous=True).then_inc(s_par, 16)
            first.load(sp)

            def store_cells(b):
                for t in range(NT):
                    sp.wait_ge(s_copy, START + NT * b + t + 1)
                    sp.dma_start(table_rows[bass.ds(b, 1), t].rearrange("o p d -> p (o d)"), cells[t % 2][:, :]).then_inc(s_table[t % 2], 16)

            store_cells(0)
            sp.wait_ge(first.s_fill, START + 16 * (IMG - 1))
            with sp.Fori(1, IMG) as b:
                store_cells(b)
            for k in range(2):
                sp.wait_ge(s_table[k], START + 16 * NT // 2 * IMG)

        @block.gpsimd
        def _(pool):
            pool.memset(first.samples[0][:, :], 0.0).then_inc(first.s_zero, 1)
            pool.memset(xpad[:, :, :], 0.0).then_inc(s_zero, 1)
            pool.memset(inside[:, :, :], 0.0).then_inc(s_zero, 1)
            pool.memset(ones[:, :], 1.0).then_inc(s_zero, 1)
            pool.wait_ge(s_zero, START + 3)
            pool.memset(inside[:, 1:1 + ROWS, 1:1 + COLS], 1.0).then_inc(s_zero, 1)
            pool.iota(part[:, 0:1], pattern=[[0, 1]], base=0, channel_multiplier=1).then_inc(s_iota, 1)
            for n, pattern in enumerate(([[0, TPI], [0, G], [0, 3], [1, 3]], [[TILE // COLS, TPI], [0, G], [1, 3], [0, 3]], [[0, TPI], [1, G], [0, 3], [0, 3]])):
                if n:
                    pool.wait_ge(s_base, START + n)
                pool.iota(steps[:, :], pattern=pattern, base=0, channel_multiplier=0).then_inc(s_iota, 1)
            pool.wait_ge(first.s_fill, START + 16 * (IMG - 1))
            with pool.Fori(0, IMG) as b:
                for k in range(2):
                    pool.wait_ge(s_table[k], START + 16 * (NT // 2) * (b + 1))
                pool.wait_ge(s_done, START + 2 * b + 1)
                first.gather(pool, b)

        @block.tensor
        def _(pe):
            pe.wait_ge(s_par, START + 16 * NPAR)
            pe.wait_ge(s_zero, START + 4)
            def start(b):
                norm.tensor(pe, 2 * b, x_halves(core, b))

            def prepare(b, start_next):
                for h in range(2):
                    pe.wait_ge(norm.s_out, START + norm.ready(2 * b, h))

                def make_cells(t):
                    bank = core.bank[4 + t % 2]
                    pe.wait_ge(s_copy, START + NT * b + max(0, t - 1))
                    for k in range(CORNERS):
                        dy, dx = divmod(k, 2)
                        at = slice((CROWS * t + dy) * BW + dx, (CROWS * (t + 1) + dy) * BW + dx)
                        out = bank[0:CROWS * CW, k * C:(k + 1) * C]
                        pe.matmul(out, xpad[:, :, :].rearrange("c h w -> c (h w)")[:, at], w_in[:, :], start=True, stop=False)
                        mm = pe.matmul(out, inside[:, :, :].rearrange("c h w -> c (h w)")[:, at], b_in[:, :], start=False, stop=True)
                    mm.then_inc(s_cell, 1)

                for t in range(EARLY):
                    make_cells(t)
                pe.wait_ge(s_conv, START + TAPS * (b + 1))
                norm.tensor(pe, 2 * b + 1, [x1[:, h * HALF:(h + 1) * HALF] for h in range(2)])
                for j in range(TPI):
                    if j % 4 == 0:
                        pe.wait_ge(s_gelu, START + 2 * b + j // 4 + 1)
                    if j % 2 == 0:
                        pe.wait_ge(s_logit, START + 4 * b + max(0, j // 2 - 1))
                    out = core.bank[6 + j // 2 % 2][:, j % 2 * NLOG:(j % 2 + 1) * NLOG]
                    pe.matmul(out, x1[:, j * TILE:(j + 1) * TILE], w_log[:, :], start=True, stop=False)
                    mm = pe.matmul(out, ones[:, :], b_log[:, :], start=False, stop=True)
                    if j % 2:
                        mm.then_inc(s_log, 1)
                start_next(b)
                for t in range(EARLY, NT):
                    make_cells(t)

            first.pipeline(pe, start, prepare, first.tensor)

        @block.scalar
        def _(act):
            act.wait_ge(s_par, START + 16 * NPAR)
            def start(b):
                norm.scalar(act, 2 * b, 1e-6)

            def prepare(b, start_next):

                def copy_cells(t):
                    act.wait_ge(s_cell, START + NT * b + t + 1)
                    act.wait_ge(s_table[t % 2], START + 16 * (NT // 2 * b + t // 2))
                    act.activation(cells[t % 2][:, :].rearrange("p (g k c) -> p k g c", g=G, k=CORNERS),
                                   core.bank[4 + t % 2][0:CROWS * CW, :].rearrange("p (k g c) -> p k g c", g=G, k=CORNERS), ACT.Copy).then_inc(s_copy, 1)

                for t in range(EARLY):
                    copy_cells(t)
                norm.scalar(act, 2 * b + 1, 1e-6)
                for h in range(2):
                    half = x1[:, h * HALF:(h + 1) * HALF]
                    act.wait_ge(norm.s_out, START + norm.ready(2 * b + 1, h))
                    act.activation(half, half, ACT.Gelu, scale=gamma[:, 0:1], bias=beta[:, 0:1]).then_inc(s_gelu, 1)
                act.wait_ge(s_done, START + 2 * b)
                for j in range(4):
                    act.wait_ge(s_log, START + 4 * b + j + 1)
                    act.activation(logit[:, 2 * j:2 * j + 2, :], core.bank[6 + j % 2][:, 0:2 * NLOG].rearrange("p (t n) -> p t n", n=NLOG), ACT.Copy).then_inc(s_logit, 1)
                start_next(b)
                for h in range(2):
                    act.wait_ge(s_step, START + NSTEP * (2 * b + h) + 3)
                    act.activation(mask[:, :, :], mask[:, :, :], ACT.Exp).then_inc(s_exp, 1)
                    for t in range(EARLY, NT if h == 0 else EARLY):
                        copy_cells(t)

            first.pipeline(act, start, prepare, first.scalar)

        def positions(dve, b, h):
            count = 0
            at = slice(h * THALF, (h + 1) * THALF)

            def step(ins):
                nonlocal count
                count += 1
                return ins.then_inc(s_step, 1)

            def after(n):
                dve.wait_ge(s_step, START + NSTEP * (2 * b + h) + n)

            ml = logit[:, at, NOFF:NLOG].rearrange("p t (g k) -> p t g k", k=TAPS)
            mg = mask[:, :, :].rearrange("p (t g) k -> p t g k", g=G)
            m3 = mask[:, :, :].rearrange("p (t g) k -> p t (g k)", g=G)
            top_t = top[:, :].rearrange("p (t g) -> p t g", g=G)
            top_wide = top[:, :].rearrange("p (n k) -> p n k", k=1).broadcast_to([TILE, THALF * G, TAPS])
            by_tile = lambda t: t.rearrange("p t s d -> p t (s d)")
            dve.wait_ge(s_done, START + 2 * b + h)
            step(dve.tensor_reduce(top_t, ml, AX.X, ALU.max))
            step(dve.tensor_tensor(by_tile(pos[:, :, :, :]), logit[:, at, 0:NOFF], by_tile(base[:, at, :, :]), ALU.add))
            after(1)
            step(dve.tensor_tensor(mg, ml, top_t.rearrange("p t (g k) -> p t g k", k=1).broadcast_to([TILE, THALF, G, TAPS]), ALU.subtract))
            after(2)
            step(dve.tensor_scalar(all_(pos), all_(pos), 0.0, float(COLS + 1), ALU.max, ALU.min))
            after(4)
            step(dve.tensor_copy(all_(whole), all_(pos)))
            after(5)
            step(dve.tensor_copy(all_(low), all_(whole)))
            after(6)
            step(dve.tensor_tensor(all_(above), all_(low), all_(pos), ALU.is_gt))
            after(7)
            step(dve.tensor_tensor(all_(low), all_(low), all_(above), ALU.subtract))
            after(8)
            step(dve.tensor_tensor(all_(pos), all_(pos), all_(low), ALU.subtract))
            after(9)
            step(dve.tensor_scalar(all_(above), all_(pos), -1.0, 1.0, ALU.mult, ALU.add))
            flat = lambda t: t[:, :, :].rearrange("p t s -> p (t s)")
            step(dve.scalar_tensor_tensor(out=flat(wy[0]), in0=along(low, 1), scalar=float(CW), in1=along(low, 0), op0=ALU.mult, op1=ALU.add))
            after(11)
            step(dve.scalar_tensor_tensor(out=index[:, at, bass.ds(b, 1), :].rearrange("p t b s -> p t (b s)"), in0=wy[0][:, :, :], scalar=float(G),
                                          in1=row0[:, :].rearrange("p (t s) -> p t s", s=GT), op0=ALU.mult, op1=ALU.add))
            dve.wait_ge(s_exp, START + 2 * b + h + 1)
            step(dve.tensor_reduce(top[:, :], mask[:, :, :], AX.X, ALU.add))
            after(13)
            step(dve.reciprocal(top[:, :], top[:, :]))
            after(12)
            if h:
                dve.tensor_scalar(row0[:, :], row0[:, :], float(CELLS), None, ALU.add)
            after(14)
            step(dve.tensor_tensor(mask[:, :, :], mask[:, :, :], top_wide, ALU.mult))
            after(15)
            dve.tensor_tensor(flat(wy[0]), along(above, 1), m3.rearrange("p t s -> p (t s)"), ALU.mult)
            step(dve.tensor_tensor(flat(wy[1]), along(pos, 1), m3.rearrange("p t s -> p (t s)"), ALU.mult))
            after(16)
            for k in range(CORNERS):
                dy, dx = divmod(k, 2)
                out = weight[:, at, bass.ds(b, 1), :, k:k + 1].rearrange("p t b s k -> p t (b s k)")
                ins = dve.tensor_tensor(out, wy[dy][:, :, :], (pos if dx else above)[:, :, :, 0:1].rearrange("p t s d -> p t (s d)"), ALU.mult)
            ins.then_inc(s_done, 1)
            assert count == NSTEP

        @block.vector
        def _(dve):
            dve.wait_ge(s_iota, START + 1)
            dve.tensor_scalar(part[:, 1:2], part[:, 0:1], COLS - 1, None, ALU.bitwise_and).then_inc(s_pixel, 1)
            dve.tensor_scalar(part[:, 2:3], part[:, 0:1], COLS.bit_length() - 1, None, ALU.logical_shift_right).then_inc(s_pixel, 1)
            dve.wait_ge(s_pixel, START + 2)
            dve.tensor_copy(partf[:, :], part[:, 1:3]).then_inc(s_pixel, 1)
            dve.wait_ge(s_pixel, START + 3)
            flat_steps = steps[:, :].rearrange("p (t s) -> p t s", s=GT)
            for d in range(XY):
                dve.wait_ge(s_iota, START + 2 + d)
                dve.tensor_scalar(along(base, d), flat_steps, partf[:, d:d + 1], None, ALU.add).then_inc(s_base, 1)
            dve.wait_ge(s_iota, START + 4)
            dve.tensor_copy(row0[:, :], steps[:, 0:THALF * GT]).then_inc(s_base, 1)
            dve.wait_ge(s_base, START + 3)
            dve.wait_ge(s_par, START + 16 * NPAR)
            dve.wait_ge(s_zero, START + 4)
            def start(b):
                norm.centre(dve, 2 * b, x_halves(core, b))

            def prepare(b, start_next):
                dve.wait_ge(s_cell, START + NT * b)
                norm.finish(dve, 2 * b, xpad_in)
                for h in range(2):
                    dve.wait_ge(norm.s_out, START + norm.ready(2 * b, h))
                dve.wait_ge(s_log, START + 4 * b)
                for t in range(TAPS):
                    win = xpad[:, t // 3:t // 3 + ROWS, t % 3:t % 3 + COLS]
                    if t == 0:
                        dve.tensor_scalar(x13, win, taps[:, 0:1], dw_bias[:, 0:1], ALU.mult, ALU.add).then_inc(s_conv, 1)
                        continue
                    dve.wait_ge(s_conv, START + TAPS * b + t)
                    dve.scalar_tensor_tensor(out=x13, in0=win, scalar=taps[:, t:t + 1], in1=x13, op0=ALU.mult, op1=ALU.add).then_inc(s_conv, 1)
                dve.wait_ge(s_conv, START + TAPS * (b + 1))
                norm.vector(dve, 2 * b + 1, [x1[:, h * HALF:(h + 1) * HALF] for h in range(2)], [x13[:, 0:HROWS], x13[:, HROWS:ROWS]])
                start_next(b)
                if not is_first(b):
                    first.sum_half(dve, b - 1, 0, s_done)
                dve.wait_ge(s_logit, START + 4 * b + 4)
                for h in range(2):
                    positions(dve, b, h)

            first.pipeline(dve, start, prepare, lambda d, b: first.vector(d, b, s_done))
    norm.done(2)


class FirstTiles:

    def __init__(self, core, args, mem, table, index, weight):
        self.core, self.args, self.table, self.index, self.weight = core, args, table, index, weight
        S = Sampling
        sb = lambda name, dims, dt=F32: core.sb(mem, f"first_{name}", dims, dt)
        self.N = S.GT // 2
        self.own = [sb(f"own_index{k}", [TILE, self.N], I32) for k in range(2)]
        self.samples = [sb(f"samples{k}", [TILE, self.N * S.CELL]) for k in range(2)]
        self.summed = sb("summed", [TILE, C])
        self.turned = sb("turned", [C, TILE])
        self.w_out, self.b_out = sb("w_out", [C, C]), sb("b_out", [C, 1])
        self.s_par, self.s_begun, self.s_own, self.s_weighted, self.s_turn, self.s_copy, self.s_out, self.s_end = (
            core.sem(f"first_{n}") for n in ("params", "begun", "own_index", "weighted", "turned", "turned_copied", "out_product", "end"))
        self.s_sum = [core.sem(f"first_summed{k}") for k in range(2)]
        self.s_zero, self.s_fill = core.sem("first_zero"), core.sem("first_filled")
        self.s_got = [core.indirect_sem() for k in range(2)]

    def pipeline(self, eng, start, prepare, tile):
        start(0)
        prepare(0, lambda b: start(b + 1))
        with eng.Fori(1, IMG - 1) as b:
            prepare(b, lambda b: start(b + 1))
            tile(eng, b - 1)
        prepare(IMG - 1, lambda b: None)
        tile(eng, IMG - 2)
        tile(eng, IMG - 1)

    def load(self, sp):
        S, FILL = Sampling, 1280
        PARTS = S.CELLS * S.CELL // (4 * FILL)
        image_table = self.table.rearrange("(i p r) d -> i p (r d)", i=IMG, p=PARTS)
        sp.wait_ge(self.s_zero, START + 1)
        zeros = self.samples[0][0:PARTS, 0:FILL].rearrange("p (o f) -> p o f", o=1).broadcast_to([PARTS, 4, FILL])
        for b in range(1, IMG):
            sp.dma_start(image_table[b].rearrange("p (o f) -> p o f", o=4), zeros).then_inc(self.s_fill, 16)
        sp.dma_start(self.w_out[:, :], self.args["L0_conv_w_out"]).then_inc(self.s_par, 16)
        sp.dma_start(self.b_out[:, :], column(self.args["L0_conv_b_out"])).then_inc(self.s_par, 16)

    def gather(self, pool, b):
        S, N = Sampling, self.N
        for k in range(2):
            pool.wait_ge(self.s_sum[k], START + b)
            pool.sem_inc(self.s_begun, 1)
            pool.tensor_copy(self.own[k][:, :], self.index[:, 0, bass.ds(b, 1), k * N:(k + 1) * N].rearrange("p o s -> p (o s)")).then_inc(self.s_own, 1)
            pool.wait_ge(self.s_own, START + 2 * b + k + 1)
            pool.sem_inc(self.s_begun, 1)
            for s in range(N):
                pool.indirect_dma_start(self.samples[k][:, s * S.CELL:(s + 1) * S.CELL], None, self.table[:, :],
                                        bass.IndirectOffsetOnAxis(ap=self.own[k][:, s:s + 1], axis=0)).then_inc(self.s_got[k], 16)

    def tensor(self, pe, b):
        pe.wait_ge(self.s_par, START + 32)
        pe.wait_ge(self.s_sum[1], START + b + 1)
        pe.transpose(self.core.bank[0][:, 0:TILE], self.summed[:, :], self.core.ident[:, :]).then_inc(self.s_turn, 1)
        pe.wait_ge(self.s_copy, START + b + 1)
        pe.matmul(self.core.bank[1][:, 0:TILE], self.w_out[:, :], self.turned[:, :], start=True, stop=True).then_inc(self.s_out, 1)

    def scalar(self, act, b):
        act.wait_ge(self.s_turn, START + b + 1)
        act.activation(self.turned[:, :], self.core.bank[0][:, 0:TILE], ACT.Copy).then_inc(self.s_copy, 1)

    def sum_half(self, dve, b, k, s_done):
        S, N = Sampling, self.N
        G, HALFC = S.G // 2, C // 2
        dve.wait_ge(s_done, START + 2 * b + 1)
        dve.wait_ge(self.s_turn, START + b)
        dve.wait_ge(self.s_got[k], 16 * N * (b + 1))
        by_value = self.samples[k][:, :].rearrange("p (s c) -> p s c", c=S.GC)
        w = (self.weight[:, 0, bass.ds(b, 1), k * N:(k + 1) * N, :].rearrange("p o s (k c) -> p (o s k) c", c=1)
             .broadcast_to([TILE, N * S.CORNERS, S.GC]))
        dve.tensor_tensor(by_value, by_value, w, ALU.mult).then_inc(self.s_weighted, 1)
        dve.wait_ge(self.s_weighted, START + 2 * b + k + 1)
        dve.tensor_reduce(self.summed[:, k * HALFC:(k + 1) * HALFC].rearrange("p (g c) -> p g c", g=G),
                          self.samples[k][:, :].rearrange("p (g s c) -> p g c s", g=G, c=S.GC), AX.X, ALU.add).then_inc(self.s_sum[k], 1)

    def vector(self, dve, b, s_done):
        if is_last(b, IMG):
            self.sum_half(dve, b, 0, s_done)
        self.sum_half(dve, b, 1, s_done)
        xs = self.core.x[:, bass.ds(b * PIX, TILE)]
        dve.wait_ge(self.s_out, START + b + 1)
        dve.scalar_tensor_tensor(out=xs, in0=self.core.bank[1][:, 0:TILE], scalar=self.b_out[:, 0:1], in1=xs, op0=ALU.add, op1=ALU.add).then_inc(self.s_end, 1)


def gather_samples(core, args, mem, table, index, weight):
    X, norm, S = core.x, core.norm, Sampling
    G, GC, GT, CORNERS, CELL, TILES = S.G, S.GC, S.GT, S.CORNERS, S.CELL, S.TILES
    GATES = (("i", 0.5), ("o", 0.5), ("c", 1.0))
    NG = len(GATES)
    W = NG * IMG
    SLOT = TILE // IMG
    UNROLL = 8
    NM = 2 * NG
    sb = lambda name, dims, dt=F32: core.sb(mem, f"dg_{name}", dims, dt)
    own = [sb(f"own_index{k}", [TILE, GT], I32) for k in range(2)]
    samples = [sb(f"samples{k}", [TILE, GT * CELL]) for k in range(2)]
    summed = [sb(f"summed{k}", [TILE, C]) for k in range(2)]
    turned = [sb(f"turned{k}", [C, TILE]) for k in range(2)]
    w_out, b_out = sb("w_out", [C, C]), sb("b_out", [C, 1])
    v = sb("v", [C, PIX])
    v3 = v[:, :].rearrange("c (b t) -> c b t", t=TILE)
    wu, wv, bias = sb("u_w", [C, NG, C]), sb("v_w", [C, NG, C]), sb("gate_bias", [C, NG])
    gx = sb("gate_inputs", [C, TILE, W])
    hs = sb("hidden", [C, TILE + 1, IMG])
    gates = sb("gates", [C, W])
    cell, hc, tc, ig, og = (sb(n, [C, IMG]) for n in ("cell", "hc", "tanh_cell", "ig", "og"))
    (s_par, s_half, s_zero, s_begun, s_own, s_weighted, s_turn, s_copy, s_out, s_end, s_gmm, s_gx,
     s_pre, s_tanh, s_ig, s_og, s_cell, s_tc, s_h, s_hc, s_carry, s_x) = (core.sem(f"dg_{n}") for n in (
        "params", "halved", "zero", "begun", "own_index", "weighted", "turned", "turned_copied", "out_product", "end", "gate_products",
        "gate_inputs", "preacts", "tanh", "ig", "og", "cell", "tanh_cell", "hidden", "hc", "carried", "x"))
    s_sum = [core.sem(f"dg_summed{k}") for k in range(2)]
    NS = 4
    s_got = [[core.indirect_sem() for n in range(NS)] for k in range(2)]
    PER = GT // NS
    NPAR = 2 + 3 * NG
    tokens = X[:, :].rearrange("c (b j t) -> c b j t", b=IMG, j=TPI)

    def phase_half(j, h):
        return tokens[:, 4 * h:4 * h + 4, bass.ds(j, 1), :].rearrange("c b j t -> c b (j t)")

    def slots(eng, steps, tile, finish):
        finish(0)
        with eng.Fori(1, TPI) as j:
            with eng.Fori(0, IMG // 2) as p:
                for k in range(2):
                    with eng.Fori(0, SLOT // UNROLL) as s:
                        for u in range(UNROLL):
                            at = (2 * p + k) * SLOT + s * UNROLL + u
                            steps((j - 1) * TILE + at, at, u)
                    tile(j, p, k)
            finish(j)
        with eng.Fori(0, TILE // UNROLL) as s:
            for u in range(UNROLL):
                steps((TPI - 1) * TILE + s * UNROLL + u, s * UNROLL + u, u)

    core.start_counts()
    with core.nc.Block() as block:
        @block.sync
        def _(sp):
            sp.dma_start(w_out[:, :], args["L0_conv_w_out"]).then_inc(s_par, 16)
            sp.dma_start(b_out[:, :], column(args["L0_conv_b_out"])).then_inc(s_par, 16)
            for n, (g, _) in enumerate(GATES):
                sp.dma_start(wu[:, n, :], args[f"L0_ffn_U_{g}"]).then_inc(s_par, 16)
                sp.dma_start(wv[:, n, :], args[f"L0_ffn_V_{g}"]).then_inc(s_par, 16)
                sp.dma_start(bias[:, n:n + 1], column(args[f"L0_ffn_b_{g}"])).then_inc(s_par, 16)

        @block.gpsimd
        def _(pool):
            pool.memset(hs[:, 0:1, :], 0.0).then_inc(s_zero, 1)
            pool.memset(hc[:, :], 0.0).then_inc(s_zero, 1)
            rows = index[:, :, :, :].rearrange("p t b s -> p (t b s)")
            with pool.Fori(0, (TILES - IMG) // 2) as p:
                for k in range(2):
                    pool.wait_ge(s_sum[k], START + p)
                    pool.sem_inc(s_begun, 1)
                    pool.tensor_copy(own[k][:, :], rows[:, bass.ds((2 * p + k + IMG) * GT, GT)]).then_inc(s_own, 1)
                    pool.wait_ge(s_own, START + 2 * p + k + 1)
                    pool.sem_inc(s_begun, 1)
                    for s in range(GT):
                        pool.indirect_dma_start(samples[k][:, s * CELL:(s + 1) * CELL], None, table[:, :],
                                                bass.IndirectOffsetOnAxis(ap=own[k][:, s:s + 1], axis=0)).then_inc(s_got[k][s // PER], 16)

        @block.tensor
        def _(pe):
            def steps(t, at, u):
                bank = core.bank[4 + u % 2]
                pe.matmul(bank[:, 0:W], core.ident[:, :], gx[:, bass.ds(at, 1), :].rearrange("c o w -> c (o w)"), start=True, stop=False)
                pe.wait_ge(s_h, START + t)
                for g in range(NG):
                    mm = pe.matmul(bank[:, g * IMG:(g + 1) * IMG], wv[:, g, :], hs[:, bass.ds(at, 1), :].rearrange("c o w -> c (o w)"),
                                   start=False, stop=(g == NG - 1))
                mm.then_inc(s_pre, 1)

            def tile(j, p, k):
                q = (j - 1) * (IMG // 2) + p
                pe.wait_ge(s_sum[k], START + q + 1)
                pe.transpose(core.bank[6][:, k * TILE:(k + 1) * TILE], summed[k][:, :], core.ident[:, :]).then_inc(s_turn, 1)
                pe.wait_ge(s_copy, START + 2 * q + k + 1)
                pe.matmul(core.bank[7][:, k * TILE:(k + 1) * TILE], w_out[:, :], turned[k][:, :], start=True, stop=True).then_inc(s_out, 1)

            def finish(j):
                pe.wait_ge(s_end, START + IMG * j)
                norm.tensor(pe, j, [phase_half(j, h) for h in range(2)])
                for h in range(2):
                    pe.wait_ge(norm.s_out, START + norm.ready(j, h))
                    for g in range(NG):
                        m = NG * h + g
                        pe.wait_ge(s_gx, START + NM * j + max(0, m - 3))
                        pe.matmul(core.bank[4 + m % 4][:, :], wu[:, g, :], v[:, h * HALF:(h + 1) * HALF], start=True, stop=True).then_inc(s_gmm, 1)
                pe.wait_ge(s_gx, START + NM * (j + 1))
                pe.wait_ge(s_carry, START + j)

            pe.wait_ge(s_par, START + 16 * NPAR)
            pe.wait_ge(s_half, START + 2)
            pe.wait_ge(s_zero, START + 2)
            slots(pe, steps, tile, finish)

        @block.scalar
        def _(act):
            def steps(t, at, u):
                act.wait_ge(s_pre, START + t + 1)
                act.activation(gates[:, :], core.bank[4 + u % 2][:, 0:W], ACT.Tanh).then_inc(s_tanh, 1)
                act.wait_ge(s_cell, START + t + 1)
                act.activation(tc[:, :], cell[:, :], ACT.Tanh).then_inc(s_tc, 1)

            def tile(j, p, k):
                act.wait_ge(s_turn, START + 2 * ((j - 1) * (IMG // 2) + p) + k + 1)
                act.activation(turned[k][:, :], core.bank[6][:, k * TILE:(k + 1) * TILE], ACT.Copy).then_inc(s_copy, 1)

            def finish(j):
                norm.scalar(act, j, 1e-5)
                for h in range(2):
                    for g, (_, scale) in enumerate(GATES):
                        m = NG * h + g
                        act.wait_ge(s_gmm, START + NM * j + m + 1)
                        act.activation(gx[:, :, g * IMG + 4 * h:g * IMG + 4 * h + 4].rearrange("c t b -> c b t"),
                                       core.bank[4 + m % 4][:, :].rearrange("c (b t) -> c b t", t=TILE), ACT.Identity,
                                       bias=bias[:, g:g + 1], scale=scale).then_inc(s_gx, 1)

            act.wait_ge(s_half, START + 2)
            slots(act, steps, tile, finish)

        @block.vector
        def _(dve):
            def steps(t, at, u):
                dve.wait_ge(s_tanh, START + t + 1)
                dve.scalar_tensor_tensor(out=ig[:, :], in0=gates[:, 0:IMG], scalar=1.0, in1=gates[:, 2 * IMG:W], op0=ALU.add, op1=ALU.mult).then_inc(s_ig, 1)
                dve.tensor_scalar(og[:, :], gates[:, IMG:2 * IMG], 0.5, 0.5, ALU.mult, ALU.add).then_inc(s_og, 1)
                dve.wait_ge(s_hc, START + t)
                dve.wait_ge(s_ig, START + t + 1)
                dve.scalar_tensor_tensor(out=cell[:, :], in0=ig[:, :], scalar=0.5, in1=hc[:, :], op0=ALU.mult, op1=ALU.add).then_inc(s_cell, 1)
                dve.wait_ge(s_og, START + t + 1)
                dve.wait_ge(s_tc, START + t + 1)
                now = hs[:, bass.ds(at + 1, 1), :].rearrange("c o w -> c (o w)")
                dve.tensor_tensor(now, og[:, :], tc[:, :], ALU.mult).then_inc(s_h, 1)
                dve.wait_ge(s_h, START + t + 1)
                dve.tensor_tensor(hc[:, :], now, cell[:, :], ALU.mult).then_inc(s_hc, 1)

            def tile(j, p, k):
                q = (j - 1) * (IMG // 2) + p
                for s in range(NS):
                    dve.wait_ge(s_got[k][s], 16 * PER * (q + 1))
                by_value = samples[k][:, :].rearrange("p (s c) -> p s c", c=GC)
                flat = weight[:, :, :, :, :].rearrange("p t b s k -> p (t b s k)")
                w = flat[:, bass.ds((2 * q + k + IMG) * (GT * CORNERS), GT * CORNERS)].rearrange("p (s c) -> p s c", c=1).broadcast_to([TILE, GT * CORNERS, GC])
                dve.tensor_tensor(by_value, by_value, w, ALU.mult).then_inc(s_weighted, 1)
                dve.wait_ge(s_weighted, START + 2 * q + k + 1)
                dve.tensor_reduce(summed[k][:, :].rearrange("p (g c) -> p g c", g=G), samples[k][:, :].rearrange("p (g s c) -> p g c s", g=G, c=GC), AX.X, ALU.add).then_inc(s_sum[k], 1)
                xs = X[:, bass.ds((2 * p + k) * PIX + j * TILE, TILE)]
                dve.wait_ge(s_out, START + 2 * q + k + 1)
                dve.scalar_tensor_tensor(out=xs, in0=core.bank[7][:, k * TILE:(k + 1) * TILE], scalar=b_out[:, 0:1], in1=xs, op0=ALU.add, op1=ALU.add).then_inc(s_end, 1)

            def add_hidden(j):
                dve.wait_ge(s_h, START + TILE * (j + 1))
                xs = tokens[:, :, bass.ds(j, 1), :].rearrange("c b j t -> c b (j t)")
                dve.tensor_tensor(xs, xs, hs[:, 1:TILE + 1, :].rearrange("c t b -> c b t"), ALU.add).then_inc(s_x, 1)
                dve.tensor_copy(hs[:, 0:1, :], hs[:, TILE:TILE + 1, :]).then_inc(s_carry, 1)

            def finish(j):
                if not isinstance(j, int):
                    add_hidden(j - 1)
                dve.wait_ge(s_end, START + IMG * j)
                norm.vector(dve, j, [phase_half(j, h) for h in range(2)], [v3[:, 4 * h:4 * h + 4] for h in range(2)], TILE)

            dve.wait_ge(s_par, START + 16 * NPAR)
            dve.tensor_scalar(wv[:, 0:2, :], wv[:, 0:2, :], 0.5, None, ALU.mult).then_inc(s_half, 1)
            dve.tensor_scalar(bias[:, 0:2], bias[:, 0:2], 0.5, None, ALU.mult).then_inc(s_half, 1)
            dve.wait_ge(s_zero, START + 2)
            slots(dve, steps, tile, finish)
            add_hidden(TPI - 1)
    norm.done()


def divisive_mixer(core, args):
    nc, norm, X = core.nc, core.norm, core.x
    G = 8
    PE_TAPS = 4
    with ExitStack() as mem:
        v = [core.sb(mem, f"dv_v{k}", [C, PIX]) for k in range(2)]
        v2 = [core.sb(mem, f"dv_squares{k}", [C, PAD, PAD]) for k in range(2)]
        pool_w = core.sb(mem, "dv_pool_w", [C, C])
        taps = core.sb(mem, "dv_taps", [C, 9])
        vecs = core.sb(mem, "dv_vecs", [C, 3])
        beta = core.sb(mem, "dv_beta", [C, 1])
        acc = [core.sb(mem, f"dv_acc{k}", [C, PIX]) for k in range(2)]
        diag = core.sb(mem, "dv_diagonals", [C, PE_TAPS, C])
        s_diag = core.sem("dv_diagonals_made")
        s_zero, s_par, s_beta, s_v2, s_pool, s_acc, s_den, s_log, s_rsqrt, s_end = (
            core.sem(f"dv_{n}") for n in ("zero", "params", "beta", "squares", "pooled", "acc", "den", "log", "rsqrt", "end"))
        TAPS = [t for t in range(9) if t != 4]
        DVE_TAPS = TAPS[:-PE_TAPS]
        NACC = len(DVE_TAPS) + 1
        NPAR = 4 + C // G
        core.start_counts()
        with nc.Block() as block:
            @block.gpsimd
            def _(pool):
                pool.memset(pool_w[:, :], 0.0).then_inc(s_zero, 1)
                for k in range(2):
                    pool.memset(v2[k][:, :, :], 0.0).then_inc(s_zero, 1)
                pool.wait_ge(s_par, START + 16 * NPAR)
                pool.tensor_scalar(beta[:, :], vecs[:, 0:1], 1e-6, None, ALU.add).then_inc(s_beta, 1)

            @block.sync
            def _(sp):
                sp.dma_start(taps[:, :], args["L1_conv_gamma_s"].rearrange("a b c o -> c (a b o)"), allow_slow_non_contiguous=True).then_inc(s_par, 16)
                for n, name in enumerate(("beta", "gamma_outside", "beta_outside")):
                    sp.dma_start(vecs[:, n:n + 1], column(args[f"L1_conv_{name}"])).then_inc(s_par, 16)
                sp.wait_ge(s_zero, START + 1)
                for g in range(C // G):
                    sp.dma_start(pool_w[G * g:G * g + G, G * g:G * g + G], args["L1_conv_gamma_k"][0, 0, :, G * g:G * g + G]).then_inc(s_par, 16)

            @block.tensor
            def _(pe):
                pe.wait_ge(s_par, START + 16 * NPAR)
                pe.wait_ge(s_diag, START + PE_TAPS)

                def pool_squares(b, k):
                    pe.wait_ge(s_den, START + b)
                    pe.wait_ge(s_v2, START + b + 1)
                    for h in range(2):
                        pe.matmul(image(core.bank[4 + h]), pool_w[:, :], inner(v2[k], h), start=True, stop=False)
                        for n, t in enumerate(TAPS[-PE_TAPS:]):
                            mm = pe.matmul(image(core.bank[4 + h]), diag[:, n, :], window(v2[k], h, t), start=False, stop=(n == PE_TAPS - 1))
                    mm.then_inc(s_pool, 1)

                ahead_by_parity(pe, IMG, lambda b, k: None, lambda b: norm.tensor(pe, b, x_halves(core, b)), pool_squares)

            @block.scalar
            def _(act):
                act.preload_act_table_set(LOG_EXP)
                act.wait_ge(s_zero, START + 3)
                act.wait_ge(s_beta, START + 1)

                def squares(b, k):
                    act.wait_ge(norm.s_out, START + norm.ready(b, 1))
                    if not isinstance(b, int) or b > 1:
                        act.wait_ge(s_pool, START + b - 1)
                        act.wait_ge(s_acc, START + NACC * (b - 1))
                    act.activation(v2[k][:, 1:1 + ROWS, 1:1 + COLS], image(v[k]), ACT.Square).then_inc(s_v2, 1)

                def rsqrt(b, k):
                    act.wait_ge(s_den, START + b + 1)
                    act.activation(acc[k][:, :], acc[k][:, :], ACT.Ln, bias=beta[:, 0:1]).then_inc(s_log, 1)
                    act.wait_ge(s_log, START + b + 1)
                    act.activation(acc[k][:, :], acc[k][:, :], ACT.Exp, scale=-0.5).then_inc(s_rsqrt, 1)

                ahead_by_parity(act, IMG, squares, lambda b: norm.scalar(act, b, 1e-6), lambda b, k: None if is_first(b) else rsqrt(b - 1, 1 - k))
                rsqrt(IMG - 1, (IMG - 1) % 2)

            @block.vector
            def _(dve):
                dve.wait_ge(s_par, START + 16 * NPAR)

                for n, t in enumerate(TAPS[-PE_TAPS:]):
                    dve.tensor_scalar(diag[:, n, :], core.ident[:, :], taps[:, t:t + 1], None, ALU.mult).then_inc(s_diag, 1)

                def normalise(b, k):
                    if not isinstance(b, int) or b > 1:
                        dve.wait_ge(s_end, START + 2 * (b - 1))
                    norm.finish(dve, b, [image(v[k][:, h * HALF:(h + 1) * HALF]) for h in range(2)])

                def finish(b, k):
                    dve.wait_ge(s_rsqrt, START + b + 1)
                    dve.scalar_tensor_tensor(out=acc[k][:, :], in0=v[k][:, :], scalar=vecs[:, 1:2], in1=acc[k][:, :], op0=ALU.mult, op1=ALU.mult).then_inc(s_end, 1)
                    dve.wait_ge(s_end, START + 2 * b + 1)
                    xs = X[:, bass.ds(b * PIX, PIX)]
                    dve.scalar_tensor_tensor(out=xs, in0=acc[k][:, :], scalar=vecs[:, 2:3], in1=xs, op0=ALU.add, op1=ALU.add).then_inc(s_end, 1)

                def add_pool(b, k):
                    dve.wait_ge(s_acc, START + NACC * b + len(DVE_TAPS))
                    dve.wait_ge(s_pool, START + b + 1)
                    dve.tensor_tensor(acc[k][:, 0:HALF], acc[k][:, 0:HALF], core.bank[4][:, :], ALU.add).then_inc(s_acc, 1)
                    dve.tensor_tensor(acc[k][:, HALF:PIX], acc[k][:, HALF:PIX], core.bank[5][:, :], ALU.add).then_inc(s_den, 1)

                def surround(b, k):
                    if not is_first(b):
                        add_pool(b - 1, 1 - k)
                    dve.wait_ge(s_v2, START + b + 1)
                    for n, t in enumerate(DVE_TAPS):
                        win = v2[k][:, t // 3:t // 3 + ROWS, t % 3:t % 3 + COLS]
                        if n == 0:
                            dve.tensor_scalar(image(acc[k]), win, taps[:, t:t + 1], None, ALU.mult).then_inc(s_acc, 1)
                            continue
                        dve.wait_ge(s_acc, START + NACC * b + n)
                        dve.scalar_tensor_tensor(out=image(acc[k]), in0=win, scalar=taps[:, t:t + 1], in1=image(acc[k]), op0=ALU.mult, op1=ALU.add).then_inc(s_acc, 1)
                    if not is_first(b):
                        finish(b - 1, 1 - k)

                ahead_by_parity(dve, IMG, normalise, lambda b: norm.centre(dve, b, x_halves(core, b)), surround)
                add_pool(IMG - 1, (IMG - 1) % 2)
                finish(IMG - 1, (IMG - 1) % 2)
        norm.done()


def routed_depth_ffn(core, args):
    nc, norm, X = core.nc, core.norm, core.x
    HID = args["L1_ffn_w1"].shape[1]
    NHC = HID // C
    CHOSEN = PIX // 2 - 1
    with ExitStack() as mem:
        v = core.sb(mem, "rd_v", [C, TOK])
        half = lambda b, h: v[:, bass.ds(b * PIX + h * HALF, HALF)]
        wr = core.sb(mem, "rd_wr", [C, 1])
        wr_wide = core.sb(mem, "rd_wr_wide", [C, C])
        br = core.sb(mem, "rd_br", [C, 1])
        w1 = core.sb(mem, "rd_w1", [C, HID])
        w2 = core.sb(mem, "rd_w2", [C, NHC, C])
        b1 = core.sb(mem, "rd_b1", [C, NHC])
        b2 = core.sb(mem, "rd_b2", [C, 1])
        ones = core.sb(mem, "rd_ones", [C, C], BF16)
        before = core.sb(mem, "rd_before", [C, C])
        weight = core.sb(mem, "rd_weight", [C, PIX])
        wcol = core.sb(mem, "rd_weight_col", [C, TPI])
        diag = core.sb(mem, "rd_diag", [C, TILE])
        equal = core.sb(mem, "rd_equal", [C, TILE])
        less = core.sb(mem, "rd_less", [C, TILE])
        precedes = core.sb(mem, "rd_ahead", [C, TPI, PIX], BF16)
        coef = core.sb(mem, "rd_coef", [C, PIX])
        hid = [core.sb(mem, f"rd_hidden{k}", [C, HALF]) for k in range(2)]
        y = [core.sb(mem, f"rd_y{h}", [C, HALF]) for h in range(2)]
        (s_par, s_const, s_wide, s_wmm, s_weight, s_diag, s_tie, s_ahead, s_rank, s_coef, s_h1, s_hid, s_y, s_ysum, s_end) = (
            core.sem(f"rd_{n}") for n in ("params", "const", "wide", "weight_product", "weight", "weight_col", "ties", "ahead", "rank",
                                          "coef", "hidden_product", "hidden", "y_product", "y_weighted", "end"))
        NPAR = 5 + NHC
        NH1 = 2 * NHC
        core.start_counts()
        with nc.Block() as block:
            @block.sync
            def _(sp):
                sp.dma_start(wr[:, :], args["L1_ffn_wr"]).then_inc(s_par, 16)
                sp.dma_start(br[:, :], args["L1_ffn_br"].rearrange("(a o) -> a o", o=1).broadcast_to([C, 1])).then_inc(s_par, 16)
                sp.dma_start(w1[:, :], args["L1_ffn_w1"]).then_inc(s_par, 16)
                sp.dma_start(w2[:, :, :], args["L1_ffn_w2"].rearrange("(k p) d -> p k d", p=C)).then_inc(s_par, 16)
                sp.dma_start(b2[:, :], column(args["L1_ffn_b2"])).then_inc(s_par, 16)
                for k in range(NHC):
                    sp.dma_start(b1[:, k:k + 1], column(args["L1_ffn_b1"][k * C:(k + 1) * C])).then_inc(s_par, 16)

            @block.gpsimd
            def _(pool):
                pool.memset(ones[:, :], 1.0).then_inc(s_const, 1)
                pool.memset(before[:, :], 1.0).then_inc(s_const, 1)
                pool.wait_ge(s_const, START + 2)
                pool.affine_select(out=before[:, :], in_=before[:, :], compare_op=ALU.is_gt, fill=0.0,
                                   base=0, pattern=[[1, C]], channel_multiplier=-1).then_inc(s_const, 1)

            @block.tensor
            def _(pe):
                pe.wait_ge(s_par, START + 16 * NPAR)
                pe.wait_ge(s_wide, START + 1)
                pe.wait_ge(s_const, START + 3)

                def hidden_product(b, h, k):
                    m = NHC * h + k
                    pe.wait_ge(s_hid, START + NH1 * b + max(0, m - 1))
                    pe.matmul(core.bank[6 + m % 2][:, :], w1[:, k * C:(k + 1) * C], half(b, h), start=True, stop=True).then_inc(s_h1, 1)

                def weights(b):
                    for h in range(2):
                        pe.wait_ge(s_weight, START + 2 * b)
                        pe.matmul(core.bank[2 + h][:, :], wr_wide[:, :], half(b, h), start=True, stop=True).then_inc(s_wmm, 1)
                    hidden_product(b, 0, 0)
                    hidden_product(b, 0, 1)

                def outputs_and_ranks(b):
                    pe.wait_ge(s_ysum, START + 2 * b)
                    for h in range(2):
                        for k in range(NHC):
                            m = NHC * h + k
                            pe.wait_ge(s_hid, START + NH1 * b + m + 1)
                            pe.matmul(core.bank[4 + h][:, :], w2[:, k, :], hid[m % 2][:, :], start=(k == 0), stop=(k == NHC - 1)).then_inc(s_y, 1)
                            if m + 2 < NH1:
                                hidden_product(b, *divmod(m + 2, NHC))
                    pe.wait_ge(s_coef, START + 2 * b)
                    pe.wait_ge(s_ahead, START + TPI * (b + 1))
                    for h in range(2):
                        for j in range(TPI):
                            mm = pe.matmul(core.bank[h][:, :], ones[:, :], precedes[:, j, h * HALF:(h + 1) * HALF], start=(j == 0), stop=(j == TPI - 1))
                        mm.then_inc(s_rank, 1)

                ahead(pe, IMG, lambda b: None, lambda b: norm.tensor(pe, b, x_halves(core, b)), lambda b: None)
                pe.wait_ge(norm.s_out, START + norm.ready(IMG - 1, 1))
                with pe.Fori(0, IMG) as b:
                    weights(b)
                    outputs_and_ranks(b)

            @block.scalar
            def _(act):
                act.wait_ge(s_par, START + 16 * NPAR)

                act.preload_act_table_set(LOG_EXP)
                with act.Fori(0, IMG) as b:
                    norm.scalar(act, b, 1e-5)
                act.preload_act_table(ACT.Gelu_apprx_tanh)
                with act.Fori(0, IMG) as b:
                    act.wait_ge(s_coef, START + 2 * b)
                    for h in range(2):
                        act.wait_ge(s_wmm, START + 2 * b + h + 1)
                        act.activation(weight[:, h * HALF:(h + 1) * HALF], core.bank[2 + h][:, :], ACT.Identity, bias=br[:, 0:1]).then_inc(s_weight, 1)
                    for m in range(NH1):
                        act.wait_ge(s_h1, START + NH1 * b + m + 1)
                        act.wait_ge(s_y, START + NH1 * b + max(0, m - 1))
                        act.activation(hid[m % 2][:, :], core.bank[6 + m % 2][:, :], ACT.Gelu_apprx_tanh, bias=b1[:, m % NHC:m % NHC + 1]).then_inc(s_hid, 1)

            @block.vector
            def _(dve):
                dve.wait_ge(s_par, START + 16 * NPAR)
                dve.tensor_copy(wr_wide[:, :], wr[:, 0:1].broadcast_to([C, C])).then_inc(s_wide, 1)
                dve.wait_ge(s_const, START + 3)
                ahead(dve, IMG, lambda b: norm.finish(dve, b, [image(half(b, h)) for h in range(2)]), lambda b: norm.centre(dve, b, x_halves(core, b)), lambda b: None)
                dve.wait_ge(norm.s_out, START + norm.ready(IMG - 1, 1))
                with dve.Fori(0, IMG) as b:
                    dve.wait_ge(s_weight, START + 2 * b + 2)
                    dve.wait_ge(s_rank, START + 2 * b)
                    for j in range(TPI):
                        own = weight[:, j * TILE:(j + 1) * TILE]
                        me = wcol[:, j:j + 1]
                        if j:
                            dve.wait_ge(s_diag, START + TPI * b + j)
                        dve.scalar_tensor_tensor(out=diag[:, :], in0=own, scalar=1.0, in1=core.ident[:, :], op0=ALU.mult, op1=ALU.mult, accum_out=me).then_inc(s_diag, 1)
                        dve.wait_ge(s_diag, START + TPI * b + j + 1)
                        if j:
                            dve.tensor_scalar(precedes[:, j, 0:j * TILE], weight[:, 0:j * TILE], me, None, ALU.is_lt)
                        if j + 1 < TPI:
                            dve.tensor_scalar(precedes[:, j, (j + 1) * TILE:PIX], weight[:, (j + 1) * TILE:PIX], me, None, ALU.is_le)
                        dve.scalar_tensor_tensor(out=equal[:, :], in0=own, scalar=me, in1=before[:, :], op0=ALU.is_equal, op1=ALU.mult).then_inc(s_tie, 1)
                        dve.wait_ge(s_tie, START + TPI * b + j + 1)
                        dve.scalar_tensor_tensor(out=precedes[:, j, j * TILE:(j + 1) * TILE], in0=own, scalar=me, in1=equal[:, :], op0=ALU.is_lt, op1=ALU.add).then_inc(s_ahead, 1)
                    for h in range(2):
                        dve.wait_ge(s_rank, START + 2 * b + h + 1)
                        dve.scalar_tensor_tensor(out=coef[:, h * HALF:(h + 1) * HALF], in0=core.bank[h][:, :], scalar=float(CHOSEN), in1=weight[:, h * HALF:(h + 1) * HALF],
                                                 op0=ALU.is_lt, op1=ALU.mult).then_inc(s_coef, 1)
                    for h in range(2):
                        xs = X[:, bass.ds(b * PIX + h * HALF, HALF)]
                        dve.wait_ge(s_y, START + NH1 * b + NHC * (h + 1))
                        dve.wait_ge(s_coef, START + 2 * b + h + 1)
                        dve.scalar_tensor_tensor(out=y[h][:, :], in0=core.bank[4 + h][:, :], scalar=b2[:, 0:1], in1=coef[:, h * HALF:(h + 1) * HALF],
                                                 op0=ALU.add, op1=ALU.mult).then_inc(s_ysum, 1)
                        dve.tensor_tensor(xs, xs, half(b, h), ALU.add).then_inc(s_end, 1)
                        dve.wait_ge(s_ysum, START + 2 * b + h + 1)
                        dve.wait_ge(s_end, START + 2 * b + h + 1)
                        dve.tensor_tensor(xs, xs, y[h][:, :], ALU.add)
        norm.done()


def scan_mixer(core, args):
    nc, norm, X = core.nc, core.norm, core.x
    GROUPS = 8
    GC = COLS // GROUPS
    RL, IL = ROWS + 1, IMG + 1
    PC = ROWS * GC
    FEED = HALF // PC
    D = IMG // FEED
    assert D == 2
    NW = 5
    LAM, OUT = 1, 3
    with ExitStack() as mem:
        v = core.sb(mem, "ss_v", [C, TOK])
        vg = v[:, :].rearrange("c (i r w) -> c i r w", r=ROWS, w=COLS)
        w_all = core.sb(mem, "ss_w_all", [C, 3 * C])
        wide = core.sb(mem, "ss_w_wide", [C, NW, C])
        bias = core.sb(mem, "ss_bias", [C, NW])
        out_w = core.sb(mem, "ss_out_w", [C, C])
        vecs = core.sb(mem, "ss_vecs", [C, 3])
        by_rows = lambda name: core.sb(mem, name, [C, IMG, GC, RL])
        by_images = lambda name: core.sb(mem, name, [C, ROWS, GC, IL])
        inp = [by_rows(f"ss_inp{k}") for k in range(2)]
        lam = [[by_rows(f"ss_lam{k}{d}") for d in range(D)] for k in range(2)]
        og = [[by_rows(f"ss_out_gate{k}{d}") for d in range(D)] for k in range(2)]
        feed, fwd, rev = by_rows("ss_feed"), by_rows("ss_fwd"), by_rows("ss_rev")
        lam_i, feed_i, fwd_i, rev_i = (by_images(f"ss_{n}_i") for n in ("lam", "feed", "fwd", "rev"))
        sig = core.sb(mem, "ss_sigmoid", [C, HALF])
        y = core.sb(mem, "ss_y", [C, PIX])
        y3 = y[:, :].rearrange("c (r w) -> c r w", w=COLS)
        flat = lambda t: t[:, :, :, :].rearrange("c a b l -> c (a b l)")
        back = lambda t: flat(t)[:, ::-1]
        (s_par, s_zero, s_wide, s_mm, s_act, s_inp, s_feed, s_feed_i, s_lam_i, s_rows, s_rows_sum, s_images, s_images_sum,
         s_sum, s_prod, s_group, s_affine, s_omm, s_end) = (core.sem(f"ss_{n}") for n in (
            "params", "zero", "wide", "products", "gates", "inp", "feed", "feed_by_images", "lam_by_images", "row_scans", "row_sums",
            "image_scans", "image_sums", "state", "gated", "group", "affine", "out_product", "end"))
        NPAR = 6 + 8
        cleared = (*inp, *lam[0], *lam[1], *og[0], *og[1], feed, fwd, rev, lam_i, feed_i, fwd_i, rev_i)

        def order(eng, gates, scans, group):
            for p in range(D):
                gates(0, 0, p)

            def whole(q, k):
                for d in range(D):
                    scans(q, k, d)
                    gates(q + 1, 1 - k, d)
                group(q, k)

            with eng.Fori(0, GROUPS // 2 - 1) as g:
                for k in range(2):
                    whole(2 * g + k, k)
            whole(GROUPS - 2, 0)
            for d in range(D):
                scans(GROUPS - 1, 1, d)
            group(GROUPS - 1, 1)

        core.start_counts()
        with nc.Block() as block:
            @block.sync
            def _(sp):
                sp.dma_start(w_all[:, :], args["L2_conv_in_w"]).then_inc(s_par, 16)
                sp.dma_start(out_w[:, :], args["L2_conv_out_w"]).then_inc(s_par, 16)
                for n, name in enumerate(("gamma", "beta", "out_b")):
                    sp.dma_start(vecs[:, n:n + 1], column(args[f"L2_conv_{name}"])).then_inc(s_par, 16)
                in_b = args["L2_conv_in_b"]
                sp.dma_start(bias[:, 0:1], column(in_b[0:C])).then_inc(s_par, 16)
                for d in range(2):
                    for e in range(2):
                        sp.dma_start(bias[e:C:2, OUT + d:OUT + d + 1], column(in_b[C + d:2 * C:2]), allow_slow_non_contiguous=True).then_inc(s_par, 16)
                        sp.dma_start(bias[e:C:2, LAM + d:LAM + d + 1], column(in_b[2 * C + d:3 * C:2]), allow_slow_non_contiguous=True).then_inc(s_par, 16)

            @block.gpsimd
            def _(pool):
                for t in cleared:
                    pool.memset(flat(t), 0.0).then_inc(s_zero, 1)
                for q in range(GROUPS):
                    for d in range(2):
                        n = 2 * q + d
                        pool.wait_ge(s_images, START + n)
                        pool.wait_ge(s_act, START + NW * D * (q + 1))
                        pool.tensor_copy(lam_i[:, :, :, 0:IMG], lam[q % 2][d][:, :, :, 0:ROWS].rearrange("c i w r -> c r w i")).then_inc(s_lam_i, 1)
                        pool.wait_ge(s_rows, START + n + 1)
                        pool.tensor_tensor(flat(fwd), flat(fwd), flat(rev), ALU.add).then_inc(s_rows_sum, 1)

            @block.tensor
            def _(pe):
                with pe.Fori(0, IMG) as b:
                    norm.tensor(pe, b, x_halves(core, b))
                pe.wait_ge(norm.s_out, START + norm.ready(IMG - 1, 1))
                pe.wait_ge(s_wide, START + NW)

                def gates(q, k, p):
                    pe.wait_ge(s_act, START + NW * (D * q + p))
                    pe.wait_ge(s_inp, START + D * q + p)
                    for w in range(NW):
                        for i in range(FEED):
                            mm = pe.matmul(core.bank[w][:, i * PC:(i + 1) * PC].rearrange("c (r w) -> c r w", w=GC), wide[:, w, :],
                                           vg[:, FEED * p + i, :, bass.ds(q * GC, GC)], start=True, stop=True)
                        mm.then_inc(s_mm, 1)

                order(pe, gates, lambda q, k, d: None, lambda q, k: None)
                pe.wait_ge(s_group, START + GROUPS)
                norm.done()

                def outputs(b):
                    pe.wait_ge(s_end, START + 2 * b)
                    for h in range(2):
                        pe.wait_ge(s_affine, START + 2 * b + h + 1)
                        pe.matmul(core.bank[4 + h][:, :], out_w[:, :], y[:, h * HALF:(h + 1) * HALF], start=True, stop=True).then_inc(s_omm, 1)

                ahead(pe, IMG, lambda b: None, lambda b: norm.tensor(pe, b, [v[:, bass.ds(o, HALF)] for o in halves(b)]), outputs)
                norm.base -= 2 * IMG

            @block.scalar
            def _(act):
                act.preload_act_table_set(LOG_EXP)
                with act.Fori(0, IMG) as b:
                    norm.scalar(act, b, 1e-6)
                act.wait_ge(s_zero, START + len(cleared))
                act.wait_ge(s_par, START + 16 * NPAR)
                act.preload_act_table(ACT.Sigmoid)

                def gates(q, k, p):
                    if not isinstance(q, int) or q > 0:
                        act.wait_ge(s_group, START + q - 1)
                    for w in range(NW):
                        act.wait_ge(s_mm, START + NW * (D * q + p) + w + 1)
                        if w == 0:
                            act.wait_ge(s_inp, START + D * q + p)
                            act.activation(sig[:, :], core.bank[0][:, :], ACT.Sigmoid, bias=bias[:, 0:1]).then_inc(s_act, 1)
                            continue
                        dst = (*lam[k], *og[k])[w - 1][:, FEED * p:FEED * (p + 1), :, 0:ROWS]
                        act.activation(dst, core.bank[w][:, :].rearrange("c (i r w) -> c i w r", i=FEED, w=GC), ACT.Sigmoid, bias=bias[:, w:w + 1]).then_inc(s_act, 1)

                def by_image(q, k, d):
                    act.wait_ge(s_images, START + D * q + d)
                    act.wait_ge(s_feed, START + D * q + d + 1)
                    act.activation(feed_i[:, :, :, 0:IMG], feed[:, :, :, 0:ROWS].rearrange("c i w r -> c r w i"), ACT.Copy).then_inc(s_feed_i, 1)

                order(act, gates, by_image, lambda q, k: None)
                norm.done()
                act.preload_act_table_set(LOG_EXP)

                def affine(b):
                    for h in range(2):
                        half = y[:, h * HALF:(h + 1) * HALF]
                        act.wait_ge(norm.s_out, START + norm.ready(b, h))
                        act.activation(half, half, ACT.Identity, bias=vecs[:, 1:2], scale=vecs[:, 0:1]).then_inc(s_affine, 1)

                ahead(act, IMG, affine, lambda b: norm.scalar(act, b, 1e-5), lambda b: None)
                norm.base -= 2 * IMG

            @block.vector
            def _(dve):
                dve.wait_ge(s_par, START + 16 * NPAR)
                dve.tensor_copy(wide[:, 0, :], w_all[:, 0:C]).then_inc(s_wide, 1)
                for d in range(2):
                    for w, at in ((LAM + d, 2 * C + d), (OUT + d, C + d)):
                        src = w_all[:, at:at - d + C:2].rearrange("c (n e) -> c n e", e=1).broadcast_to([C, C // 2, 2])
                        dve.tensor_copy(wide[:, w, :].rearrange("c (n e) -> c n e", e=2), src).then_inc(s_wide, 1)
                ahead(dve, IMG, lambda b: norm.finish(dve, b, [image(v[:, bass.ds(o, HALF)]) for o in halves(b)]),
                      lambda b: norm.centre(dve, b, x_halves(core, b)), lambda b: None)
                dve.wait_ge(s_zero, START + len(cleared))

                def gates(q, k, p):
                    dve.wait_ge(s_act, START + NW * (D * q + p) + 1)
                    for i in range(FEED):
                        at = slice(i * PC, (i + 1) * PC)
                        ins = dve.scalar_tensor_tensor(out=inp[k][:, FEED * p + i, :, 0:ROWS].rearrange("c w r -> c r w"),
                                                       in0=core.bank[0][:, at].rearrange("c (r w) -> c r w", w=GC), scalar=bias[:, 0:1],
                                                       in1=sig[:, at].rearrange("c (r w) -> c r w", w=GC), op0=ALU.add, op1=ALU.mult)
                    ins.then_inc(s_inp, 1)

                def scans(q, k, d):
                    if d == 0:
                        dve.wait_ge(s_inp, START + D * (q + 1))
                        dve.wait_ge(s_act, START + NW * D * (q + 1))
                    n = D * q + d
                    dve.wait_ge(s_feed_i, START + n)
                    dve.scalar_tensor_tensor(out=flat(feed), in0=flat(lam[k][d]), scalar=1.0, in1=flat(inp[k]), op0=ALU.subtract, op1=ALU.mult).then_inc(s_feed, 1)
                    dve.wait_ge(s_feed, START + n + 1)
                    dve.wait_ge(s_prod, START + n)
                    dve.tensor_tensor_scan(flat(fwd), flat(lam[k][d]), flat(feed), 0.0, ALU.mult, ALU.subtract)
                    dve.tensor_tensor_scan(back(rev), back(lam[k][d]), back(feed), 0.0, ALU.mult, ALU.subtract).then_inc(s_rows, 1)
                    dve.wait_ge(s_feed_i, START + n + 1)
                    dve.wait_ge(s_lam_i, START + n + 1)
                    dve.tensor_tensor_scan(flat(fwd_i), flat(lam_i), flat(feed_i), 0.0, ALU.mult, ALU.subtract)
                    dve.tensor_tensor_scan(back(rev_i), back(lam_i), back(feed_i), 0.0, ALU.mult, ALU.subtract).then_inc(s_images, 1)
                    dve.wait_ge(s_images, START + n + 1)
                    dve.tensor_tensor(flat(fwd_i), flat(fwd_i), flat(rev_i), ALU.add).then_inc(s_images_sum, 1)
                    dve.wait_ge(s_rows_sum, START + n + 1)
                    dve.wait_ge(s_images_sum, START + n + 1)
                    state = fwd[:, :, :, 0:ROWS]
                    dve.tensor_tensor(state, state, fwd_i[:, :, :, 0:IMG].rearrange("c r w i -> c i w r"), ALU.add).then_inc(s_sum, 1)
                    dve.wait_ge(s_sum, START + n + 1)
                    dve.tensor_tensor(flat(og[k][d]), flat(og[k][d]), flat(fwd), ALU.mult).then_inc(s_prod, 1)
                def group(q, k):
                    dve.wait_ge(s_prod, START + D * (q + 1))
                    dve.tensor_tensor(vg[:, :, :, bass.ds(q * GC, GC)].rearrange("c i r w -> c i w r"), og[k][0][:, :, :, 0:ROWS], og[k][1][:, :, :, 0:ROWS], ALU.add).then_inc(s_group, 1)

                order(dve, gates, scans, group)
                dve.wait_ge(s_group, START + GROUPS)
                norm.done()

                def normalise(b):
                    dve.wait_ge(s_omm, START + 2 * b)
                    norm.finish(dve, b, [y3[:, 0:HROWS], y3[:, HROWS:ROWS]])

                def add_outputs(b):
                    for h in range(2):
                        xs = X[:, bass.ds(b * PIX + h * HALF, HALF)]
                        dve.wait_ge(s_omm, START + 2 * b + h + 1)
                        dve.scalar_tensor_tensor(out=xs, in0=core.bank[4 + h][:, :], scalar=vecs[:, 2:3], in1=xs, op0=ALU.add, op1=ALU.add).then_inc(s_end, 1)

                ahead(dve, IMG, normalise, lambda b: norm.centre(dve, b, [v[:, bass.ds(o, HALF)] for o in halves(b)]), add_outputs)
                norm.base -= 2 * IMG
        norm.done(2)


class Grouped:

    PAIR = 2
    GROUP = 4

    def __init__(self, core, mem, name, gate_w, gate_b, hid, out=None):
        nc, self.core = core.nc, core
        self.E = E = gate_w.shape[1]
        self.gate_w, self.gate_b = gate_w, gate_b
        self.TILES = T = TOK // TILE
        self.BLOCKS = self.PAIR * T + 2 * E
        self.GROUPS = self.BLOCKS // self.GROUP
        self.MID = self.GROUPS // 2
        assert self.BLOCKS % (4 * self.GROUP) == 0 and T * E % HALF == 0
        rows = (self.BLOCKS * TILE, C)
        self.xs = nc.dram_tensor(f"{name}_slot_inputs", rows, F32).ap()
        self.ys = [nc.dram_tensor(f"{name}_slot_outputs{z}", (self.BLOCKS // 2 * TILE, C), F32).ap() for z in range(2)]
        sb = lambda n, shape, dtype=F32: core.sb(mem, f"{name}_{n}", shape, dtype)
        self.w = sb("gate_w", [C, E])
        self.b = sb("gate_b", [TILE, E])
        self.v = sb("v", [C, PIX])
        self.rows = sb("rows", [TILE, TOK])
        self.p = sb("probs", [TILE, T * E])
        self.q = sb("scratch", [TILE, T * E])
        self.hot = [sb(f"hot{k}", [TILE, T * E]) for k in range(2)]
        self.both = sb("both", [TILE, T * E], BF16)
        self.order = sb("order", [TILE, E])
        self.top = sb("top", [TILE, T])
        self.share = sb("share", [TILE, T, self.PAIR])
        self.slot = sb("slot", [TILE, T, self.PAIR])
        self.index = sb("index", [TILE, T, self.PAIR], I32)
        self.index_y = sb("index_y", [TILE, T, self.PAIR], I32)
        self.limit_i = sb("limits_int", [TILE, self.BLOCKS], I32)
        self.limit = sb("limits", [TILE, self.BLOCKS])
        self.past = sb("past", [1, self.BLOCKS * E])
        self.expert = sb("expert", [1, self.BLOCKS])
        self.small = sb("small", [TILE, 4, 2 * E])
        self.ids = sb("ids", [1, 3, self.BLOCKS], I32)
        self.tri = sb("before", [TILE, TILE])
        self.tri16 = sb("before16", [TILE, TILE], BF16)
        self.ones16 = sb("ones16", [TILE, TILE], BF16)
        self.zero1 = sb("zero", [TILE, 1])
        self.xin = [sb(f"slots_in{k}", [TILE, self.GROUP, C]) for k in range(2)]
        self.yout = [sb(f"slots_out{k}", [TILE, self.GROUP, C]) for k in range(2)]
        self.own = [sb(f"own_index{k}", [TILE, self.GROUP * self.PAIR], I32) for k in range(2)]
        self.gathered = [sb(f"gathered{k}", [TILE, self.GROUP * self.PAIR * C]) for k in range(2)]
        self.xt = [sb(f"slots_t{k}", [C, TILE]) for k in range(2)]
        self.w1 = [sb(f"w1_of_block{k}", [C, hid]) for k in range(2)]
        (self.s_par, self.s_const, self.s_logit, self.s_logits, self.s_turn, self.s_rows, self.s_step, self.s_exp, self.s_both, self.s_count,
         self.s_index, self.s_ids, self.s_fill, self.s_stage, self.s_begun, self.s_own, self.s_t, self.s_xt, self.s_w1, self.s_h, self.s_act,
         self.s_hid, self.s_o, self.s_y) = (
            core.sem(f"{name}_{n}") for n in ("params", "const", "logit_products", "logits", "rows_turned", "rows_ready", "steps", "exp", "both",
                                              "counted", "index", "ids", "filled", "staged", "begun", "own_index", "slots_turned", "slots_t", "block_w1",
                                              "products", "activated", "hidden", "outputs", "outputs_out"))
        self.s_weighted, self.s_sum, self.s_end = ([[core.sem(f"{name}_{n}{z}{k}") for k in range(2)] for z in range(2)] for n in ("weighted", "summed", "end"))
        self.out = None if out is None else Output(core, mem, out)
        self.s_in = [core.sem(f"{name}_slots_in{k}") for k in range(2)]
        self.s_stored = [core.sem(f"{name}_stored{k}") for k in range(2)]
        self.s_scatter = [core.indirect_sem() for k in range(2)]
        self.s_scatter_second = core.indirect_sem()
        self.s_got = [core.indirect_sem() for k in range(2)]
        self.s_got_first = [core.indirect_sem() for i in range(IMG)]

    NCONST = 6
    NIDS = 5

    def group_rows(self, dram, g):
        view = dram.rearrange("(g j p) c -> g p j c", j=self.GROUP, p=TILE)
        return view[g] if isinstance(g, int) else view[bass.ds(g, 1)].rearrange("o p j c -> p (o j) c")


    def load(self, sp):
        sp.dma_start(self.w[:, :], self.gate_w).then_inc(self.s_par, 16)
        sp.dma_start(self.b[:, :], self.gate_b.rearrange("(o e) -> o e", o=1).broadcast_to([TILE, self.E])).then_inc(self.s_par, 16)
        sp.wait_ge(self.s_const, START + self.NCONST)
        with sp.Fori(0, self.GROUPS) as g:
            sp.dma_start(self.group_rows(self.xs, g), self.xin[0][:, :, :]).then_inc(self.s_fill, 16)

    def constants(self, pool):
        pool.memset(self.xin[0][:, :, :], 0.0).then_inc(self.s_const, 1)
        pool.memset(self.ones16[:, :], 1.0).then_inc(self.s_const, 1)
        pool.memset(self.zero1[:, :], 0.0).then_inc(self.s_const, 1)
        pool.memset(self.tri[:, :], 1.0).then_inc(self.s_const, 1)
        pool.iota(self.limit_i[:, :], pattern=[[TILE, self.BLOCKS]], base=0, channel_multiplier=0).then_inc(self.s_const, 1)
        pool.wait_ge(self.s_const, START + 5)
        pool.affine_select(out=self.tri[:, :], in_=self.tri[:, :], compare_op=ALU.is_gt, fill=0.0,
                           base=0, pattern=[[1, TILE]], channel_multiplier=-1).then_inc(self.s_const, 1)
        for e in range(self.E):
            pool.memset(self.order[:, e:e + 1], float(self.E - e)).then_inc(self.s_const, 1)

    def route_tensor(self, pe, b, v):
        pe.wait_ge(self.s_logits, START + b)
        for j in range(TPI):
            mm = pe.matmul(self.core.bank[4][:, j * self.E:(j + 1) * self.E], v[:, j * TILE:(j + 1) * TILE], self.w[:, :], start=True, stop=True)
        mm.then_inc(self.s_logit, 1)

    def route_vector(self, dve, b):
        E = self.E
        dve.wait_ge(self.s_logit, START + b + 1)
        dve.tensor_tensor(self.p[:, bass.ds(b * (TPI * E), TPI * E)].rearrange("p (t e) -> p t e", e=E),
                          self.core.bank[4][:, 0:TPI * E].rearrange("p (t e) -> p t e", e=E),
                          self.b[:, :].rearrange("p (t e) -> p t e", t=1).broadcast_to([TILE, TPI, E]), ALU.add).then_inc(self.s_logits, 1)

    def rows_tensor(self, pe, b, src):
        for h in range(2):
            pe.wait_ge(self.s_rows, START + 2 * b)
            for j in range(4):
                mm = pe.transpose(self.core.bank[6 + h][:, j * TILE:(j + 1) * TILE], src[:, h * HALF + j * TILE:h * HALF + (j + 1) * TILE], self.core.ident[:, :])
            mm.then_inc(self.s_turn, 1)

    def rows_scalar(self, act, b):
        for h in range(2):
            act.wait_ge(self.s_turn, START + 2 * b + h + 1)
            act.activation(self.rows[:, bass.ds((2 * b + h) * HALF, HALF)], self.core.bank[6 + h][:, :], ACT.Copy).then_inc(self.s_rows, 1)


    def choose_scalar(self, act):
        act.wait_ge(self.s_step, START + 2)
        act.activation(self.p[:, :], self.p[:, :], ACT.Exp).then_inc(self.s_exp, 1)

    def choose_tensor(self, pe):
        pe.wait_ge(self.s_const, START + self.NCONST + self.E + 2)
        pe.wait_ge(self.s_rows, START + 2 * IMG)
        pe.wait_ge(self.s_both, START + 1)
        N = self.TILES * self.E // HALF
        for n in range(N):
            pe.matmul(self.core.bank[4 + n][:, :], self.tri16[:, :], self.both[:, n * HALF:(n + 1) * HALF], start=True, stop=True).then_inc(self.s_count, 1)
            pe.matmul(self.core.bank[6 + n][:, :], self.ones16[:, :], self.both[:, n * HALF:(n + 1) * HALF], start=True, stop=True).then_inc(self.s_count, 1)

    def choose_vector(self, dve):
        E, T, B, s = self.E, self.TILES, self.BLOCKS, self.s_step
        n = count(1)
        by = lambda t: t[:, :].rearrange("p (t e) -> p t e", e=E)
        p, q = by(self.p), by(self.q)
        top = self.top[:, :]
        wide = top.rearrange("p (t e) -> p t e", e=1).broadcast_to([TILE, T, E])
        order = self.order[:, :].rearrange("p (t e) -> p t e", t=1).broadcast_to([TILE, T, E])
        dve.wait_ge(self.s_const, START + self.NCONST + E)
        dve.tensor_copy(self.tri16[:, :], self.tri[:, :]).then_inc(self.s_const, 1)
        dve.tensor_copy(self.limit[:, :], self.limit_i[:, :]).then_inc(self.s_const, 1)
        dve.wait_ge(self.s_logits, START + IMG)
        dve.tensor_reduce(top, p, AX.X, ALU.max).then_inc(s, 1)
        dve.wait_ge(s, START + next(n))
        dve.tensor_tensor(p, p, wide, ALU.subtract).then_inc(s, 1)
        next(n)
        dve.wait_ge(self.s_exp, START + 1)
        dve.tensor_reduce(top, p, AX.X, ALU.add).then_inc(s, 1)
        dve.wait_ge(s, START + next(n))
        dve.reciprocal(top, top).then_inc(s, 1)
        dve.wait_ge(s, START + next(n))
        dve.tensor_tensor(p, p, wide, ALU.mult).then_inc(s, 1)
        dve.wait_ge(s, START + next(n))
        for k, src in enumerate((p, q)):
            hot = by(self.hot[k])
            dve.tensor_reduce(top, src, AX.X, ALU.max).then_inc(s, 1)
            dve.wait_ge(s, START + next(n))
            dve.tensor_copy(self.share[:, :, k], top).then_inc(s, 1)
            dve.tensor_tensor(hot, src, wide, ALU.is_equal).then_inc(s, 1)
            next(n)
            dve.wait_ge(s, START + next(n))
            dve.tensor_tensor(hot, hot, order, ALU.mult).then_inc(s, 1)
            dve.wait_ge(s, START + next(n))
            dve.tensor_reduce(top, hot, AX.X, ALU.max).then_inc(s, 1)
            dve.wait_ge(s, START + next(n))
            dve.tensor_tensor(hot, hot, wide, ALU.is_equal).then_inc(s, 1)
            dve.wait_ge(s, START + next(n))
            if k == 0:
                dve.scalar_tensor_tensor(out=q, in0=hot, scalar=-2.0, in1=p, op0=ALU.mult, op1=ALU.add).then_inc(s, 1)
                dve.wait_ge(s, START + next(n))
        dve.tensor_tensor(self.both[:, :], self.hot[0][:, :], self.hot[1][:, :], ALU.add).then_inc(self.s_both, 1)
        dve.tensor_tensor(top, self.share[:, :, 0], self.share[:, :, 1], ALU.add).then_inc(s, 1)
        dve.wait_ge(s, START + next(n))
        dve.reciprocal(top, top).then_inc(s, 1)
        dve.wait_ge(s, START + next(n))
        dve.tensor_tensor(self.share[:, :, :], self.share[:, :, :],
                          top.rearrange("p (t k) -> p t k", k=1).broadcast_to([TILE, T, self.PAIR]), ALU.mult).then_inc(s, 1)
        next(n)
        TH = T // 2
        by_expert = lambda t: t.rearrange("p (e t) -> p e t", t=TH)
        of_experts = lambda t: t.rearrange("p (e t) -> p e t", t=1).broadcast_to([TILE, 2 * E, TH])
        zeros = lambda width: self.zero1[:, 0:1].broadcast_to([TILE, width])
        part = [slice(z * TH * E, (z + 1) * TH * E) for z in range(2)]

        def counted(bank, z):
            n, at = divmod(z * TH * E, HALF)
            return self.core.bank[bank + n][:, at:at + TH * E]

        tokens, upto, begun = self.q[:, :], self.p[:, :], self.gathered[0][:, 0:T * E]
        number, blocks, ends, shift = (self.small[:, r, :] for r in range(4))
        dve.wait_ge(self.s_count, START + 2 * (T * E // HALF))
        for z in range(2):
            dve.tensor_copy(by_expert(tokens[:, part[z]]), counted(6, z).rearrange("p (t e) -> p e t", e=E)).then_inc(s, 1)
            dve.wait_ge(s, START + next(n))
        dve.tensor_tensor_scan(upto, tokens, zeros(T * E), 0.0, ALU.add, ALU.add).then_inc(s, 1)
        dve.tensor_reduce(number, by_expert(tokens), AX.X, ALU.add).then_inc(s, 1)
        next(n)
        dve.wait_ge(s, START + next(n))
        dve.tensor_tensor(by_expert(begun), of_experts(number), self.limit[:, 0:TH].rearrange("p (e t) -> p e t", e=1).broadcast_to([TILE, 2 * E, TH]), ALU.is_gt).then_inc(s, 1)
        dve.tensor_tensor(tokens, upto, tokens, ALU.subtract).then_inc(s, 1)
        next(n)
        dve.wait_ge(s, START + next(n))
        dve.tensor_reduce(blocks, by_expert(begun), AX.X, ALU.add).then_inc(s, 1)
        dve.wait_ge(s, START + next(n))
        dve.tensor_scalar(blocks, blocks, float(TILE), None, ALU.mult).then_inc(s, 1)
        dve.wait_ge(s, START + next(n))
        for z in range(2):
            own = slice(z * E, (z + 1) * E)
            dve.tensor_tensor_scan(ends[:, own], blocks[:, own], zeros(E), float(z * (B // 2) * TILE), ALU.add, ALU.add).then_inc(s, 1)
            dve.wait_ge(s, START + next(n))
        dve.tensor_tensor(shift, ends, blocks, ALU.subtract).then_inc(s, 1)
        dve.tensor_tensor(number, by_expert(upto)[:, :, TH - 1], number, ALU.subtract).then_inc(s, 1)
        next(n)
        dve.wait_ge(s, START + next(n))
        dve.tensor_tensor(shift, shift, number, ALU.subtract).then_inc(s, 1)
        dve.wait_ge(s, START + next(n))
        dve.tensor_tensor(by_expert(tokens), by_expert(tokens), of_experts(shift), ALU.add).then_inc(s, 1)
        dve.wait_ge(s, START + next(n))
        for z in range(2):
            dve.tensor_tensor(self.p[:, part[z]].rearrange("p (t e) -> p t e", e=E), counted(4, z).rearrange("p (t e) -> p t e", e=E),
                              tokens[:, part[z]].rearrange("p (e t) -> p t e", t=TH), ALU.add).then_inc(s, 1)
            dve.wait_ge(s, START + next(n))
        for k in range(self.PAIR):
            dve.tensor_tensor(self.hot[k][:, :], self.hot[k][:, :], self.p[:, :], ALU.mult).then_inc(s, 1)
            dve.wait_ge(s, START + next(n))
            dve.tensor_reduce(self.slot[:, :, k], by(self.hot[k]), AX.X, ALU.add).then_inc(s, 1)
            dve.wait_ge(s, START + next(n))
        dve.tensor_copy(self.index[:, :, :], self.slot[:, :, :]).then_inc(self.s_index, 1)
        dve.wait_ge(self.s_index, START + 1)
        dve.tensor_scalar(self.slot[:, TH:T, :], self.slot[:, TH:T, :], float(B // 2 * TILE), None, ALU.subtract).then_inc(s, 1)
        dve.wait_ge(s, START + next(n))
        dve.tensor_copy(self.index_y[:, :, :], self.slot[:, :, :]).then_inc(self.s_index, 1)
        past = self.past[:, :].rearrange("p (s e) -> p s e", e=E)
        for z in range(2):
            own = slice(z * (B // 2), (z + 1) * (B // 2))
            dve.tensor_tensor(past[:, own, :], ends[0:1, z * E:(z + 1) * E].rearrange("p (s e) -> p s e", s=1).broadcast_to([1, B // 2, E]),
                              self.limit[0:1, own].rearrange("p (s e) -> p s e", e=1).broadcast_to([1, B // 2, E]), ALU.is_le).then_inc(s, 1)
        next(n)
        dve.wait_ge(s, START + next(n))
        dve.tensor_reduce(self.expert[:, :], past, AX.X, ALU.add).then_inc(s, 1)
        dve.wait_ge(s, START + next(n))
        dve.tensor_scalar(self.expert[:, :], self.expert[:, :], float(E - 1), None, ALU.min).then_inc(s, 1)
        dve.wait_ge(s, START + next(n))
        dve.tensor_copy(self.ids[:, 0, 1:B], self.expert[:, 0:B - 1]).then_inc(self.s_ids, 1)
        dve.tensor_copy(self.ids[:, 0, 0:1], self.expert[:, 0:1]).then_inc(self.s_ids, 1)
        dve.tensor_copy(self.ids[:, 1, :], self.expert[:, :]).then_inc(self.s_ids, 1)
        dve.tensor_copy(self.ids[:, 2, 0:B - 1], self.expert[:, 1:B]).then_inc(self.s_ids, 1)
        dve.tensor_copy(self.ids[:, 2, B - 1:B], self.expert[:, B - 1:B]).then_inc(self.s_ids, 1)


    def staged(self, k):
        return self.gathered[k][:, 0:self.GROUP * C].rearrange("p (j c) -> p j c", c=C)

    def scatter_scalar(self, act):
        def stage(p, k):
            act.activation(self.staged(k), self.rows[:, bass.ds((2 * p + k) * HALF, HALF)].rearrange("p (j c) -> p j c", c=C), ACT.Copy).then_inc(self.s_stage, 1)

        act.wait_ge(self.s_rows, START + 2 * IMG)
        act.wait_ge(self.s_index, START + 1)
        stage(0, 0)
        stage(0, 1)
        with act.Fori(1, IMG // 2) as p:
            for k in range(2):
                act.wait_ge(self.s_scatter[k], 16 * self.GROUP * self.PAIR * p)
                stage(p, k)

    def scatter_gpsimd(self, pool):
        N = self.GROUP * self.PAIR
        pool.wait_ge(self.s_fill, START + 16 * self.GROUPS)
        pool.wait_ge(self.s_index, START + 1)
        with pool.Fori(0, IMG // 2) as p:
            for k in range(2):
                pool.wait_ge(self.s_stage, START + 2 * p + k + 1)
                pool.sem_inc(self.s_begun, 1)
                pool.tensor_copy(self.own[k][:, :], self.indices(self.index, 2 * p + k)).then_inc(self.s_own, 1)
                pool.wait_ge(self.s_own, START + 2 * p + k + 1)
                pool.sem_inc(self.s_begun, 1)
                for m in range(N):
                    pool.indirect_dma_start(self.xs[:, :], bass.IndirectOffsetOnAxis(ap=self.own[k][:, m:m + 1], axis=0),
                                            self.staged(k)[:, m // self.PAIR, :], None).then_inc(self.s_scatter[k], 16)
        for t in range(self.TILES // 2, self.TILES):
            for m in range(self.PAIR):
                pool.indirect_dma_start(self.xs[:, :], bass.IndirectOffsetOnAxis(ap=self.index[:, t, m:m + 1], axis=0),
                                        self.rows[:, t * C:(t + 1) * C], None).then_inc(self.s_scatter_second, 16)

    def indices(self, index, half):
        N = self.GROUP * self.PAIR
        return index[:, :, :].rearrange("p t k -> p (t k)")[:, bass.ds(half * N, N)]


    def groups(self, group):
        pairs = self.MID // 2 - 1

        def run(eng):
            group(0, 0, 0, 0)
            with eng.Fori(0, pairs) as p:
                group(2 * p + 1, 1, p + 1, 0)
                group(2 * p + 2, 0, p + 1, 0)
            for g in (self.MID - 1, self.MID):
                group(g, g % 2, (g + 1) // 2, 0)
            with eng.Fori(pairs + 1, 2 * pairs + 1) as p:
                group(2 * p + 1, 1, p + 1, 1)
                group(2 * p + 2, 0, p + 1, 1)
            group(self.GROUPS - 1, 1, self.GROUPS // 2, 1)
        return run

    def experts_of(self, engine, row, g):
        _, ids = self.core.nc.values_load_multi_w_load_instructions(
            self.ids[0:1, row, bass.ds(g * self.GROUP, self.GROUP)], [engine], min_val=0, max_val=self.E - 1,
            skip_runtime_bounds_check_because="the ids are counts of experts, and their minimum with the last expert was taken")
        return ids

    def blocks_sync(self, sp):
        def load(g, k):
            sp.dma_start(self.xin[k][:, :, :], self.group_rows(self.xs, g)).then_inc(self.s_in[k], 16)

        def store(g, k, z):
            sp.wait_ge(self.s_y, START + self.GROUP * (g + 1))
            sp.dma_start(self.group_rows(self.ys[z], g - z * self.MID), self.yout[k][:, :, :]).then_inc(self.s_stored[k], 16)

        for k in range(2):
            sp.wait_ge(self.s_scatter[k], 16 * self.GROUP * self.PAIR * (IMG // 2))
        load(0, 0)

        def group(g, k, half, z):
            if not is_last(g, self.GROUPS):
                sp.wait_ge(self.s_t, START + self.GROUP * g)
                if isinstance(g, int) and g == self.MID - 1:
                    sp.wait_ge(self.s_scatter_second, 16 * self.PAIR * (self.TILES // 2))
                load(g + 1, 1 - k)
            if not is_first(g):
                store(g - 1, 1 - k, z)

        self.groups(group)(sp)
        store(self.GROUPS - 1, 1, 1)
        for k in range(2):
            sp.wait_ge(self.s_stored[k], START + 16 * self.MID)

    def blocks_tensor(self, pe, first, second):
        G, BLOCKS, PE = self.GROUP, self.BLOCKS, mybir.EngineType.PE
        pe.wait_ge(self.s_ids, START + self.NIDS)

        def turn(n, j, k):
            pe.wait_ge(self.s_xt, START + lag(n))
            pe.transpose(self.core.bank[j % 2][:, 0:TILE], self.xin[k][:, j, :], self.core.ident[:, :]).then_inc(self.s_t, 1)

        def out(n, r, expert):
            pe.wait_ge(self.s_hid, START + n + 1)
            pe.wait_ge(self.s_y, START + lag(n))
            second(r, expert).then_inc(self.s_o, 1)

        pe.wait_ge(self.s_in[0], START + 16)
        turn(0, 0, 0)

        def group(g, k, half, z):
            before = self.experts_of(PE, 0, g)
            for j in range(G):
                n = G * g + j
                if not is_last(n, BLOCKS):
                    if j + 1 < G:
                        turn(n + 1, j + 1, k)
                    else:
                        pe.wait_ge(self.s_in[1 - k], START + 16 * (half + 1))
                        turn(n + 1, 0, 1 - k)
                pe.wait_ge(self.s_xt, START + n + 1)
                pe.wait_ge(self.s_w1, START + n + 1)
                pe.wait_ge(self.s_hid, START + lag(n))
                first(j % 2).then_inc(self.s_h, 1)
                if not is_first(n):
                    out(n - 1, (j - 1) % 2, before[j])

        self.groups(group)(pe)
        out(BLOCKS - 1, (BLOCKS - 1) % 2, self.experts_of(PE, 1, self.GROUPS - 1)[G - 1])

    def blocks_scalar(self, act, turned, activated, by_expert=False):
        def experts(row, g):
            return self.experts_of(mybir.EngineType.Activation, row, g) if by_expert else [None] * self.GROUP

        if by_expert:
            act.wait_ge(self.s_ids, START + self.NIDS)

        def turn(n, r, expert):
            act.wait_ge(self.s_t, START + n + 1)
            act.wait_ge(self.s_h, START + lag(n))
            turned(r, expert).then_inc(self.s_xt, 1)

        turn(0, 0, experts(1, 0)[0])

        def group(g, k, half, z):
            after, own = experts(2, g), experts(1, g)
            for j in range(self.GROUP):
                n = self.GROUP * g + j
                if not is_last(n, self.BLOCKS):
                    turn(n + 1, (j + 1) % 2, after[j])
                act.wait_ge(self.s_h, START + n + 1)
                activated(n, j % 2, own[j])

        self.groups(group)(act)

    def blocks_vector(self, dve, copy_w1, gated, out, by_expert=False):
        G, DVE = self.GROUP, mybir.EngineType.DVE
        dve.wait_ge(self.s_ids, START + self.NIDS)

        def weights(n, r, expert):
            dve.wait_ge(self.s_h, START + lag(n))
            copy_w1(r, expert).then_inc(self.s_w1, 1)

        def leave(n, j, k, expert):
            dve.wait_ge(self.s_o, START + n + 1)
            out(j % 2, self.yout[k][:, j, :], expert).then_inc(self.s_y, 1)

        weights(0, 0, self.experts_of(DVE, 1, 0)[0])

        def group(g, k, half, z):
            after = self.experts_of(DVE, 2, g)
            before = self.experts_of(DVE, 0, g) if by_expert else [None] * G
            for j in range(G):
                n = G * g + j
                if not is_last(n, self.BLOCKS):
                    weights(n + 1, (j + 1) % 2, after[j])
                gated(n, j % 2)
                if j == 1:
                    dve.wait_ge(self.s_stored[k], START + 16 * (half - k))
                if j:
                    leave(n - 1, j - 1, k, before[j])
                elif not is_first(n):
                    leave(n - 1, G - 1, 1 - k, before[j])

        self.groups(group)(dve)
        expert = self.experts_of(DVE, 1, self.GROUPS - 1)[G - 1] if by_expert else None
        leave(self.BLOCKS - 1, G - 1, (self.GROUPS - 1) % 2, expert)


    def first_outputs(self, i):
        N = self.GROUP * self.PAIR * C
        return self.rows[:, i * N:(i + 1) * N]

    def combine_gpsimd(self, pool):
        N = self.GROUP * self.PAIR
        pool.wait_ge(self.s_index, START + 2)
        pool.wait_ge(self.s_scatter_second, 16 * self.PAIR * (self.TILES // 2))
        for k in range(2):
            pool.wait_ge(self.s_stored[k], START + 16 * (self.MID // 2))
        for i in range(IMG):
            for m in range(N):
                t, choice = self.GROUP * i + m // self.PAIR, m % self.PAIR
                pool.indirect_dma_start(self.first_outputs(i)[:, m * C:(m + 1) * C], None, self.ys[0][:, :],
                                        bass.IndirectOffsetOnAxis(ap=self.index_y[:, t, choice:choice + 1], axis=0)).then_inc(self.s_got_first[i], 16)
        for k in range(2):
            pool.wait_ge(self.s_stored[k], START + 16 * self.MID)
        with pool.Fori(0, IMG // 2) as p:
            for k in range(2):
                pool.wait_ge(self.s_sum[1][k], START + p)
                pool.sem_inc(self.s_begun, 1)
                pool.tensor_copy(self.own[k][:, :], self.indices(self.index_y, IMG + 2 * p + k)).then_inc(self.s_own, 1)
                pool.wait_ge(self.s_own, START + IMG + 2 * p + k + 1)
                pool.sem_inc(self.s_begun, 1)
                for m in range(N):
                    pool.indirect_dma_start(self.gathered[k][:, m * C:(m + 1) * C], None, self.ys[1][:, :],
                                            bass.IndirectOffsetOnAxis(ap=self.own[k][:, m:m + 1], axis=0)).then_inc(self.s_got[k], 16)

    def combine_tensor(self, pe):
        def add(z, p, k, outputs):
            pe.wait_ge(self.s_end[z][k], START + p)
            pe.wait_ge(self.s_weighted[z][k], START + p + 1)
            for j in range(self.GROUP):
                for m in range(self.PAIR):
                    at = (j * self.PAIR + m) * C
                    mm = pe.matmul(self.core.bank[k][:, j * TILE:(j + 1) * TILE], outputs[:, at:at + C], self.core.ident[:, :],
                                   start=(m == 0), stop=(m == self.PAIR - 1))
            mm.then_inc(self.s_sum[z][k], 1)
            if self.out:
                pe.wait_ge(self.s_end[z][k], START + p + 1)
                self.out.tensor(pe, z * (IMG // 2) + p, k)

        for i in range(IMG):
            add(0, i // 2, i % 2, self.first_outputs(i))
        for k in range(2):
            pe.wait_ge(self.s_end[0][k], START + IMG // 2)
        with pe.Fori(0, IMG // 2) as p:
            for k in range(2):
                add(1, p, k, self.gathered[k])

    def combine_vector(self, dve):
        N = self.GROUP * self.PAIR
        share = self.share[:, :, :].rearrange("p t k -> p (t k)")

        def weigh(z, p, k, outputs):
            g = outputs.rearrange("p (m c) -> p m c", c=C)
            w = share[:, bass.ds((z * IMG + 2 * p + k) * N, N)].rearrange("p (m c) -> p m c", c=1).broadcast_to([TILE, N, C])
            dve.tensor_tensor(g, g, w, ALU.mult).then_inc(self.s_weighted[z][k], 1)

        def add(z, p, k):
            xs = self.core.x[:, bass.ds((z * IMG + 2 * p + k) * HALF, HALF)]
            to = xs
            if self.out:
                to = self.out.sums[k][:, :]
                dve.wait_ge(self.out.s_turn[k], START + z * (IMG // 2) + p)
            dve.wait_ge(self.s_sum[z][k], START + p + 1)
            dve.tensor_tensor(to, xs, self.core.bank[k][:, :], ALU.add).then_inc(self.s_end[z][k], 1)

        for i in range(IMG):
            dve.wait_ge(self.s_got_first[i], 16 * N)
            weigh(0, i // 2, i % 2, self.first_outputs(i))
            if i:
                add(0, (i - 1) // 2, (i - 1) % 2)
        add(0, (IMG - 1) // 2, (IMG - 1) % 2)
        with dve.Fori(0, IMG // 2) as p:
            for k in range(2):
                dve.wait_ge(self.s_got[k], 16 * N * (p + 1))
                weigh(1, p, k, self.gathered[k][:, :])
                add(1, p, k)


def is_first(n):
    return isinstance(n, int) and n == 0


def is_last(n, count):
    return isinstance(n, int) and n == count - 1


def lag(n):
    return max(n - 1, 0) if isinstance(n, int) else n - 1


def experts_ffn(core, args):
    nc, norm, X = core.nc, core.norm, core.x
    E, _, HID = args["L2_ffn_w1"].shape
    K = HID // C
    W = HID * 2
    with ExitStack() as mem:
        ex = Grouped(core, mem, "ex", args["L2_ffn_gate_w"], args["L2_ffn_gate_b"], W)
        w12 = core.sb(mem, "ex_w12", [C, E * W])
        w3 = core.sb(mem, "ex_w3", [C, E * HID])
        by_w = w12[:, :].rearrange("c (e n h) -> c e n h", e=E, n=2)
        by_w3 = w3[:, :].rearrange("p (e k d) -> p e k d", e=E, k=K)
        silu = [core.sb(mem, f"ex_silu{k}", [C, HID]) for k in range(2)]
        hid = [core.sb(mem, f"ex_hidden{k}", [C, HID]) for k in range(2)]
        s_w = core.sem("ex_weights")
        pre, outs = core.bank[2:4], core.bank[4:6]
        core.start_counts()
        with nc.Block() as block:
            @block.sync
            def _(sp):
                ex.load(sp)
                for k in range(K):
                    sp.dma_start(by_w3[:, :, k], args["L2_ffn_w3"].rearrange("e (k p) d -> k p e d", p=C)[k]).then_inc(s_w, 16)
                for n, name in enumerate(("w1", "w2")):
                    sp.dma_start(by_w[:, :, n], args[f"L2_ffn_{name}"].rearrange("e c h -> c e h")).then_inc(s_w, 16)
                ex.blocks_sync(sp)

            @block.gpsimd
            def _(pool):
                ex.constants(pool)
                ex.scatter_gpsimd(pool)
                ex.combine_gpsimd(pool)

            @block.tensor
            def _(pe):
                pe.wait_ge(ex.s_par, START + 32)

                def route(b):
                    for h in range(2):
                        pe.wait_ge(norm.s_out, START + norm.ready(b, h))
                    ex.route_tensor(pe, b, ex.v)
                    ex.rows_tensor(pe, b, ex.v)

                ahead(pe, IMG, lambda b: None, lambda b: norm.tensor(pe, b, x_halves(core, b)), route)
                ex.choose_tensor(pe)
                pe.wait_ge(s_w, START + 16 * (K + 2))

                def first(r):
                    for c in range(2 * K):
                        mm = pe.matmul(pre[r][:, c * TILE:(c + 1) * TILE], ex.w1[r][:, c * C:(c + 1) * C], ex.xt[r][:, :], start=True, stop=True)
                    return mm

                def second(r, expert):
                    for c in range(K):
                        mm = pe.matmul(outs[r][:, 0:C], hid[r][:, c * TILE:(c + 1) * TILE], w3[:, bass.ds(expert * HID + c * C, C)],
                                       start=(c == 0), stop=(c == K - 1))
                    return mm

                ex.blocks_tensor(pe, first, second)
                ex.combine_tensor(pe)

            @block.scalar
            def _(act):
                act.preload_act_table_set(LOG_EXP)
                ahead(act, IMG, lambda b: None, lambda b: norm.scalar(act, b, 1e-5), lambda b: ex.rows_scalar(act, b))
                ex.choose_scalar(act)
                act.preload_act_table(ACT.Silu)
                ex.scatter_scalar(act)

                def turned(r, expert):
                    return act.activation(ex.xt[r][:, :], core.bank[r][:, 0:TILE], ACT.Copy)

                def activated(n, r, expert):
                    act.wait_ge(ex.s_hid, START + lag(n))
                    act.activation(silu[r][:, :], pre[r][:, 0:HID], ACT.Silu).then_inc(ex.s_act, 1)

                ex.blocks_scalar(act, turned, activated)

            @block.vector
            def _(dve):
                dve.wait_ge(ex.s_par, START + 32)

                def normalise(b):
                    dve.wait_ge(ex.s_turn, START + 2 * b)
                    norm.finish(dve, b, [image(ex.v[:, h * HALF:(h + 1) * HALF]) for h in range(2)])

                ahead(dve, IMG, normalise, lambda b: norm.centre(dve, b, x_halves(core, b)), lambda b: ex.route_vector(dve, b))
                ex.choose_vector(dve)
                dve.wait_ge(s_w, START + 16 * (K + 2))

                def copy_w1(r, expert):
                    return dve.tensor_copy(ex.w1[r][:, :], w12[:, bass.ds(expert * W, W)])

                def gated(n, r):
                    dve.wait_ge(ex.s_act, START + n + 1)
                    dve.wait_ge(ex.s_o, START + lag(n))
                    dve.tensor_tensor(hid[r][:, :], silu[r][:, :], pre[r][:, HID:W], ALU.mult).then_inc(ex.s_hid, 1)

                def out(r, to, expert):
                    return dve.tensor_copy(to, outs[r][:, 0:C])

                ex.blocks_vector(dve, copy_w1, gated, out)
                ex.combine_vector(dve)
        norm.done()


def sign_conv_mixer(core, args):
    nc, norm, X = core.nc, core.norm, core.x
    TAPS = 9
    with ExitStack() as mem:
        v = [core.sb(mem, f"sc_v{k}", [C, PAD, PAD]) for k in range(2)]
        w = core.sb(mem, "sc_w", [C, TAPS, C])
        pruning = core.sb(mem, "sc_pruning", [C, TAPS, C])
        signs = core.sb(mem, "sc_signs", [C, TAPS, C])
        size = core.sb(mem, "sc_size", [C, TAPS, C])
        clipped = core.sb(mem, "sc_clipped", [C, TAPS, C])
        total = core.sb(mem, "sc_total", [C, C])
        scale = core.sb(mem, "sc_scale", [C, C])
        (s_par, s_zero, s_act, s_w, s_tot, s_conv, s_end) = (
            core.sem(f"sc_{n}") for n in ("params", "zero", "signs", "weights", "scale", "convolved", "end"))
        core.start_counts()
        with nc.Block() as block:
            @block.sync
            def _(sp):
                sp.dma_start(w[:, :, :], args["L3_conv_w"].rearrange("a b i o -> i (a b) o")).then_inc(s_par, 16)
                sp.dma_start(pruning[:, :, :], args["L3_conv_pruning_mask"].rearrange("(t i) o -> i t o", i=C)).then_inc(s_par, 16)

            @block.gpsimd
            def _(pool):
                for k in range(2):
                    pool.memset(v[k][:, :, :], 0.0).then_inc(s_zero, 1)

            @block.tensor
            def _(pe):
                pe.wait_ge(s_w, START + 1)
                pe.matmul(core.bank[4][:, 0:C], core.mean_w[:, :], total[:, :], start=True, stop=True).then_inc(s_tot, 1)
                pe.wait_ge(s_w, START + 7)

                def convolve(p, k):
                    pe.wait_ge(norm.s_out, START + norm.ready(2 * p + k, 1))
                    pe.wait_ge(s_end, START + 4 * p)
                    for h in range(2):
                        bank = core.bank[4 + 2 * k + h]
                        for t in range(TAPS):
                            mm = pe.matmul(image(bank), w[:, t, :], window(v[k], h, t), start=(t == 0), stop=(t == TAPS - 1))
                        mm.then_inc(s_conv, 1)

                norm.tensor(pe, 0, x_halves(core, 0))
                with pe.Fori(0, IMG // 2 - 1) as p:
                    for k in range(2):
                        norm.tensor(pe, 2 * p + k + 1, x_halves(core, 2 * p + k + 1))
                        convolve(p, k)
                norm.tensor(pe, IMG - 1, x_halves(core, IMG - 1))
                for k in range(2):
                    convolve(IMG // 2 - 1, k)

            @block.scalar
            def _(act):
                act.wait_ge(s_par, START + 32)
                act.activation(size[:, :, :], w[:, :, :], ACT.Abs).then_inc(s_act, 1)
                act.activation(signs[:, :, :], w[:, :, :], ACT.Sign).then_inc(s_act, 1)
                act.wait_ge(s_zero, START + 2)
                act.preload_act_table_set(LOG_EXP)
                with act.Fori(0, IMG) as b:
                    norm.scalar(act, b, 1e-6)

            @block.vector
            def _(dve):
                dve.wait_ge(s_act, START + 2)
                dve.tensor_reduce(total[:, :], size[:, :, :].rearrange("i t o -> i o t"), AX.X, ALU.add).then_inc(s_w, 1)
                dve.wait_ge(s_tot, START + 1)
                dve.tensor_scalar(scale[:, :], core.bank[4][:, 0:C], 1.0 / TAPS, None, ALU.mult).then_inc(s_w, 1)
                dve.tensor_scalar(clipped[:, :, :], w[:, :, :], -1.0, 1.0, ALU.max, ALU.min).then_inc(s_w, 1)
                dve.wait_ge(s_w, START + 3)
                dve.tensor_tensor(w[:, :, :], signs[:, :, :], scale[:, :].rearrange("i (t o) -> i t o", t=1).broadcast_to([C, TAPS, C]), ALU.mult).then_inc(s_w, 1)
                dve.wait_ge(s_w, START + 4)
                dve.tensor_tensor(w[:, :, :], w[:, :, :], clipped[:, :, :], ALU.subtract).then_inc(s_w, 1)
                dve.wait_ge(s_w, START + 5)
                dve.tensor_tensor(w[:, :, :], w[:, :, :], clipped[:, :, :], ALU.add).then_inc(s_w, 1)
                dve.wait_ge(s_w, START + 6)
                dve.tensor_tensor(w[:, :, :], w[:, :, :], pruning[:, :, :], ALU.mult).then_inc(s_w, 1)
                dve.wait_ge(s_zero, START + 2)
                norm.vector(dve, 0, [X[:, 0:HALF], X[:, HALF:PIX]], [inner(v[0], 0), inner(v[0], 1)])

                def finish(p, k):
                    for h in range(2):
                        xs = X[:, bass.ds(p * (2 * PIX) + (k * PIX + h * HALF), HALF)]
                        dve.wait_ge(s_conv, START + 4 * p + 2 * k + h + 1)
                        dve.tensor_tensor(xs, xs, core.bank[4 + 2 * k + h][:, :], ALU.add).then_inc(s_end, 1)

                with dve.Fori(0, IMG // 2 - 1) as p:
                    for k in range(2):
                        dve.wait_ge(s_conv, START + 4 * p + 2 * k)
                        norm.vector(dve, 2 * p + k + 1, [X[:, bass.ds(p * (2 * PIX) + ((k + 1) * PIX + h * HALF), HALF)] for h in range(2)],
                                    [inner(v[1 - k], 0), inner(v[1 - k], 1)])
                        finish(p, k)
                p = IMG // 2 - 1
                dve.wait_ge(s_conv, START + 4 * p)
                norm.vector(dve, 2 * p + 1, [X[:, 2 * p * PIX + PIX + h * HALF:2 * p * PIX + PIX + (h + 1) * HALF] for h in range(2)],
                            [inner(v[1], 0), inner(v[1], 1)])
                finish(p, 0)
                finish(p, 1)
        norm.done()


def normed_experts_ffn(core, args):
    nc, norm, X = core.nc, core.norm, core.x
    E, _, HID = args["L3_ffn_W1"].shape
    K = HID // C
    with ExitStack() as mem:
        ex = Grouped(core, mem, "nx", args["L3_ffn_Wr"], args["L3_ffn_br"], HID, core.out)
        u = core.sb(mem, "nx_u", [C, PIX])
        w1 = core.sb(mem, "nx_w1", [C, E * HID])
        w2 = core.sb(mem, "nx_w2", [C, E * HID])
        by_w2 = w2[:, :].rearrange("p (e k d) -> p e k d", e=E, k=K)
        b1 = core.sb(mem, "nx_b1", [C, E * K])
        b2 = core.sb(mem, "nx_b2", [TILE, E * C])
        gain = core.sb(mem, "nx_gain", [C, 2, E])
        hid = [core.sb(mem, f"nx_hidden{k}", [C, HID]) for k in range(2)]
        s_w = core.sem("nx_weights")
        pre, outs = core.bank[2:4], core.bank[4:6]
        NPAR = K + 5
        core.start_counts()
        with nc.Block() as block:
            @block.sync
            def _(sp):
                ex.load(sp)
                for n, name in enumerate(("g", "b")):
                    sp.dma_start(gain[:, n, :], args[f"L3_ffn_ln_{name}"].rearrange("e c -> c e"), allow_slow_non_contiguous=True).then_inc(s_w, 16)
                sp.dma_start(b1[:, :], args["L3_ffn_b1"].rearrange("e (k p) -> p (e k)", p=C), allow_slow_non_contiguous=True).then_inc(s_w, 16)
                sp.dma_start(b2[:, :], args["L3_ffn_b2"].rearrange("(o e) c -> o (e c)", o=1).broadcast_to([TILE, E * C])).then_inc(s_w, 16)
                sp.dma_start(w1[:, :].rearrange("c (e h) -> c e h", e=E), args["L3_ffn_W1"].rearrange("e c h -> c e h")).then_inc(s_w, 16)
                for k in range(K):
                    sp.dma_start(by_w2[:, :, k], args["L3_ffn_W2"].rearrange("e (k p) d -> k p e d", p=C)[k]).then_inc(s_w, 16)
                ex.blocks_sync(sp)
                ex.out.sync(sp)

            @block.gpsimd
            def _(pool):
                ex.constants(pool)
                ex.scatter_gpsimd(pool)
                ex.combine_gpsimd(pool)

            @block.tensor
            def _(pe):
                pe.wait_ge(ex.s_par, START + 32)

                def route(b):
                    for h in range(2):
                        pe.wait_ge(norm.s_out, START + norm.ready(2 * b, h))
                    norm.tensor(pe, 2 * b + 1, [ex.v[:, h * HALF:(h + 1) * HALF] for h in range(2)])
                    ex.route_tensor(pe, b, ex.v)

                def rows(b):
                    for h in range(2):
                        pe.wait_ge(norm.s_out, START + norm.ready(2 * b + 1, h))
                    ex.rows_tensor(pe, b, u)

                ahead(pe, IMG, route, lambda b: norm.tensor(pe, 2 * b, x_halves(core, b)), rows)
                ex.choose_tensor(pe)
                pe.wait_ge(s_w, START + 16 * NPAR)

                def first(r):
                    for c in range(K):
                        mm = pe.matmul(pre[r][:, c * TILE:(c + 1) * TILE], ex.w1[r][:, c * C:(c + 1) * C], ex.xt[r][:, :], start=True, stop=True)
                    return mm

                def second(r, expert):
                    for c in range(K):
                        mm = pe.matmul(outs[r][:, 0:C], hid[r][:, c * TILE:(c + 1) * TILE], w2[:, bass.ds(expert * HID + c * C, C)],
                                       start=(c == 0), stop=(c == K - 1))
                    return mm

                ex.blocks_tensor(pe, first, second)
                ex.combine_tensor(pe)

            @block.scalar
            def _(act):
                act.preload_act_table_set(LOG_EXP)
                ahead(act, IMG, lambda b: norm.scalar(act, 2 * b + 1, 1e-5), lambda b: norm.scalar(act, 2 * b, 1e-5), lambda b: ex.rows_scalar(act, b))
                ex.choose_scalar(act)
                act.preload_act_table(ACT.Gelu)
                ex.scatter_scalar(act)
                act.wait_ge(s_w, START + 16 * NPAR)

                def turned(r, expert):
                    return act.activation(ex.xt[r][:, :], core.bank[r][:, 0:TILE], ACT.Identity, bias=gain[:, 1, bass.ds(expert, 1)], scale=gain[:, 0, bass.ds(expert, 1)])

                def activated(n, r, expert):
                    act.wait_ge(ex.s_o, START + lag(n))
                    for c in range(K):
                        ins = act.activation(hid[r][:, c * TILE:(c + 1) * TILE], pre[r][:, c * TILE:(c + 1) * TILE], ACT.Gelu, bias=b1[:, bass.ds(expert * K + c, 1)])
                    ins.then_inc(ex.s_hid, 1)

                ex.blocks_scalar(act, turned, activated, by_expert=True)
                ex.out.scalar(act)

            @block.vector
            def _(dve):
                dve.wait_ge(ex.s_par, START + 32)

                def normalise(b):
                    norm.finish(dve, 2 * b, [image(ex.v[:, h * HALF:(h + 1) * HALF]) for h in range(2)])
                    for h in range(2):
                        dve.wait_ge(norm.s_out, START + norm.ready(2 * b, h))
                    norm.centre(dve, 2 * b + 1, [ex.v[:, h * HALF:(h + 1) * HALF] for h in range(2)])
                    dve.wait_ge(ex.s_turn, START + 2 * b)
                    norm.finish(dve, 2 * b + 1, [image(u[:, h * HALF:(h + 1) * HALF]) for h in range(2)])

                ahead(dve, IMG, normalise, lambda b: norm.centre(dve, 2 * b, x_halves(core, b)), lambda b: ex.route_vector(dve, b))
                ex.choose_vector(dve)
                dve.wait_ge(s_w, START + 16 * NPAR)

                def copy_w1(r, expert):
                    return dve.tensor_copy(ex.w1[r][:, :], w1[:, bass.ds(expert * HID, HID)])

                def out(r, to, expert):
                    return dve.tensor_tensor(to, outs[r][:, 0:C], b2[:, bass.ds(expert * C, C)], ALU.add)

                ex.blocks_vector(dve, copy_w1, lambda n, r: None, out, by_expert=True)
                ex.combine_vector(dve)
        norm.done(2)


BRANCHES = [deformable_mixer_and_recurrence, divisive_mixer, routed_depth_ffn, scan_mixer, experts_ffn, sign_conv_mixer, normed_experts_ffn]


def program(nc, args, out, branches=BRANCHES):
    with ExitStack() as ctx:
        core = Core(nc, ctx, out)
        core.run(load_x, args["x"])
        for branch in branches:
            core.run(branch, args)


def kernel(**inputs):
    import numpy as np
    import concourse.bacc as bacc
    from concourse.bass_utils import run_bass_kernel_spmd

    nc = bacc.Bacc("TRN2", target_bir_lowering=False, num_devices=1)
    arrays, args = {}, {}
    for name, value in inputs.items():
        a = np.ascontiguousarray(value)
        arrays[f"in_{name}"] = a
        args[name] = nc.dram_tensor(f"in_{name}", a.shape, mybir.dt.from_np(a.dtype), kind="ExternalInput").ap()
    out = nc.dram_tensor("out_0_dram", (IMG, ROWS, COLS, C), F32, kind="ExternalOutput").ap()
    program(nc, args, out)
    r = run_bass_kernel_spmd(nc, [arrays], core_ids=[0])
    return r.results[0]["out_0_dram"]
```
